# Optimizing a Trainium2 kernel written in Bass

```python
import numpy as np
import jax
import jax.numpy as jnp

def _softmax(x, axis=-1):
    return jax.nn.softmax(x, axis=axis)

def _gelu(x):
    return jax.nn.gelu(x, approximate=True)

def _silu(x):
    return jax.nn.silu(x)

def _sigmoid(x):
    return jax.nn.sigmoid(x)

def _layernorm(x, axis=-1, eps=1e-05):
    m = jnp.mean(x, axis=axis, keepdims=True)
    v = jnp.var(x, axis=axis, keepdims=True)
    return (x - m) / jnp.sqrt(v + eps)

def _scatter_add(tgt, idx, src, axis=0):
    return tgt.at[idx].add(src)

def _segment_sum(src, seg, n):
    return jax.ops.segment_sum(src, seg, n)
kernel_name = 'mk_gnn_preln_d4_gnn_r16_abe3fc'

def setup_inputs(seed: int=0):
    np.random.seed(seed)
    _w = jnp.asarray

    def _rec_inputs():
        import jax
        import jax.numpy as jnp
        _gk = jax.random.key(seed)
        x = -0.000202 + 1 * jax.random.normal(jax.random.fold_in(_gk, 1), (6250, 64), jnp.float32)
        src = jax.random.randint(jax.random.fold_in(_gk, 2), (200000,), 0, 6250, jnp.int32)
        dst = jnp.minimum((6250 * jax.random.uniform(jax.random.fold_in(_gk, 3), (200000,)) ** 2.0).astype(jnp.int32), 99999)
        _o = jnp.argsort(dst, stable=True)
        src = src[_o]
        dst = dst[_o]
        edge_attr_32 = -9.77346e-05 + 0.999888 * jax.random.normal(jax.random.fold_in(_gk, 12), (200000, 32), jnp.float32)
        return (x, src, dst, edge_attr_32)
    x, src, dst, edge_attr_32 = _rec_inputs()

    def _L0_gnn_setup():
        import jax, jax.numpy as jnp
        import numpy as np
        EPS = 1e-05
        N_NODES = 6250
        N_EDGES = 100000
        F_NODE = 64
        F_EDGE = 32
        D_IN = 2 * F_NODE + F_EDGE

        def _bn(x, gamma, beta):
            mu = jnp.mean(x, axis=0)
            var = jnp.mean(jnp.square(x - mu), axis=0)
            return gamma * (x - mu) * jax.lax.rsqrt(var + EPS) + beta
        key = jax.random.key(seed)
        ks = jax.random.split(key, 8)
        s = 1.0 / np.sqrt(D_IN)
        return {'node_feats': jax.random.normal(ks[0], (N_NODES, F_NODE), jnp.float32), 'edge_feats': jax.random.normal(ks[1], (N_EDGES, F_EDGE), jnp.float32), 'src': jax.random.randint(ks[2], (N_EDGES,), 0, N_NODES, jnp.int32), 'dst': jax.random.randint(ks[3], (N_EDGES,), 0, N_NODES, jnp.int32), 'W_int': jax.random.normal(ks[4], (D_IN, F_NODE), jnp.float32) * s, 'b_int': jnp.zeros((F_NODE,), jnp.float32), 'g_int': jnp.ones((F_NODE,), jnp.float32), 'be_int': jnp.zeros((F_NODE,), jnp.float32), 'W_upd': jax.random.normal(ks[5], (D_IN, F_NODE), jnp.float32) * s, 'b_upd': jnp.zeros((F_NODE,), jnp.float32), 'g_upd': jnp.ones((F_NODE,), jnp.float32), 'be_upd': jnp.zeros((F_NODE,), jnp.float32), 'g_bn': jnp.ones((F_NODE,), jnp.float32), 'be_bn': jnp.zeros((F_NODE,), jnp.float32)}
    _L0_gnn_all = _L0_gnn_setup()
    _L0_gnn_in = {k: v for k, v in _L0_gnn_all.items() if k in ('W_int', 'b_int', 'g_int', 'be_int', 'W_upd', 'b_upd', 'g_upd', 'be_upd', 'g_bn', 'be_bn')}
    del _L0_gnn_all

    def _L1_gnn_setup():
        import jax, jax.numpy as jnp
        import numpy as np
        N_NODES = 6250
        N_EDGES = 75000
        DIM_IN = 64
        DIM_OUT = 64
        key = jax.random.key(seed)
        k_x, k_e, k_wl, k_wr = jax.random.split(key, 4)
        x = jax.random.normal(k_x, (N_NODES, DIM_IN), dtype=jnp.float32)
        edge_index = jax.random.randint(k_e, (2, N_EDGES), 0, N_NODES, dtype=jnp.int64)
        scale = 1.0 / np.sqrt(DIM_IN)
        w_l = jax.random.uniform(k_wl, (DIM_OUT, DIM_IN), dtype=jnp.float32, minval=-scale, maxval=scale)
        w_r = jax.random.uniform(k_wr, (DIM_OUT, DIM_IN), dtype=jnp.float32, minval=-scale, maxval=scale)
        b = jnp.zeros((DIM_OUT,), dtype=jnp.float32)
        return {'x': x, 'edge_index': edge_index, 'w_l': w_l, 'w_r': w_r, 'b': b}
    _L1_gnn_all = _L1_gnn_setup()
    _L1_gnn_in = {k: v for k, v in _L1_gnn_all.items() if k in ('w_l', 'w_r', 'b')}
    del _L1_gnn_all

    def _L2_gnn_setup():
        import jax, jax.numpy as jnp
        import numpy as np
        N_NODES = 6250
        N_EDGES = 75000
        HID = 64
        N_LAYERS = 3
        GAMMA = -0.45
        ZETA = 1.05
        key = jax.random.key(seed)
        ks = jax.random.split(key, 8)
        s = 0.05
        return {'features': jax.random.normal(ks[0], (N_NODES, HID), jnp.float32), 'nb_W': jax.random.normal(ks[1], (N_LAYERS, HID, HID), jnp.float32) * s, 'nb_b': jnp.zeros((N_LAYERS, HID), jnp.float32), 'self_W': jax.random.normal(ks[2], (N_LAYERS, HID, HID), jnp.float32) * s, 'self_b': jnp.zeros((N_LAYERS, HID), jnp.float32), 'att1_W': jax.random.normal(ks[3], (N_LAYERS, 2 * HID, HID), jnp.float32) * s, 'att1_b': jnp.zeros((N_LAYERS, HID), jnp.float32), 'att2_W': jax.random.normal(ks[4], (N_LAYERS, HID, 1), jnp.float32) * s, 'att2_b': jnp.zeros((N_LAYERS, 1), jnp.float32), 'row': jax.random.randint(ks[5], (N_EDGES,), 0, N_NODES, jnp.int32), 'col': jax.random.randint(ks[6], (N_EDGES,), 0, N_NODES, jnp.int32)}
    _L2_gnn_all = _L2_gnn_setup()
    _L2_gnn_in = {k: v for k, v in _L2_gnn_all.items() if k in ('nb_W', 'nb_b', 'self_W', 'self_b', 'att1_W', 'att1_b', 'att2_W', 'att2_b')}
    del _L2_gnn_all

    def _L3_gnn_setup():
        import jax, jax.numpy as jnp
        import numpy as np
        V = 6250
        E = 100000
        D = 64
        EF = 32
        EPS = 1e-05
        key = jax.random.key(seed)
        ks = jax.random.split(key, 10)
        h = jax.random.normal(ks[0], (V, D), dtype=jnp.float32)
        edge_index = jax.random.randint(ks[1], (2, E), 0, V, dtype=jnp.int64)
        edge_attr = jax.random.normal(ks[2], (E, EF), dtype=jnp.float32)
        lim1 = 1.0 / np.sqrt(D + EF)
        lim2 = 1.0 / np.sqrt(D)
        W1 = jax.random.uniform(ks[3], (D + EF, D), jnp.float32, -lim1, lim1)
        b1 = jax.random.uniform(ks[4], (D,), jnp.float32, -lim1, lim1)
        W2 = jax.random.uniform(ks[5], (D, D), jnp.float32, -lim2, lim2)
        b2 = jax.random.uniform(ks[6], (D,), jnp.float32, -lim2, lim2)
        gamma = jnp.ones((D,), jnp.float32)
        beta = jnp.zeros((D,), jnp.float32)
        return {'h': h, 'edge_index': edge_index, 'edge_attr': edge_attr, 'W1': W1, 'b1': b1, 'W2': W2, 'b2': b2, 'gamma': gamma, 'beta': beta}
    _L3_gnn_all = _L3_gnn_setup()
    _L3_gnn_in = {k: v for k, v in _L3_gnn_all.items() if k in ('W1', 'b1', 'W2', 'b2', 'gamma', 'beta')}
    del _L3_gnn_all
    return {'x': x, 'src': src, 'dst': dst, 'edge_attr_32': edge_attr_32, 'L0_gnn_W_int': _L0_gnn_in['W_int'], 'L0_gnn_b_int': _L0_gnn_in['b_int'], 'L0_gnn_g_int': _L0_gnn_in['g_int'], 'L0_gnn_be_int': _L0_gnn_in['be_int'], 'L0_gnn_W_upd': _L0_gnn_in['W_upd'], 'L0_gnn_b_upd': _L0_gnn_in['b_upd'], 'L0_gnn_g_upd': _L0_gnn_in['g_upd'], 'L0_gnn_be_upd': _L0_gnn_in['be_upd'], 'L0_gnn_g_bn': _L0_gnn_in['g_bn'], 'L0_gnn_be_bn': _L0_gnn_in['be_bn'], 'L1_gnn_w_l': _L1_gnn_in['w_l'], 'L1_gnn_w_r': _L1_gnn_in['w_r'], 'L1_gnn_b': _L1_gnn_in['b'], 'L2_gnn_nb_W': _L2_gnn_in['nb_W'], 'L2_gnn_nb_b': _L2_gnn_in['nb_b'], 'L2_gnn_self_W': _L2_gnn_in['self_W'], 'L2_gnn_self_b': _L2_gnn_in['self_b'], 'L2_gnn_att1_W': _L2_gnn_in['att1_W'], 'L2_gnn_att1_b': _L2_gnn_in['att1_b'], 'L2_gnn_att2_W': _L2_gnn_in['att2_W'], 'L2_gnn_att2_b': _L2_gnn_in['att2_b'], 'L3_gnn_W1': _L3_gnn_in['W1'], 'L3_gnn_b1': _L3_gnn_in['b1'], 'L3_gnn_W2': _L3_gnn_in['W2'], 'L3_gnn_b2': _L3_gnn_in['b2'], 'L3_gnn_gamma': _L3_gnn_in['gamma'], 'L3_gnn_beta': _L3_gnn_in['beta']}

def reference(x, src, dst, edge_attr_32, L0_gnn_W_int, L0_gnn_b_int, L0_gnn_g_int, L0_gnn_be_int, L0_gnn_W_upd, L0_gnn_b_upd, L0_gnn_g_upd, L0_gnn_be_upd, L0_gnn_g_bn, L0_gnn_be_bn, L1_gnn_w_l, L1_gnn_w_r, L1_gnn_b, L2_gnn_nb_W, L2_gnn_nb_b, L2_gnn_self_W, L2_gnn_self_b, L2_gnn_att1_W, L2_gnn_att1_b, L2_gnn_att2_W, L2_gnn_att2_b, L3_gnn_W1, L3_gnn_b1, L3_gnn_W2, L3_gnn_b2, L3_gnn_gamma, L3_gnn_beta):
    import jax
    import jax.numpy as jnp

    def _L0_gnn_ref(node_feats, edge_feats, src, dst, W_int, b_int, g_int, be_int, W_upd, b_upd, g_upd, be_upd, g_bn, be_bn):
        import jax, jax.numpy as jnp
        import numpy as np
        EPS = 1e-05
        N_NODES = 6250
        N_EDGES = 100000
        F_NODE = 64
        F_EDGE = 32
        D_IN = 2 * F_NODE + F_EDGE

        def _bn(x, gamma, beta):
            mu = jnp.mean(x, axis=0)
            var = jnp.mean(jnp.square(x - mu), axis=0)
            return gamma * (x - mu) * jax.lax.rsqrt(var + EPS) + beta
        z = jnp.concatenate([node_feats[src], node_feats[dst], edge_feats], axis=1)
        gate = jax.nn.sigmoid(_bn(z @ W_int + b_int, g_int, be_int))
        upd = jax.nn.softplus(_bn(z @ W_upd + b_upd, g_upd, be_upd))
        agg = jax.ops.segment_sum(gate * upd, dst, num_segments=N_NODES)
        return jax.nn.softplus(node_feats + _bn(agg, g_bn, be_bn))

    def _L1_gnn_ref(x, edge_index, w_l, w_r, b):
        import jax, jax.numpy as jnp
        import numpy as np
        N_NODES = 6250
        N_EDGES = 75000
        DIM_IN = 64
        DIM_OUT = 64
        src = edge_index[0]
        dst = edge_index[1]
        n = x.shape[0]
        msgs = x[src]
        summed = jax.ops.segment_sum(msgs, dst, num_segments=n)
        deg = jax.ops.segment_sum(jnp.ones((msgs.shape[0],), dtype=x.dtype), dst, num_segments=n)
        mean_aggr = summed / jnp.maximum(deg, 1.0)[:, None]
        out = mean_aggr @ w_l.T + x @ w_r.T + b
        return out

    def _L2_gnn_ref(features, nb_W, nb_b, self_W, self_b, att1_W, att1_b, att2_W, att2_b, row, col):
        import jax, jax.numpy as jnp
        import numpy as np
        N_NODES = 6250
        N_EDGES = 75000
        HID = 64
        N_LAYERS = 3
        GAMMA = -0.45
        ZETA = 1.05
        n = features.shape[0]
        x = features
        out = features
        for l in range(N_LAYERS):
            f1 = jax.nn.relu(x[row] @ nb_W[l] + nb_b[l])
            f2 = jax.nn.relu(x[col] @ self_W[l] + self_b[l])
            h = jax.nn.relu(jnp.concatenate([f1, f2], axis=1) @ att1_W[l] + att1_b[l])
            log_alpha = (h @ att2_W[l] + att2_b[l])[:, 0]
            mask = jnp.clip(jax.nn.sigmoid(log_alpha) * (ZETA - GAMMA) + GAMMA, 0.0, 1.0)
            rowsum = jax.ops.segment_sum(mask, row, num_segments=n) + 1e-06
            d_inv_sqrt = jnp.clip(rowsum ** (-0.5), 0.0, 10.0)
            vals = mask * d_inv_sqrt[row] * d_inv_sqrt[col]
            x = jax.ops.segment_sum(vals[:, None] * x[col], row, num_segments=n)
            out = out + x
        return out

    def _L3_gnn_ref(h, edge_index, edge_attr, W1, b1, W2, b2, gamma, beta):
        import jax, jax.numpy as jnp
        import numpy as np
        V = 6250
        E = 100000
        D = 64
        EF = 32
        EPS = 1e-05
        src, dst = (edge_index[0], edge_index[1])
        x = jnp.concatenate([h[src], edge_attr], axis=-1)
        msg = jnp.maximum(x @ W1 + b1, 0.0) @ W2 + b2
        n_nodes = h.shape[0]
        agg = jax.ops.segment_sum(msg, dst, num_segments=n_nodes)
        cnt = jax.ops.segment_sum(jnp.ones((dst.shape[0],), h.dtype), dst, num_segments=n_nodes)
        agg = agg / jnp.maximum(cnt, 1.0)[:, None]
        y = h + agg
        mu = jnp.mean(y, axis=-1, keepdims=True)
        var = jnp.mean(jnp.square(y - mu), axis=-1, keepdims=True)
        return (y - mu) * jax.lax.rsqrt(var + EPS) * gamma + beta
    edge_index = jnp.stack([src, dst])
    h = jnp.maximum(_layernorm(x, axis=-1), 0.0)
    x = x + _L0_gnn_ref(h, edge_attr_32, src, dst, L0_gnn_W_int, L0_gnn_b_int, L0_gnn_g_int, L0_gnn_be_int, L0_gnn_W_upd, L0_gnn_b_upd, L0_gnn_g_upd, L0_gnn_be_upd, L0_gnn_g_bn, L0_gnn_be_bn)
    h = jnp.maximum(_layernorm(x, axis=-1), 0.0)
    x = x + _L1_gnn_ref(h, edge_index, L1_gnn_w_l, L1_gnn_w_r, L1_gnn_b)
    h = jnp.maximum(_layernorm(x, axis=-1), 0.0)
    x = x + _L2_gnn_ref(h, L2_gnn_nb_W, L2_gnn_nb_b, L2_gnn_self_W, L2_gnn_self_b, L2_gnn_att1_W, L2_gnn_att1_b, L2_gnn_att2_W, L2_gnn_att2_b, src, dst)
    h = jnp.maximum(_layernorm(x, axis=-1), 0.0)
    x = x + _L3_gnn_ref(h, edge_index, edge_attr_32, L3_gnn_W1, L3_gnn_b1, L3_gnn_W2, L3_gnn_b2, L3_gnn_gamma, L3_gnn_beta)
    return x

_drawn_inputs = setup_inputs


def setup_inputs(seed=0):
    import zlib

    import numpy as np

    out = dict(_drawn_inputs(seed))
    spreads = {'L0_gnn_b_int': (0.0, 2.0),
     'L0_gnn_g_int': (1.0, 0.6),
     'L0_gnn_be_int': (0.0, 0.8),
     'L0_gnn_b_upd': (0.0, 2.0),
     'L0_gnn_g_upd': (1.0, 0.6),
     'L0_gnn_be_upd': (0.0, 0.8),
     'L0_gnn_g_bn': (1.0, 0.2),
     'L0_gnn_be_bn': (0.0, 0.1),
     'L1_gnn_b': (0.0, 0.1),
     'L2_gnn_nb_b': (0.0, 0.8),
     'L2_gnn_self_b': (0.0, 0.8),
     'L2_gnn_att1_b': (0.0, 0.8),
     'L2_gnn_att2_b': (0.0, 0.8),
     'L3_gnn_gamma': (1.0, 0.6),
     'L3_gnn_beta': (0.0, 2.0)}
    factors = {'L2_gnn_nb_W': 8.0,
     'L2_gnn_self_W': 8.0,
     'L2_gnn_att1_W': 8.0,
     'L2_gnn_att2_W': 8.0,
     'L3_gnn_b1': 64.0,
     'L3_gnn_W1': 8.0,
     'L3_gnn_W2': 8.0,
     'L3_gnn_b2': 8.0}
    for name, (base, spread) in spreads.items():
        noise = np.random.default_rng([zlib.crc32(name.encode()), seed]).standard_normal(out[name].shape)
        drawn = base * np.exp(spread * noise) if base else spread * noise
        out[name] = jnp.asarray(drawn.astype(out[name].dtype))
    for name, factor in factors.items():
        out[name] = (out[name] * factor).astype(out[name].dtype)
    return out
```

```python
import concourse.bass as bass
from concourse import mybir
from contextlib import ExitStack
import numpy as np

fp32 = mybir.dt.float32
i32 = mybir.dt.int32
ALU = mybir.AluOpType
ACT = mybir.ActivationFunctionType
AX = mybir.AxisListType

P = 128
N = 6250
F = 64
EF = 32
E = 200000
NB = -(-N // P)
NPAD = NB * P
EC = 1568
SENTINEL = NPAD
PAIR = 2 * P
BATCH = 8
PPB = BATCH // 2
PAIRS_MAX = (E + NB * (PAIR - 1)) // PAIR
ITERS = -(-PAIRS_MAX // (2 * PPB))
T = ITERS * 2 * BATCH
TP = T + 16
QR = 7
EPS = 1e-5
ROW = EF + 2
GROUP = 3
GROUPS = [range(g, min(g + GROUP, BATCH)) for g in range(0, BATCH, GROUP)]
GAMMA, ZETA = -0.45, 1.05
LAYERS = 3


class Order:

    def __init__(self, eng, sem, per_step=0, k=None, before=0):
        self.eng, self.sem, self.n = eng, sem, before
        self.base = 0 if k is None else k * per_step
        self.last = before + per_step

    def mark(self, ins):
        ins.then_inc(self.sem, 1)
        self.n += 1
        return self

    def wait(self):
        self.eng.wait_ge(self.sem, self.base + self.n)

    def then(self, ins):
        self.mark(ins).wait()


class Net:
    pass


def b3(ap, n):
    return ap.unsqueeze(2).to_broadcast([ap.shape[0], ap.shape[1], n])


def b2(ap, n):
    return ap.unsqueeze(1).to_broadcast([ap.shape[0], n, ap.shape[1]])


class Stage(ExitStack):

    def __init__(self, nc):
        super().__init__()
        self.nc, self.sems = nc, []
        self.callback(self.clear)

    def sem(self, name):
        self.sems.append(self.nc.alloc_semaphore(name=name))
        return self.sems[-1]

    def clear(self):
        if self.sems:
            self.nc.clear_and_free_semaphores(self.sems)
            self.nc.all_engine_barrier()


def stage(nc, names):
    ctx = Stage(nc)
    return ctx, [ctx.sem(n) for n in names]


def load_pair_blocks(nc, eng, m, k, j):
    _, values = nc.values_load_multi_w_load_instructions(
        m.table[0:1, bass.ds(k * 2 * PPB + j * PPB, PPB)], engines=[eng.engine], min_val=0, max_val=NB - 1)
    return values


def fetch_rows(nc, pool, index, index_now, rows, table, slot_free, copied, gate, arrived):
    for j in range(2):
        pool.sem_inc(slot_free[j], 1)
    with pool.Fori(0, ITERS) as k:
        for j in range(2):
            pool.wait_ge(slot_free[j], k + 1)
            pool.sem_inc(gate, 1)
            nc.gpsimd.tensor_copy(index_now[:, j, :], index[:, bass.ds(k * 2 * BATCH + j * BATCH, BATCH)]).then_inc(copied, 1)
            pool.wait_ge(copied, k * 2 + j + 1)
            pool.sem_inc(gate, 1)
            for t in range(BATCH):
                nc.gpsimd.indirect_dma_start(rows[:, j, t, :], None, table,
                                             bass.IndirectOffsetOnAxis(index_now[:, j, t:t + 1], 0)).then_inc(arrived[j], 16)


def one_hots(nc, m, onehot, keys, k, j, scale=None):
    for t in range(BATCH):
        at = bass.ds(k * 2 * BATCH + j * BATCH + t, 1)
        if scale is None:
            last = nc.vector.tensor_scalar(onehot[:, j, t, :], m.iota_p[:], keys[:, at], None, ALU.is_equal)
        else:
            last = nc.vector.tensor_scalar(onehot[:, j, t, :], m.iota_p[:], keys[:, at], scale[:, at],
                                           ALU.is_equal, ALU.mult)
    return last


def add_to_nodes(nc, dve, o, m, acc, sums, blocks):
    w = acc.shape[2]
    for q in range(PPB):
        o.wait()
        at = acc[:, bass.ds(blocks[q], 1), :].rearrange("p a f -> p (a f)")
        ins = nc.vector.tensor_tensor(at, at, sums[:, q, 0:w], ALU.add)
        if q < PPB - 1:
            o.mark(ins)
    return ins



def stage_constants(nc, m, a):
    ctx, (made, loaded, ordered) = stage(nc, ["const_made", "x_loaded", "const_order"])
    with ctx, nc.Block() as block:
        @block.sync
        def _(sp):
            sp.wait_ge(ordered, 1)
            full = NB - 1
            sp.dma_start(m.X[:, 0:full, :], a["x"][0:full * P, :].rearrange("(b p) f -> p b f", p=P)).then_inc(loaded, 16)
            sp.dma_start(m.X[0:N - full * P, full, :], a["x"][full * P:N, :]).then_inc(loaded, 16)
            sp.wait_ge(loaded, 32)

        @block.gpsimd
        def _(pool):
            nc.gpsimd.iota(m.iota_p[:], pattern=[[1, P]], base=0, channel_multiplier=0,
                           allow_small_or_imprecise_dtypes=True).then_inc(made, 1)
            nc.gpsimd.memset(m.ident[:], 0.0).then_inc(made, 1)
            nc.gpsimd.memset(m.ones[:], 1.0).then_inc(made, 1)
            nc.gpsimd.memset(m.before[:], 1.0).then_inc(made, 1)
            nc.gpsimd.memset(m.valid[:], 1.0).then_inc(made, 1)
            pool.wait_ge(made, 5)
            nc.gpsimd.affine_select(out=m.ident[:], in_=m.ident[:], compare_op=ALU.not_equal, fill=1.0, base=0,
                                    pattern=[[-1, P]], channel_multiplier=1).then_inc(made, 1)
            nc.gpsimd.affine_select(out=m.before[:], in_=m.before[:], compare_op=ALU.is_gt, fill=0.0, base=0,
                                    pattern=[[1, P]], channel_multiplier=-1).then_inc(made, 1)
            nc.gpsimd.affine_select(out=m.valid[:], in_=m.valid[:], compare_op=ALU.is_gt, fill=0.0,
                                    base=N - (NB - 1) * P, pattern=[[0, P]], channel_multiplier=-1).then_inc(made, 1)

        @block.vector
        def _(dve):
            nc.vector.memset(m.X[:], 0.0).then_inc(ordered, 1)


def stage_place(nc, m, name, key_dram, key_int, local, address, block_table):
    ctx, (loaded, numbered, order, counted, summed, tabled, flat, gate) = stage(nc, [f"{name}_{x}" for x in (
        "loaded", "numbered", "order", "counted", "summed", "tabled", "flat", "gate")])
    with ctx:
        def sb(n, s, d):
            return ctx.enter_context(nc.sbuf_tensor(f"{name}_{n}", s, d))
        blk = sb("blk", [P, EC], fp32)
        tmp = sb("tmp", [P, EC], i32)
        hit = sb("hit", [P, EC], fp32)
        rank = sb("rank", [P, EC], fp32)
        slot = sb("slot", [P, EC], fp32)
        numbers = sb("numbers", [P, NB + 1], fp32)
        cnt = sb("cnt", [P, NB], fp32)
        tot = sb("tot", [P, NB], fp32)
        pairs_i = sb("pairs_i", [P, NB], i32)
        pairs = sb("pairs", [P, NB], fp32)
        upto = sb("upto", [P, NB], fp32)
        off = sb("off", [P, NB], fp32)
        pair_no = sb("pair_no", [P, QR], fp32)
        past = sb("past", [P, QR, NB], fp32)
        pair_blk = sb("pair_blk", [P, QR], fp32)
        pair_blk_i = sb("pair_blk_i", [P, QR], i32)
        psum = ctx.enter_context(nc.psum_tensor(f"{name}_ps", [P, 2, NB], fp32))
        flat_dram = nc.dram_tensor(f"{name}_flat", [P * QR], i32).ap()
        with nc.Block() as block:
            @block.sync
            def _(sp):
                sp.dma_start(key_int[:], key_dram).then_inc(loaded, 16)
                sp.wait_ge(tabled, 1)
                sp.dma_start(flat_dram.rearrange("(p q) -> p q", q=QR), pair_blk_i[:]).then_inc(flat, 16)
                sp.wait_ge(flat, 16)
                sp.dma_start(block_table[:], flat_dram.rearrange("(a n) -> a n", a=1)).then_inc(flat, 16)
                sp.wait_ge(flat, 32)

            @block.gpsimd
            def _(pool):
                nc.gpsimd.iota(numbers[:], pattern=[[1, NB + 1]], base=0, channel_multiplier=0,
                               allow_small_or_imprecise_dtypes=True).then_inc(numbered, 1)
                nc.gpsimd.iota(pair_no[:], pattern=[[1, QR]], base=0, channel_multiplier=QR,
                               allow_small_or_imprecise_dtypes=True).then_inc(numbered, 1)
                nc.gpsimd.iota(slot[:], pattern=[[1, EC]], base=T * P + 1, channel_multiplier=0,
                               allow_small_or_imprecise_dtypes=True).then_inc(numbered, 1)

            @block.tensor
            def _(pe):
                pe.wait_ge(counted, 1)
                nc.tensor.matmul(psum[:, 0, :], m.before[:], cnt[:], start=True, stop=True)
                nc.tensor.matmul(psum[:, 1, :], m.ones[:], cnt[:], start=True, stop=True).then_inc(summed, 1)

            @block.vector
            def _(dve):
                o = Order(dve, order)
                dve.wait_ge(loaded, 16)
                dve.wait_ge(numbered, 3)
                o.then(nc.vector.tensor_single_scalar(tmp[:], key_int[:], 7, ALU.logical_shift_right))
                o.then(nc.vector.tensor_copy(blk[:], tmp[:]))
                o.then(nc.vector.tensor_single_scalar(tmp[:], key_int[:], P - 1, ALU.bitwise_and))
                o.then(nc.vector.tensor_copy(local[:], tmp[:]))
                start = o.n
                with dve.Fori(0, NB) as b:
                    s = Order(dve, order, 1, b, start)
                    s.then(nc.vector.tensor_scalar(hit[:], blk[:], numbers[:, bass.ds(b, 1)], 0.0, ALU.is_equal,
                                                   ALU.add, accum_out=cnt[:, bass.ds(b, 1)]))
                o.n = start + NB
                dve.wait_ge(order, o.n)
                dve.sem_inc(counted, 1)
                dve.wait_ge(summed, 1)
                o.then(nc.vector.tensor_scalar(tot[:], psum[:, 1, :], float(PAIR - 1), None, ALU.add))
                o.then(nc.vector.tensor_copy(pairs_i[:], tot[:]))
                o.then(nc.vector.tensor_single_scalar(pairs_i[:], pairs_i[:], 8, ALU.logical_shift_right))
                o.then(nc.vector.tensor_copy(pairs[:], pairs_i[:]))
                o.then(nc.vector.tensor_tensor_scan(upto[:], pairs[:], pairs[:], 0.0, ALU.add, ALU.bypass))
                o.then(nc.vector.tensor_tensor(off[:], upto[:], pairs[:], ALU.subtract))
                o.then(nc.vector.scalar_tensor_tensor(out=off[:], in0=off[:], scalar=float(PAIR), in1=psum[:, 0, :],
                                                      op0=ALU.mult, op1=ALU.add))
                o.then(nc.vector.tensor_tensor(past[:], b3(pair_no[:], NB), b2(upto[:], QR), ALU.is_ge))
                o.then(nc.vector.tensor_reduce(pair_blk[:], past[:], AX.X, ALU.add))
                o.then(nc.vector.tensor_scalar(pair_blk[:], pair_blk[:], float(NB - 1), None, ALU.min))
                nc.vector.tensor_copy(pair_blk_i[:], pair_blk[:]).then_inc(tabled, 1)
                start = o.n
                with dve.Fori(0, NB) as b:
                    s = Order(dve, order, 3, b, start)
                    s.then(nc.vector.tensor_scalar(hit[:], blk[:], numbers[:, bass.ds(b, 1)], None, ALU.is_equal))
                    s.then(nc.vector.tensor_tensor_scan(rank[:], hit[:], hit[:], off[:, bass.ds(b, 1)], ALU.add, ALU.bypass))
                    dve.sem_inc(gate, 1)
                    s.then(nc.vector.copy_predicated(slot[:], hit[:].bitcast(i32), rank[:]))
                o.n = start + 3 * NB
                o.wait()
                o.then(nc.vector.tensor_scalar(tmp[:], slot[:], -1.0, None, ALU.add))
                o.then(nc.vector.tensor_single_scalar(address[:], tmp[:], 7, ALU.logical_shift_right))
                o.then(nc.vector.tensor_copy(rank[:], address[:]))
                o.then(nc.vector.tensor_single_scalar(address[:], tmp[:], P - 1, ALU.bitwise_and))
                o.then(nc.vector.tensor_copy(hit[:], address[:]))
                o.then(nc.vector.scalar_tensor_tensor(out=address[:], in0=hit[:], scalar=float(TP), in1=rank[:],
                                                      op0=ALU.mult, op1=ALU.add))


def stage_reorder(nc, m, a):
    FILL = T // 16
    ctx = Stage(nc)
    with ctx:
        def sb(n, s, d):
            return ctx.enter_context(nc.sbuf_tensor(n, s, d))

        def sem(n):
            return ctx.sem(n)
        empty = sb("empty", [P, FILL, ROW], fp32)
        empty2 = sb("empty2", [P, T, 2], fp32)
        by_dst = sb("by_dst", [P, 2, BATCH, ROW], fp32)
        by_src = sb("by_src", [P, 2, BATCH, 2], fp32)
        to_dst = sb("to_dst", [P, 2, BATCH], i32)
        to_src = sb("to_src", [P, 2, BATCH], i32)
        emptied, cleared, order = sem("emptied"), sem("cleared"), sem("fill_order")
        features = [sem("features0"), sem("features1")]
        filled = [sem("filled0"), sem("filled1")]
        written = [sem("written0"), sem("written1")]
        gate = sem("reorder_gate")
        steps = EC // (2 * BATCH)
        e_view = a["e"].rearrange("(p c) f -> p c f", c=EC)
        with nc.Block() as block:
            @block.sync
            def _(sp):
                sp.wait_ge(emptied, 1)
                for c in range(T // FILL):
                    sp.dma_start(m.rows_dst[:, c * FILL:(c + 1) * FILL, :], empty[:]).then_inc(cleared, 16)
                sp.dma_start(m.rows_src[:, 0:T, :], empty2[:]).then_inc(cleared, 16)

                def load(j, k):
                    sp.dma_start(by_dst[:, j, :, 0:EF],
                                 e_view[:, bass.ds(k * 2 * BATCH + j * BATCH, BATCH), :]).then_inc(features[j], 16)
                for j in range(2):
                    load(j, 0)
                with sp.Fori(1, steps) as k:
                    for j in range(2):
                        sp.wait_ge(written[j], k * (32 * BATCH))
                        load(j, k)

            @block.gpsimd
            def _(pool):
                pool.wait_ge(cleared, 16 * (T // FILL) + 16)
                pool.sem_inc(gate, 1)
                with pool.Fori(0, steps) as k:
                    for j in range(2):
                        pool.wait_ge(filled[j], k + 1)
                        pool.wait_ge(features[j], k * 16 + 16)
                        pool.sem_inc(gate, 1)
                        for c in range(BATCH):
                            nc.gpsimd.indirect_dma_start(
                                m.rows_dst.rearrange("p t w -> (p t) w"), bass.IndirectOffsetOnAxis(to_dst[:, j, c:c + 1], 0),
                                by_dst[:, j, c, :], None).then_inc(written[j], 16)
                            nc.gpsimd.indirect_dma_start(
                                m.rows_src.rearrange("p t w -> (p t) w"), bass.IndirectOffsetOnAxis(to_src[:, j, c:c + 1], 0),
                                by_src[:, j, c, :], None).then_inc(written[j], 16)
                for j in range(2):
                    pool.wait_ge(written[j], steps * 32 * BATCH)

            @block.vector
            def _(dve):
                o = Order(dve, order)
                o.mark(nc.vector.memset(empty[:], 0.0))
                o.then(nc.vector.memset(empty2[:].bitcast(i32), 0))
                o.mark(nc.vector.memset(empty[:, :, EF:EF + 1].bitcast(i32), N))
                o.mark(nc.vector.memset(empty[:, :, EF + 1:ROW], -1.0))
                o.then(nc.vector.memset(empty2[:, :, 1:2], -1.0))
                dve.sem_inc(emptied, 1)

                def fill(j, k):
                    at = bass.ds(k * 2 * BATCH + j * BATCH, BATCH)
                    nc.vector.tensor_copy(by_dst[:, j, :, EF].bitcast(i32), m.src[:, at])
                    nc.vector.tensor_copy(by_dst[:, j, :, EF + 1], m.dst_local[:, at])
                    nc.vector.tensor_copy(by_src[:, j, :, 0].bitcast(i32), m.dst[:, at])
                    nc.vector.tensor_copy(by_src[:, j, :, 1], m.src_local[:, at])
                    nc.vector.tensor_copy(to_dst[:, j, :], m.addr_dst[:, at])
                    nc.vector.tensor_copy(to_src[:, j, :], m.addr_src[:, at]).then_inc(filled[j], 1)
                for j in range(2):
                    fill(j, 0)
                with dve.Fori(1, steps) as k:
                    for j in range(2):
                        dve.wait_ge(written[j], k * (32 * BATCH))
                        dve.sem_inc(gate, 1)
                        fill(j, k)


def stage_keys(nc, m):
    CH = T // 16
    ctx = Stage(nc)
    with ctx:
        chunk = ctx.enter_context(nc.sbuf_tensor("key_chunk", [P, 2, CH, ROW], fp32))
        pairs = ctx.enter_context(nc.sbuf_tensor("key_pairs", [P, T, 2], fp32))
        came = [ctx.sem(f"chunk_came{j}") for j in range(2)]
        taken, src_came = (ctx.sem(n) for n in ("chunk_taken", "src_came"))
        with nc.Block() as block:
            @block.sync
            def _(sp):
                sp.dma_start(pairs[:], m.rows_src[:, 0:T, :]).then_inc(src_came, 16)
                for c in range(T // CH):
                    if c >= 2:
                        sp.wait_ge(taken, 2 * (c - 1))
                    sp.dma_start(chunk[:, c % 2], m.rows_dst[:, c * CH:(c + 1) * CH, :]).then_inc(came[c % 2], 16)

            @block.vector
            def _(dve):
                for c in range(T // CH):
                    dve.wait_ge(came[c % 2], 16 * (c // 2 + 1))
                    nc.vector.tensor_copy(m.index_src[:, c * CH:(c + 1) * CH], chunk[:, c % 2, :, EF].bitcast(i32)).then_inc(taken, 1)
                    nc.vector.tensor_copy(m.key_dst[:, c * CH:(c + 1) * CH], chunk[:, c % 2, :, EF + 1]).then_inc(taken, 1)
                dve.wait_ge(src_came, 16)
                nc.vector.tensor_copy(m.index_dst[:], pairs[:, :, 0].bitcast(i32))
                nc.vector.tensor_copy(m.key_src[:], pairs[:, :, 1])



STEP = 7
assert NB % STEP == 0


def stage_weights(nc, m, a):
    ctx, (zeroed, loaded) = stage(nc, ["weights_zeroed", "weights_loaded"])
    with ctx, nc.Block() as block:
        loads = []
        for i, n in enumerate(("int", "upd")):
            W, cols = a[f"W_{n}"], slice(i * F, (i + 1) * F)
            loads.append((m.w_src[:, cols], W[0:F, :]))
            loads.append((m.w_dst[0:F, cols], W[F:2 * F, :]))
            loads.append((m.w_dst[F:F + 1, cols], a[f"b_{n}"].unsqueeze(0)))
            loads += [(m.w_edge[q * ROW:q * ROW + EF, q, cols], W[2 * F:, :]) for q in range(GROUP)]
            loads.append((m.gain[:, cols], a[f"g_{n}"].partition_broadcast(P)))
            loads.append((m.shift[:, cols], a[f"be_{n}"].partition_broadcast(P)))
        loads += [(m.w_edge3[q * ROW:q * ROW + EF, q, :], a["W1"][F:, :]) for q in range(GROUP)]
        for t, W, b in ((m.w_h3, a["W1"][0:F, :], a["b1"]), (m.w_out3, a["W2"], a["b2"])):
            loads += [(t[0:F, :], W), (t[F:F + 1, :], b.unsqueeze(0))]
        for l in range(LAYERS):
            for t, W, b in ((m.w_nb, a["nb_W"][l], a["nb_b"][l]), (m.w_self, a["self_W"][l], a["self_b"][l]),
                            (m.w_att_row, a["att1_W"][l, 0:F, :], a["att1_b"][l])):
                loads += [(t[0:F, l, :], W), (t[F:F + 1, l, :], b.unsqueeze(0))]
            loads.append((m.w_att_col[:, l, :], a["att1_W"][l, F:2 * F, :]))
            loads.append((m.att2[:, l, :], a["att2_W"][l, :, 0].partition_broadcast(P)))
            loads.append((m.att2_b[:, l:l + 1], a["att2_b"][l].partition_broadcast(P)))
        loads += [(t[:], a[n].partition_broadcast(P)) for t, n in
                  ((m.g_bn, "g_bn"), (m.be_bn, "be_bn"), (m.gamma3, "gamma"), (m.beta3, "beta"))]
        loads.append((m.w_r[F:F + 1, :], a["b_l1"].unsqueeze(0)))
        turned = [(m.w_l[:], a["w_l"].rearrange("o i -> i o")), (m.w_r[0:F, :], a["w_r"].rearrange("o i -> i o"))]

        @block.vector
        def _(dve):
            nc.vector.memset(m.w_edge[:], 0.0).then_inc(zeroed, 1)
            nc.vector.memset(m.w_edge3[:], 0.0).then_inc(zeroed, 1)

        @block.sync
        def _(sp):
            sp.wait_ge(zeroed, 2)
            for to, of in loads:
                sp.dma_start(to, of, allow_slow_non_contiguous=True).then_inc(loaded, 16)

        @block.scalar
        def _(act):
            for to, of in turned:
                act.dma_start(to, of, allow_slow_non_contiguous=True).then_inc(loaded, 16)
            act.wait_ge(loaded, 16 * (len(loads) + len(turned)))


def normalize(nc, dve, o, x, out, stat, std_sem, var_sem):
    mean, var = stat[:, 0, :], stat[:, 1, :]
    o.wait()
    o.then(nc.vector.tensor_reduce(mean, x, AX.X, ALU.add))
    o.then(nc.vector.tensor_scalar(mean, mean, 1.0 / F, None, ALU.mult))
    o.then(nc.vector.tensor_tensor(out[0], x, b3(mean, F), ALU.subtract))
    o.then(nc.vector.tensor_tensor(out[1], out[0], out[0], ALU.mult))
    o.then(nc.vector.tensor_reduce(var, out[1], AX.X, ALU.add))
    nc.vector.tensor_scalar(var, var, 1.0 / F, EPS, ALU.mult, ALU.add).then_inc(var_sem, 1)
    dve.wait_ge(std_sem, 1)
    o.then(nc.vector.reciprocal(mean, var))
    o.then(nc.vector.tensor_tensor(out[0], out[0], b3(mean, F), ALU.mult))


def root(nc, act, stat, var_sem, std_sem):
    act.wait_ge(var_sem, 1)
    nc.scalar.activation(stat[:, 1, :], stat[:, 1, :], ACT.Sqrt).then_inc(std_sem, 1)


def stage_norm(nc, m, name, x, h, table=None):
    ctx, (order, var_sem, std_sem, ready, stored) = stage(nc, [f"{name}_{s}" for s in (
        "order", "var", "std", "ready", "stored")])
    with ctx:
        stat = ctx.enter_context(nc.sbuf_tensor(f"{name}_stat", [P, 2, NB], fp32))
        square = ctx.enter_context(nc.sbuf_tensor(f"{name}_sq", [P, NB, F], fp32))
        with nc.Block() as block:
            @block.vector
            def _(dve):
                o = Order(dve, order)
                o.mark(nc.vector.memset(stat[:], 0.0))
                normalize(nc, dve, o, x, (h, square[:]), stat, std_sem, var_sem)
                nc.vector.tensor_scalar(h, h, 0.0, None, ALU.max).then_inc(ready, 1)

            @block.scalar
            def _(act):
                root(nc, act, stat, var_sem, std_sem)

            @block.sync
            def _(sp):
                if table is not None:
                    sp.wait_ge(ready, 1)
                    sp.dma_start(table.rearrange("(b p) f -> p b f", p=P), h).then_inc(stored, 16)
                    sp.wait_ge(stored, 16)


def stage_turn(nc, m, name, x, turned, w=F):
    ctx, (done, taken) = stage(nc, [f"{name}_{s}" for s in ("done", "taken")])
    with ctx:
        ps = ctx.enter_context(nc.psum_tensor(f"{name}_ps", [P, 8 * P], fp32))
        with nc.Block() as block:
            @block.tensor
            def _(pe):
                for k in range(NB // STEP):
                    pe.wait_ge(taken, k + 1)
                    for i in range(STEP):
                        src = x[:, k * STEP + i, :]
                        last = nc.tensor.transpose(ps[0:w, i * P:(i + 1) * P], src, m.ident[:])
                    last.then_inc(done, 1)

            @block.vector
            def _(dve):
                if w == F:
                    nc.vector.memset(turned[F:F + 1, :], 1.0).then_inc(taken, 1)
                else:
                    dve.sem_inc(taken, 1)
                for k in range(NB // STEP):
                    dve.wait_ge(done, k + 1)
                    nc.vector.tensor_copy(turned[0:w, bass.ds(k * STEP * P, STEP * P)],
                                          ps[0:w, 0:STEP * P]).then_inc(taken, 1)


def stage_product(nc, m, name, terms, out, width, plus=None, table=None):
    ctx, (done, taken, stored) = stage(nc, [f"{name}_{s}" for s in ("done", "taken", "stored")])
    with ctx:
        ps = ctx.enter_context(nc.psum_tensor(f"{name}_ps", [P, 8, P], fp32))
        with nc.Block() as block:
            @block.tensor
            def _(pe):
                pe.sem_inc(taken, 1)
                for k in range(NB // STEP):
                    pe.wait_ge(taken, k + 1)
                    for i in range(STEP):
                        for n, (turned, w) in enumerate(terms):
                            last = nc.tensor.matmul(ps[:, i, 0:width], turned[0:w.shape[0], bass.ds((k * STEP + i) * P, P)], w,
                                                    start=n == 0, stop=n == len(terms) - 1)
                    last.then_inc(done, 1)

            @block.vector
            def _(dve):
                for k in range(NB // STEP):
                    dve.wait_ge(done, k + 1)
                    at = bass.ds(k * STEP, STEP)
                    if plus is None:
                        nc.vector.tensor_copy(out[:, at, :], ps[:, 0:STEP, 0:width]).then_inc(taken, 1)
                    else:
                        nc.vector.tensor_tensor(out[:, at, :], ps[:, 0:STEP, 0:width], plus[:, at, :], ALU.add).then_inc(taken, 1)

            @block.sync
            def _(sp):
                if table is not None:
                    sp.wait_ge(taken, NB // STEP + 1)
                    sp.dma_start(table.rearrange("(b p) f -> p b f", p=P), out).then_inc(stored, 16)
                    sp.wait_ge(stored, 16)


def stage_attention(nc, m, l, turned, row_part, col_part, table):
    ctx, (inner, relued, outer, taken, stored) = stage(nc, [f"att{l}_{s}" for s in (
        "inner", "relued", "outer", "taken", "stored")])
    HALF = STEP * P // 2
    with ctx:
        hidden_ps = ctx.enter_context(nc.psum_tensor(f"att{l}_hid", [P, 4, 512], fp32))
        out_ps = ctx.enter_context(nc.psum_tensor(f"att{l}_out", [P, 2, 512], fp32))
        hidden = ctx.enter_context(nc.sbuf_tensor(f"att{l}_hidden", [F + 1, 2, STEP * P], fp32))
        with nc.Block() as block:
            @block.tensor
            def _(pe):
                for k in range(NB // STEP):
                    pe.wait_ge(taken, k + 1)
                    for s, w in enumerate((m.w_nb, m.w_self)):
                        for h in range(2):
                            last = nc.tensor.matmul(hidden_ps[0:F, 2 * s + h, 0:HALF], w[:, l, :],
                                                    turned[:, bass.ds(k * STEP * P + h * HALF, HALF)], start=True, stop=True)
                    last.then_inc(inner, 1)
                    pe.wait_ge(relued, k + 1)
                    for s, (w, n) in enumerate(((m.w_att_row, F + 1), (m.w_att_col, F))):
                        for i in range(STEP):
                            last = nc.tensor.matmul(out_ps[:, s, i * F:(i + 1) * F], hidden[0:n, s, i * P:(i + 1) * P],
                                                    w[:, l, :], start=True, stop=True)
                    last.then_inc(outer, 1)

            @block.vector
            def _(dve):
                nc.vector.memset(hidden[F:F + 1, :, :], 1.0).then_inc(taken, 1)
                for k in range(NB // STEP):
                    dve.wait_ge(inner, k + 1)
                    for s in range(2):
                        last = nc.vector.tensor_scalar(hidden[0:F, s, :].rearrange("p (h c) -> p h c", h=2),
                                                       hidden_ps[0:F, 2 * s:2 * s + 2, 0:HALF], 0.0, None, ALU.max)
                    last.then_inc(relued, 1)
                    dve.wait_ge(outer, k + 1)
                    for s, part in enumerate((row_part, col_part)):
                        last = nc.vector.tensor_copy(part[:, bass.ds(k * STEP, STEP), :],
                                                     out_ps[:, s, 0:STEP * F].rearrange("p (b f) -> p b f", f=F))
                    last.then_inc(taken, 1)

            @block.sync
            def _(sp):
                sp.wait_ge(taken, NB // STEP + 1)
                sp.dma_start(table.rearrange("(b p) f -> p b f", p=P), col_part[:]).then_inc(stored, 16)
                sp.wait_ge(stored, 16)


def stage_gate_norm(nc, m, sum_acc, square_acc, scale, shift):
    ctx, (order, summed, var_sem, std_sem) = stage(nc, ["gn_order", "gn_summed", "gn_var", "gn_std"])
    with ctx:
        ps = ctx.enter_context(nc.psum_tensor("gn_ps", [P, 2, 512], fp32))
        mu = ctx.enter_context(nc.sbuf_tensor("gn_mu", [P, 2 * F], fp32))
        var = ctx.enter_context(nc.sbuf_tensor("gn_var", [P, 2 * F], fp32))
        with nc.Block() as block:
            @block.tensor
            def _(pe):
                for i, acc in enumerate((sum_acc, square_acc)):
                    for c in range(BATCH):
                        last = nc.tensor.matmul(ps[:, i, 0:2 * F], m.ones[:], acc[:, c, :], start=c == 0, stop=c == BATCH - 1)
                last.then_inc(summed, 1)

            @block.vector
            def _(dve):
                o = Order(dve, order)
                dve.wait_ge(summed, 1)
                o.then(nc.vector.tensor_scalar(mu[:], ps[:, 0, 0:2 * F], 1.0 / E, None, ALU.mult))
                o.then(nc.vector.tensor_tensor(shift[:], mu[:], mu[:], ALU.mult))
                o.then(nc.vector.scalar_tensor_tensor(out=var[:], in0=ps[:, 1, 0:2 * F], scalar=1.0 / E, in1=shift[:],
                                                      op0=ALU.mult, op1=ALU.subtract))
                nc.vector.tensor_scalar(var[:], var[:], 0.0, EPS, ALU.max, ALU.add).then_inc(var_sem, 1)
                dve.wait_ge(std_sem, 1)
                o.then(nc.vector.reciprocal(scale[:], var[:]))
                o.then(nc.vector.tensor_tensor(scale[:], scale[:], m.gain[:], ALU.mult))
                o.then(nc.vector.tensor_tensor(mu[:], mu[:], scale[:], ALU.mult))
                o.then(nc.vector.tensor_tensor(shift[:], m.shift[:], mu[:], ALU.subtract))

            @block.scalar
            def _(act):
                act.wait_ge(var_sem, 1)
                nc.scalar.activation(var[:], var[:], ACT.Sqrt).then_inc(std_sem, 1)


def softplus_tail(nc, act, t, ready, done, n):
    act.wait_ge(ready, n)
    nc.scalar.activation(t, t, ACT.Exp).then_inc(done, 1)


def stage_conv_out(nc, m):
    ctx, (order, d_sem, mean_sem, var_sem, std_sem, neg_sem, log_sem, a_order) = stage(nc, ["co_" + s for s in (
        "order", "diff", "mean", "var", "std", "neg", "log", "act_order")])
    with ctx:
        ps = ctx.enter_context(nc.psum_tensor("co_ps", [P, 2, 512], fp32))
        d = ctx.enter_context(nc.sbuf_tensor("co_d", [P, NB, F], fp32))
        q = ctx.enter_context(nc.sbuf_tensor("co_q", [P, NB, F], fp32))
        mu = ctx.enter_context(nc.sbuf_tensor("co_mu", [P, F], fp32))
        std = ctx.enter_context(nc.sbuf_tensor("co_std", [P, F], fp32))
        with nc.Block() as block:
            @block.tensor
            def _(pe):
                for b in range(NB):
                    last = nc.tensor.matmul(ps[:, 0, 0:F], m.ones[:], m.acc[:, b, 0:F], start=b == 0, stop=b == NB - 1)
                last.then_inc(mean_sem, 1)
                pe.wait_ge(d_sem, 1)
                for b in range(NB):
                    last = nc.tensor.matmul(ps[:, 1, 0:F], (m.valid if b == NB - 1 else m.ones)[:], q[:, b, :],
                                            start=b == 0, stop=b == NB - 1)
                last.then_inc(var_sem, 1)

            @block.vector
            def _(dve):
                o = Order(dve, order)
                dve.wait_ge(mean_sem, 1)
                o.then(nc.vector.tensor_scalar(mu[:], ps[:, 0, 0:F], 1.0 / N, None, ALU.mult))
                o.then(nc.vector.tensor_tensor(d[:], m.acc[:, :, 0:F], b2(mu[:], NB), ALU.subtract))
                nc.vector.tensor_tensor(q[:], d[:], d[:], ALU.mult).then_inc(d_sem, 1)
                dve.wait_ge(var_sem, 1)
                nc.vector.tensor_scalar(std[:], ps[:, 1, 0:F], 1.0 / N, EPS, ALU.mult, ALU.add).then_inc(d_sem, 1)
                dve.wait_ge(std_sem, 1)
                o.then(nc.vector.reciprocal(mu[:], std[:]))
                o.then(nc.vector.tensor_tensor(mu[:], mu[:], m.g_bn[:], ALU.mult))
                o.then(nc.vector.tensor_tensor(d[:], d[:], b2(mu[:], NB), ALU.mult))
                o.then(nc.vector.tensor_tensor(d[:], d[:], b2(m.be_bn[:], NB), ALU.add))
                o.then(nc.vector.tensor_tensor(d[:], d[:], m.H[:], ALU.add))
                o.then(nc.vector.tensor_scalar(q[:], d[:], -1.0, None, ALU.mult))
                nc.vector.tensor_tensor(q[:], q[:], d[:], ALU.min).then_inc(neg_sem, 1)
                o.then(nc.vector.scalar_tensor_tensor(out=m.X[:], in0=d[:], scalar=0.0, in1=m.X[:], op0=ALU.max, op1=ALU.add))
                dve.wait_ge(log_sem, 1)
                o.then(nc.vector.tensor_tensor(m.X[:], m.X[:], q[:], ALU.add))

            @block.scalar
            def _(act):
                act.wait_ge(d_sem, 2)
                nc.scalar.activation(std[:], std[:], ACT.Sqrt).then_inc(std_sem, 1)
                act.wait_ge(neg_sem, 1)
                nc.scalar.activation(q[:], q[:], ACT.Exp).then_inc(a_order, 1)
                act.wait_ge(a_order, 1)
                nc.scalar.activation(q[:], q[:], ACT.Ln, bias=1.0).then_inc(log_sem, 1)


def stage_vector(nc, name, steps):
    ctx, (order,) = stage(nc, [f"{name}_order"])
    with ctx, nc.Block() as block:
        @block.vector
        def _(dve):
            steps(Order(dve, order))



def stage_conv_sums(nc, m, part_dst, table, kept, sum_acc, square_acc):
    W = 2 * F
    ctx = Stage(nc)
    with ctx:
        def sb(n, s, d=fp32):
            return ctx.enter_context(nc.sbuf_tensor(f"cs_{n}", s, d))

        def sem(n):
            return ctx.sem(f"cs_{n}")

        def sem2(n):
            return [sem(f"{n}{j}") for j in range(2)]
        e = sb("e", [P, 2, BATCH, ROW])
        rows = sb("rows", [P, 2, BATCH, W])
        index_now = sb("index", [P, 2, BATCH], i32)
        onehot = sb("onehot", [P, 2, BATCH, P])
        turned = sb("turned", [P, 2, BATCH, P])
        e_turned = sb("e_turned", [GROUP * ROW, 2, len(GROUPS), P])
        v = sb("v", [P, 2, BATCH, W])
        square = sb("square", [P, BATCH, W])
        turn_ps = ctx.enter_context(nc.psum_tensor("cs_turn_ps", [P, BATCH, P], fp32))
        e_ps = ctx.enter_context(nc.psum_tensor("cs_e_ps", [P, 4, P], fp32))
        v_ps = [ctx.enter_context(nc.psum_tensor(f"cs_v_ps{j}", [P, BATCH, W], fp32)) for j in range(2)]
        slot_free, arrived = sem2("free"), sem2("arrived")
        copied, gate, order = sem("copied"), sem("gate"), sem("order")
        e_came, e_turned_s, hot, turned_ps_s, turned_s, v_done, v_ready, squared, stored = (
            sem2(n) for n in ("e_came", "e_turned", "hot", "turn", "turned", "v", "ready", "squared", "stored"))
        steps = ITERS

        with nc.Block() as block:
            @block.gpsimd
            def _(pool):
                fetch_rows(nc, pool, m.index_src, index_now, rows, table, slot_free, copied, gate, arrived)

            @block.sync
            def _(sp):
                def load(j, col):
                    sp.dma_start(e[:, j, :, :], m.rows_dst[:, bass.ds(col, BATCH), :]).then_inc(e_came[j], 16)

                def store(j, col):
                    sp.dma_start(kept[:, bass.ds(col, BATCH), :], v[:, j, :, :]).then_inc(stored[j], 16)
                for j in range(2):
                    load(j, j * BATCH)
                with sp.Fori(0, steps - 1) as k:
                    for j in range(2):
                        sp.wait_ge(turned_ps_s[j], k + 1)
                        load(j, (k + 1) * 2 * BATCH + j * BATCH)
                    for j in range(2):
                        sp.wait_ge(v_ready[j], k + 1)
                        store(j, k * 2 * BATCH + j * BATCH)
                for j in range(2):
                    sp.wait_ge(v_ready[j], steps)
                    store(j, (steps - 1) * 2 * BATCH + j * BATCH)
                for j in range(2):
                    sp.wait_ge(stored[j], 16 * steps)

            @block.tensor
            def _(pe):
                with pe.Fori(0, steps) as k:
                    for j in range(2):
                        blocks = load_pair_blocks(nc, pe, m, k, j)
                        pe.wait_ge(hot[j], k + 1)
                        pe.wait_ge(e_came[j], k * 16 + 16)
                        if j == 0:
                            pe.wait_ge(turned_s[1], k + 1)
                        else:
                            pe.wait_ge(turned_s[0], k + 2)
                        pe.sem_inc(gate, 1)
                        for t in range(BATCH):
                            nc.tensor.transpose(turn_ps[:, t, :], onehot[:, j, t, :], m.ident[:])
                        for g, tiles in enumerate(GROUPS):
                            last = nc.tensor.transpose(e_ps[0:len(tiles) * ROW, g, :],
                                                       e[:, j, tiles[0]:tiles[-1] + 1, :].rearrange("p t w -> p (t w)"), m.ident[:])
                        last.then_inc(turned_ps_s[j], 1)
                        pe.wait_ge(turned_s[j], k + 2)
                        pe.sem_inc(gate, 1)
                        for t in range(BATCH):
                            at = part_dst[:, bass.ds(blocks[t // 2], 1), :].rearrange("p a f -> p (a f)")
                            nc.tensor.matmul(v_ps[j][:, t, :], turned[:, j, t, :], at, start=True, stop=False)
                            n = len(GROUPS[t // GROUP]) * ROW
                            last = nc.tensor.matmul(v_ps[j][:, t, :], e_turned[0:n, j, t // GROUP, :],
                                                    m.w_edge[0:n, t % GROUP, :], start=False, stop=True)
                        last.then_inc(v_done[j], 1)

            @block.scalar
            def _(act):
                for j in range(2):
                    act.sem_inc(turned_s[j], 1)
                with act.Fori(0, steps) as k:
                    for j in range(2):
                        act.wait_ge(turned_ps_s[j], k + 1)
                        act.sem_inc(gate, 1)
                        for h in range(2):
                            nc.scalar.copy(turned[:, j, 4 * h:4 * h + 4, :], turn_ps[:, 4 * h:4 * h + 4, :])
                        whole, rest = len(GROUPS) - 1, len(GROUPS[-1]) * ROW
                        nc.scalar.copy(e_turned[:, j, 0:whole, :], e_ps[0:GROUP * ROW, 0:whole, :])
                        nc.scalar.copy(e_turned[0:rest, j, whole, :], e_ps[0:rest, whole, :]).then_inc(turned_s[j], 1)
                        act.wait_ge(v_ready[j], k + 1)
                        act.wait_ge(order, k * 2 + j + 1)
                        act.sem_inc(gate, 1)
                        nc.scalar.square(square[:], v[:, j, :, :]).then_inc(squared[j], 1)

            @block.vector
            def _(dve):
                nc.vector.memset(sum_acc[:], 0.0)
                nc.vector.memset(square_acc[:], 0.0).then_inc(order, 1)
                dve.wait_ge(order, 1)

                def step(k, first):
                    for j in range(2):
                        one_hots(nc, m, onehot, m.key_dst, k, j).then_inc(hot[j], 1)
                        dve.wait_ge(v_done[j], k + 1)
                        dve.wait_ge(arrived[j], k * (16 * BATCH) + 16 * BATCH)
                        if not first:
                            dve.wait_ge(stored[j], k * 16)
                        dve.sem_inc(gate, 1)
                        nc.vector.tensor_tensor(v[:, j, :, :], v_ps[j][:], rows[:, j, :, :], ALU.add).then_inc(v_ready[j], 1)
                        dve.wait_ge(v_ready[j], k + 1)
                        dve.sem_inc(slot_free[j], 1)
                        nc.vector.tensor_tensor(sum_acc[:], sum_acc[:], v[:, j, :, :], ALU.add)
                        dve.wait_ge(squared[j], k + 1)
                        dve.sem_inc(gate, 1)
                        nc.vector.tensor_tensor(square_acc[:], square_acc[:], square[:], ALU.add).then_inc(order, 1)
                        dve.wait_ge(order, k * 2 + j + 2)
                step(0, True)
                with dve.Fori(1, steps) as k:
                    step(k, False)


def stage_conv_messages(nc, m, kept, scale, shift):
    W = 2 * F
    ctx = Stage(nc)
    with ctx:
        def sb(n, s, d=fp32):
            return ctx.enter_context(nc.sbuf_tensor(f"cm_{n}", s, d))

        def sem(n):
            return ctx.sem(f"cm_{n}")

        def sem2(n):
            return [sem(f"{n}{j}") for j in range(2)]
        v = sb("v", [P, 2, BATCH, W])
        log = sb("log", [P, 2, BATCH, W])
        gate_v = sb("gate", [P, 2, BATCH, F])
        message = sb("message", [P, 2, BATCH, F + 1])
        onehot = sb("onehot", [P, 2, BATCH, P])
        sums = [ctx.enter_context(nc.psum_tensor(f"cm_sums_ps{j}", [P, PPB, P], fp32)) for j in range(2)]
        came, normed, softened, gated, opened, ready, summed = (
            sem2(n) for n in ("came", "normed", "softened", "gated", "opened", "ready", "summed"))
        gate, order, cleared, act_order, normal = sem("gate_s"), sem("order"), sem("cleared"), sem("act_order"), sem("pool_order")
        with nc.Block() as block:
            @block.sync
            def _(sp):
                for j in range(2):
                    sp.sem_inc(ready[j], 1)
                with sp.Fori(0, ITERS) as k:
                    for j in range(2):
                        sp.wait_ge(ready[j], k + 1)
                        sp.dma_start(v[:, j, :, :], kept[:, bass.ds(k * 2 * BATCH + j * BATCH, BATCH), :]).then_inc(came[j], 16)

            @block.gpsimd
            def _(pool):
                with pool.Fori(0, ITERS) as k:
                    for j in range(2):
                        pool.wait_ge(came[j], k * 16 + 16)
                        pool.sem_inc(gate, 1)
                        nc.gpsimd.tensor_tensor(v[:, j, :, :], v[:, j, :, :], b2(scale[:], BATCH), ALU.mult).then_inc(normed[j], 1)

            @block.vector
            def _(dve):
                o = Order(dve, order)
                o.mark(nc.vector.memset(m.acc[:], 0.0))
                o.then(nc.vector.memset(message[:, :, :, F:F + 1], 1.0))
                with dve.Fori(0, ITERS) as k:
                    s = Order(dve, order, 2 + 2 * (2 + PPB), k, o.n)
                    for j in range(2):
                        dve.wait_ge(normed[j], k + 1)
                        s.wait()
                        s.then(nc.vector.tensor_tensor(v[:, j, :, :], v[:, j, :, :], b2(shift[:], BATCH), ALU.add))
                        nc.vector.scalar_tensor_tensor(out=log[:, j, :, :], in0=v[:, j, :, :], scalar=-1.0, in1=v[:, j, :, :],
                                                       op0=ALU.mult, op1=ALU.min).then_inc(softened[j], 1)
                    for j in range(2):
                        one_hots(nc, m, onehot, m.key_dst, k, j)
                        dve.wait_ge(gated[j], k * 2 + 1)
                        s.wait()
                        nc.vector.scalar_tensor_tensor(out=gate_v[:, j, :, :], in0=v[:, j, :, 0:F], scalar=0.0,
                                                       in1=log[:, j, :, 0:F], op0=ALU.min, op1=ALU.subtract).then_inc(opened[j], 1)
                        s.then(nc.vector.scalar_tensor_tensor(out=log[:, j, :, F:W], in0=v[:, j, :, F:W], scalar=0.0,
                                                              in1=log[:, j, :, F:W], op0=ALU.max, op1=ALU.add))
                        dve.wait_ge(gated[j], k * 2 + 2)
                        dve.sem_inc(gate, 1)
                        nc.vector.tensor_tensor(message[:, j, :, 0:F], gate_v[:, j, :, :], log[:, j, :, F:W],
                                                ALU.mult).then_inc(ready[j], 1)
                    for j in range(2):
                        blocks = load_pair_blocks(nc, dve, m, k, j)
                        dve.wait_ge(summed[j], k + 1)
                        s.mark(add_to_nodes(nc, dve, s, m, m.acc[:], sums[j], blocks))
                        s.mark(nc.vector.memset(gate_v[:, j, 0, 0:1], 0.0))
                    assert s.n == s.last, (s.n, s.last)

            @block.scalar
            def _(act):
                with act.Fori(0, ITERS) as k:
                    for j in range(2):
                        act.wait_ge(softened[j], k + 1)
                        act.sem_inc(gate, 1)
                        nc.scalar.activation(log[:, j, :, :], log[:, j, :, :], ACT.Exp).then_inc(act_order, 1)
                        act.wait_ge(act_order, k * 2 + j + 1)
                        nc.scalar.activation(log[:, j, :, :], log[:, j, :, :], ACT.Ln, bias=1.0).then_inc(gated[j], 1)
                    for j in range(2):
                        act.wait_ge(opened[j], k + 1)
                        act.sem_inc(gate, 1)
                        nc.scalar.activation(gate_v[:, j, :, :], gate_v[:, j, :, :], ACT.Exp).then_inc(gated[j], 1)

            @block.tensor
            def _(pe):
                with pe.Fori(0, ITERS) as k:
                    for j in range(2):
                        pe.wait_ge(ready[j], k + 2)
                        pe.sem_inc(gate, 1)
                        for t in range(BATCH):
                            last = nc.tensor.matmul(sums[j][:, t // 2, 0:F + 1], onehot[:, j, t, :], message[:, j, t, :],
                                                    start=t % 2 == 0, stop=t % 2 == 1)
                        last.then_inc(summed[j], 1)


def stage_gather_sum(nc, m, name, index, keys, table, acc, weight=None):
    ctx = Stage(nc)
    with ctx:
        def sem(n):
            return ctx.sem(f"{name}_{n}")

        def sem2(n):
            return [sem(f"{n}{j}") for j in range(2)]
        rows = ctx.enter_context(nc.sbuf_tensor(f"{name}_rows", [P, 2, BATCH, F], fp32))
        index_now = ctx.enter_context(nc.sbuf_tensor(f"{name}_index", [P, 2, BATCH], i32))
        onehot = ctx.enter_context(nc.sbuf_tensor(f"{name}_onehot", [P, 2, BATCH, P], fp32))
        sums = [ctx.enter_context(nc.psum_tensor(f"{name}_sums_ps{j}", [P, PPB, P], fp32)) for j in range(2)]
        slot_free, arrived, hot, summed = sem2("free"), sem2("arrived"), sem2("hot"), sem2("summed")
        copied, gate, order = sem("copied"), sem("gate"), sem("order")
        with nc.Block() as block:
            @block.gpsimd
            def _(pool):
                fetch_rows(nc, pool, index, index_now, rows, table, slot_free, copied, gate, arrived)

            @block.vector
            def _(dve):
                o = Order(dve, order)
                o.then(nc.vector.memset(acc, 0.0))
                with dve.Fori(0, ITERS) as k:
                    s = Order(dve, order, 2 * PPB, k, o.n)
                    for j in range(2):
                        one_hots(nc, m, onehot, keys, k, j, weight).then_inc(hot[j], 1)
                        blocks = load_pair_blocks(nc, dve, m, k, j)
                        dve.wait_ge(summed[j], k + 1)
                        dve.sem_inc(slot_free[j], 1)
                        s.mark(add_to_nodes(nc, dve, s, m, acc, sums[j], blocks))
                    assert s.n == s.last

            @block.tensor
            def _(pe):
                with pe.Fori(0, ITERS) as k:
                    for j in range(2):
                        pe.wait_ge(order, k * (2 * PPB) + j * PPB + 1)
                        pe.wait_ge(hot[j], k + 1)
                        pe.wait_ge(arrived[j], k * (16 * BATCH) + 16 * BATCH)
                        pe.sem_inc(gate, 1)
                        for t in range(BATCH):
                            last = nc.tensor.matmul(sums[j][:, t // 2, 0:F], onehot[:, j, t, :], rows[:, j, t, :],
                                                    start=t % 2 == 0, stop=t % 2 == 1)
                        last.then_inc(summed[j], 1)


def stage_masks(nc, m, l, row_part, table, mask, rowsum):
    name = f"mask{l}"
    ctx = Stage(nc)
    with ctx:
        def sb(n, s, d=fp32):
            return ctx.enter_context(nc.sbuf_tensor(f"{name}_{n}", s, d))

        def sem(n):
            return ctx.sem(f"{name}_{n}")

        def sem2(n):
            return [sem(f"{n}{j}") for j in range(2)]
        rows = sb("rows", [P, 2, BATCH, F])
        index_now = sb("index", [P, 2, BATCH], i32)
        onehot = sb("onehot", [P, 2, BATCH, P])
        turned = sb("turned", [P, 2, BATCH, P])
        hidden = sb("hidden", [P, 2, BATCH, F])
        logit = sb("logit", [P, 2, BATCH])
        mask_now = sb("mask", [P, 2, BATCH])
        turn_ps = ctx.enter_context(nc.psum_tensor(f"{name}_turn_ps", [P, BATCH, P], fp32))
        part_ps = [ctx.enter_context(nc.psum_tensor(f"{name}_part_ps{j}", [P, BATCH, F], fp32)) for j in range(2)]
        sums = [ctx.enter_context(nc.psum_tensor(f"{name}_sums_ps{j}", [P, PPB, P], fp32)) for j in range(2)]
        slot_free, arrived, hot, turn, turned_s, part, logits, opened, masked, summed = (
            sem2(n) for n in ("free", "arrived", "hot", "turn", "turned", "part", "logits", "opened", "masked", "summed"))
        copied, gate, order = sem("copied"), sem("gate"), sem("order")
        L = 2 * (3 + PPB)
        with nc.Block() as block:
            @block.gpsimd
            def _(pool):
                fetch_rows(nc, pool, m.index_dst, index_now, rows, table, slot_free, copied, gate, arrived)

            @block.vector
            def _(dve):
                o = Order(dve, order)
                o.then(nc.vector.memset(rowsum, 0.0))
                with dve.Fori(0, ITERS) as k:
                    s = Order(dve, order, L, k, o.n)
                    for j in range(2):
                        one_hots(nc, m, onehot, m.key_src, k, j).then_inc(hot[j], 1)
                        dve.wait_ge(part[j], k + 1)
                        dve.wait_ge(arrived[j], k * (16 * BATCH) + 16 * BATCH)
                        dve.sem_inc(gate, 1)
                        s.then(nc.vector.tensor_tensor(hidden[:, j, :, :], part_ps[j][:], rows[:, j, :, :], ALU.add))
                        dve.sem_inc(slot_free[j], 1)
                        s.then(nc.vector.scalar_tensor_tensor(out=hidden[:, j, :, :], in0=hidden[:, j, :, :], scalar=0.0,
                                                              in1=b2(m.att2[:, l, :], BATCH), op0=ALU.max, op1=ALU.mult))
                        nc.vector.tensor_reduce(logit[:, j, :], hidden[:, j, :, :], AX.X, ALU.add).then_inc(logits[j], 1)
                        dve.wait_ge(opened[j], k + 1)
                        s.wait()
                        s.then(nc.vector.tensor_scalar(mask_now[:, j, :], logit[:, j, :], ZETA - GAMMA, GAMMA, ALU.mult, ALU.add))
                        nc.vector.tensor_scalar(mask_now[:, j, :], mask_now[:, j, :], 0.0, 1.0, ALU.max, ALU.min).then_inc(masked[j], 1)
                        blocks = load_pair_blocks(nc, dve, m, k, j)
                        dve.wait_ge(masked[j], k + 1)
                        dve.sem_inc(gate, 1)
                        nc.vector.tensor_copy(mask[:, bass.ds(k * 2 * BATCH + j * BATCH, BATCH)], mask_now[:, j, :])
                        dve.wait_ge(summed[j], k + 1)
                        s.mark(add_to_nodes(nc, dve, s, m, rowsum, sums[j], blocks))
                    assert s.n == s.last

            @block.scalar
            def _(act):
                for j in range(2):
                    act.sem_inc(turned_s[j], 1)
                with act.Fori(0, ITERS) as k:
                    for j in range(2):
                        act.wait_ge(turn[j], k + 1)
                        act.sem_inc(gate, 1)
                        nc.scalar.copy(turned[:, j, 0:4, :], turn_ps[:, 0:4, :])
                        nc.scalar.copy(turned[:, j, 4:8, :], turn_ps[:, 4:8, :]).then_inc(turned_s[j], 1)
                        act.wait_ge(logits[j], k + 1)
                        act.sem_inc(gate, 1)
                        nc.scalar.activation(logit[:, j, :], logit[:, j, :], ACT.Sigmoid, bias=m.att2_b[:, l:l + 1]).then_inc(opened[j], 1)

            @block.tensor
            def _(pe):
                with pe.Fori(0, ITERS) as k:
                    for j in range(2):
                        blocks = load_pair_blocks(nc, pe, m, k, j)
                        pe.wait_ge(hot[j], k + 1)
                        pe.wait_ge(turned_s[1 - j], k + 1 + j)
                        pe.sem_inc(gate, 1)
                        for t in range(BATCH):
                            last = nc.tensor.transpose(turn_ps[:, t, :], onehot[:, j, t, :], m.ident[:])
                        last.then_inc(turn[j], 1)
                        pe.wait_ge(turned_s[j], k + 2)
                        pe.sem_inc(gate, 1)
                        for t in range(BATCH):
                            at = row_part[:, bass.ds(blocks[t // 2], 1), :].rearrange("p a f -> p (a f)")
                            last = nc.tensor.matmul(part_ps[j][:, t, :], turned[:, j, t, :], at, start=True, stop=True)
                        last.then_inc(part[j], 1)
                        pe.wait_ge(masked[j], k + 1)
                        pe.sem_inc(gate, 1)
                        for t in range(BATCH):
                            last = nc.tensor.matmul(sums[j][:, t // 2, 0:1], onehot[:, j, t, :], mask_now[:, j, t:t + 1],
                                                    start=t % 2 == 0, stop=t % 2 == 1)
                        last.then_inc(summed[j], 1)


def stage_edge_mlp(nc, m, table, acc):
    ctx = Stage(nc)
    with ctx:
        def sb(n, s, d=fp32):
            return ctx.enter_context(nc.sbuf_tensor(f"mlp_{n}", s, d))

        def sem(n):
            return ctx.sem(f"mlp_{n}")

        def sem2(n):
            return [sem(f"{n}{j}") for j in range(2)]
        e = sb("e", [P, 2, BATCH, ROW])
        rows = sb("rows", [P, 2, BATCH, F])
        index_now = sb("index", [P, 2, BATCH], i32)
        onehot = sb("onehot", [P, 2, BATCH, P])
        e_turned = sb("e_turned", [GROUP * ROW, 2, len(GROUPS), P])
        hidden = sb("hidden", [P, 2, BATCH, F])
        e_ps = [ctx.enter_context(nc.psum_tensor(f"mlp_e_ps{j}", [P, 4, P], fp32)) for j in range(2)]
        part_ps = [ctx.enter_context(nc.psum_tensor(f"mlp_part_ps{j}", [P, BATCH, F], fp32)) for j in range(2)]
        sums = [ctx.enter_context(nc.psum_tensor(f"mlp_sums_ps{j}", [P, PPB, P], fp32)) for j in range(2)]
        slot_free, arrived, e_came, turn, turned_s, part, ready, summed = (
            sem2(n) for n in ("free", "arrived", "e_came", "turn", "turned", "part", "ready", "summed"))
        copied, gate, order = sem("copied"), sem("gate"), sem("order")
        with nc.Block() as block:
            @block.gpsimd
            def _(pool):
                fetch_rows(nc, pool, m.index_src, index_now, rows, table, slot_free, copied, gate, arrived)

            @block.sync
            def _(sp):
                for j in range(2):
                    sp.sem_inc(turn[j], 1)
                with sp.Fori(0, ITERS) as k:
                    for j in range(2):
                        sp.wait_ge(turn[j], k + 1)
                        sp.dma_start(e[:, j, :, :], m.rows_dst[:, bass.ds(k * 2 * BATCH + j * BATCH, BATCH), :]).then_inc(e_came[j], 16)

            @block.tensor
            def _(pe):
                with pe.Fori(0, ITERS) as k:
                    for j in range(2):
                        pe.wait_ge(e_came[j], k * 16 + 16)
                        pe.sem_inc(gate, 1)
                        for g, tiles in enumerate(GROUPS):
                            last = nc.tensor.transpose(e_ps[j][0:len(tiles) * ROW, g, :],
                                                       e[:, j, tiles[0]:tiles[-1] + 1, :].rearrange("p t w -> p (t w)"), m.ident[:])
                        last.then_inc(turn[j], 1)
                        pe.wait_ge(turned_s[j], k + 1)
                        pe.sem_inc(gate, 1)
                        for t in range(BATCH):
                            n = len(GROUPS[t // GROUP]) * ROW
                            last = nc.tensor.matmul(part_ps[j][:, t, :], e_turned[0:n, j, t // GROUP, :],
                                                    m.w_edge3[0:n, t % GROUP, :], start=True, stop=True)
                        last.then_inc(part[j], 1)
                        pe.wait_ge(ready[j], k + 1)
                        pe.sem_inc(gate, 1)
                        for t in range(BATCH):
                            last = nc.tensor.matmul(sums[j][:, t // 2, 0:F], onehot[:, j, t, :], hidden[:, j, t, :],
                                                    start=t % 2 == 0, stop=t % 2 == 1)
                        last.then_inc(summed[j], 1)

            @block.scalar
            def _(act):
                with act.Fori(0, ITERS) as k:
                    for j in range(2):
                        act.wait_ge(turn[j], k + 2)
                        act.sem_inc(gate, 1)
                        whole, rest = len(GROUPS) - 1, len(GROUPS[-1]) * ROW
                        nc.scalar.copy(e_turned[:, j, 0:whole, :], e_ps[j][0:GROUP * ROW, 0:whole, :])
                        nc.scalar.copy(e_turned[0:rest, j, whole, :], e_ps[j][0:rest, whole, :]).then_inc(turned_s[j], 1)

            @block.vector
            def _(dve):
                o = Order(dve, order)
                o.then(nc.vector.memset(acc, 0.0))
                with dve.Fori(0, ITERS) as k:
                    s = Order(dve, order, 2 * (1 + PPB), k, o.n)
                    for j in range(2):
                        one_hots(nc, m, onehot, m.key_dst, k, j)
                        dve.wait_ge(part[j], k + 1)
                        dve.wait_ge(arrived[j], k * (16 * BATCH) + 16 * BATCH)
                        dve.sem_inc(gate, 1)
                        s.then(nc.vector.tensor_tensor(hidden[:, j, :, :], part_ps[j][:], rows[:, j, :, :], ALU.add))
                        dve.sem_inc(slot_free[j], 1)
                        nc.vector.tensor_scalar(hidden[:, j, :, :], hidden[:, j, :, :], 0.0, None, ALU.max).then_inc(ready[j], 1)
                        blocks = load_pair_blocks(nc, dve, m, k, j)
                        dve.wait_ge(summed[j], k + 1)
                        s.mark(add_to_nodes(nc, dve, s, m, acc, sums[j], blocks))
                    assert s.n == s.last



def build(nc, a, out):
    m = Net()
    top = ExitStack()
    with top:
        def sb(n, s, d=fp32, ctx=top):
            return ctx.enter_context(nc.sbuf_tensor(n, s, d))

        def dram(n, s, d=fp32):
            return nc.dram_tensor(n, s, d).ap()
        m.X, m.H = sb("X", [P, NB, F]), sb("H", [P, NB, F])
        m.acc = sb("acc", [P, NB, F + 1])
        m.out = sb("out", [P, NB, F])
        m.iota_p, m.ident, m.ones = sb("iota_p", [P, P]), sb("ident", [P, P]), sb("ones", [P, P])
        m.before, m.valid = sb("before", [P, P]), sb("valid", [P, P])
        m.w_src, m.w_dst, m.w_edge = sb("w_src", [F, 2 * F]), sb("w_dst", [F + 1, 2 * F]), sb("w_edge", [P, GROUP, 2 * F])
        m.w_edge3, m.w_h3, m.w_out3 = sb("w_edge3", [P, GROUP, F]), sb("w_h3", [F + 1, F]), sb("w_out3", [F + 1, F])
        m.w_l, m.w_r = sb("w_l", [F, F]), sb("w_r", [F + 1, F])
        m.w_nb, m.w_self, m.w_att_row = (sb(n, [F + 1, LAYERS, F]) for n in ("w_nb", "w_self", "w_att_row"))
        m.w_att_col, m.att2, m.att2_b = sb("w_att_col", [F, LAYERS, F]), sb("att2", [P, LAYERS, F]), sb("att2_b", [P, LAYERS])
        m.gain, m.shift = sb("gain", [P, 2 * F]), sb("shift", [P, 2 * F])
        m.g_bn, m.be_bn, m.gamma3, m.beta3 = (sb(n, [P, F]) for n in ("g_bn", "be_bn", "gamma3", "beta3"))
        m.index_src, m.index_dst = sb("index_src", [P, T], i32), sb("index_dst", [P, T], i32)
        m.key_dst, m.key_src = sb("key_dst", [P, T]), sb("key_src", [P, T])
        m.table_dst, m.table_src = sb("table_dst", [1, P * QR], i32), sb("table_src", [1, P * QR], i32)
        m.rows_dst, m.rows_src = dram("rows_dst", [P, TP, ROW]), dram("rows_src", [P, TP, 2])
        kept = dram("kept", [P, T, 2 * F])
        fetched128 = dram("fetched128", [NPAD, 2 * F])

        stage_constants(nc, m, a)
        stage_weights(nc, m, a)

        with ExitStack() as sort:
            m.src, m.dst = sb("src", [P, EC], i32, sort), sb("dst", [P, EC], i32, sort)
            m.src_local, m.dst_local = sb("src_local", [P, EC], fp32, sort), sb("dst_local", [P, EC], fp32, sort)
            m.addr_src, m.addr_dst = sb("addr_src", [P, EC], i32, sort), sb("addr_dst", [P, EC], i32, sort)
            stage_place(nc, m, "dst", a["dst"], m.dst, m.dst_local, m.addr_dst, m.table_dst)
            stage_place(nc, m, "src", a["src"], m.src, m.src_local, m.addr_src, m.table_src)
            stage_reorder(nc, m, a)
        stage_keys(nc, m)

        m.table = m.table_dst
        stage_norm(nc, m, "n0", m.X[:], m.H[:])
        with ExitStack() as conv:
            part_dst = sb("part_dst", [P, NB, 2 * F], ctx=conv)
            with ExitStack() as pre:
                turned, part_src = sb("turned0", [F + 1, NPAD], ctx=pre), sb("part_src", [P, NB, 2 * F], ctx=pre)
                stage_turn(nc, m, "t0", m.H[:], turned)
                stage_product(nc, m, "p0", [(turned, m.w_dst[:])], part_dst[:], 2 * F)
                stage_product(nc, m, "p1", [(turned, m.w_src[:])], part_src[:], 2 * F, table=fetched128)
            sum_acc, square_acc = sb("sum_acc", [P, BATCH, 2 * F], ctx=conv), sb("square_acc", [P, BATCH, 2 * F], ctx=conv)
            scale, shift = sb("bn_scale", [P, 2 * F], ctx=conv), sb("bn_shift", [P, 2 * F], ctx=conv)
            stage_conv_sums(nc, m, part_dst, fetched128, kept, sum_acc, square_acc)
            stage_gate_norm(nc, m, sum_acc, square_acc, scale, shift)
            stage_conv_messages(nc, m, kept, scale, shift)
        stage_conv_out(nc, m)

        inverse = sb("inverse", [P, NB])
        count = sb("count", [P, NB])
        table1 = dram("table1", [NPAD, F])
        stage_norm(nc, m, "n1", m.X[:], m.H[:], table=table1)

        def counts(o):
            o.then(nc.vector.tensor_copy(count[:], m.acc[:, :, F]))
            o.then(nc.vector.tensor_scalar(inverse[:], count[:], 1.0, None, ALU.max))
            o.then(nc.vector.reciprocal(inverse[:], inverse[:]))
        stage_vector(nc, "counts", counts)
        stage_gather_sum(nc, m, "sage", m.index_src, m.key_dst, table1, m.out[:])

        def mean(o):
            o.then(nc.vector.tensor_tensor(m.out[:], m.out[:], b3(inverse[:], F), ALU.mult))
        stage_vector(nc, "mean", mean)
        with ExitStack() as sage:
            turned_h, turned_m = sb("turned_h", [F + 1, NPAD], ctx=sage), sb("turned_m", [F + 1, NPAD], ctx=sage)
            stage_turn(nc, m, "t1", m.H[:], turned_h)
            stage_turn(nc, m, "t2", m.out[:], turned_m)
            stage_product(nc, m, "p2", [(turned_m, m.w_l[:]), (turned_h, m.w_r[:])], m.X[:], F, plus=m.X[:])

        m.table = m.table_src
        stage_norm(nc, m, "n2", m.X[:], m.H[:])
        with ExitStack() as hops:
            mask, rowsum = sb("mask", [P, T], ctx=hops), sb("rowsum", [P, NB, 1], ctx=hops)
            inv_root = sb("inv_root", [P, NB], ctx=hops)
            row_part = sb("row_part", [P, NB, F], ctx=hops)

            def start(o):
                o.then(nc.vector.tensor_copy(m.out[:], m.H[:]))
            stage_vector(nc, "hops", start)
            for l in range(LAYERS):
                cols, feats = dram(f"cols{l}", [NPAD, F]), dram(f"feats{l}", [NPAD, F])
                with ExitStack() as pre:
                    turned, col_part = sb(f"turned_l{l}", [F + 1, NPAD], ctx=pre), sb(f"col_part{l}", [P, NB, F], ctx=pre)
                    stage_turn(nc, m, f"tl{l}", m.H[:], turned)
                    stage_attention(nc, m, l, turned, row_part, col_part, cols)
                stage_masks(nc, m, l, row_part, cols, mask, rowsum[:])
                stage_degree(nc, m, l, rowsum, inv_root, feats)
                stage_gather_sum(nc, m, f"hop{l}", m.index_dst, m.key_src, feats, m.H[:], weight=mask)

                def after(o):
                    o.then(nc.vector.tensor_tensor(m.H[:], m.H[:], b3(inv_root[:], F), ALU.mult))
                    o.then(nc.vector.tensor_tensor(m.out[:], m.out[:], m.H[:], ALU.add))
                stage_vector(nc, f"after{l}", after)

        def hops_out(o):
            o.then(nc.vector.tensor_tensor(m.X[:], m.X[:], m.out[:], ALU.add))
        stage_vector(nc, "hops_out", hops_out)

        m.table = m.table_dst
        stage_norm(nc, m, "n3", m.X[:], m.H[:])
        table3 = dram("table3", [NPAD, F])
        with ExitStack() as mlp:
            turned = sb("turned3", [F + 1, NPAD], ctx=mlp)
            stage_turn(nc, m, "t3", m.H[:], turned)
            stage_product(nc, m, "p3", [(turned, m.w_h3[:])], m.out[:], F, table=table3)
        stage_edge_mlp(nc, m, table3, m.acc[:, :, 0:F])

        with ExitStack() as mlp:
            turned = sb("turned4", [F + 1, NPAD], ctx=mlp)
            stage_turn(nc, m, "t4", m.acc[:], turned, F + 1)
            stage_product(nc, m, "p4", [(turned, m.w_out3[:])], m.out[:], F)
        stage_last_norm(nc, m, inverse, out)


def stage_degree(nc, m, l, rowsum, inv_root, table):
    ctx, (order, rooted, ready, stored) = stage(nc, [f"deg{l}_{s}" for s in ("order", "rooted", "ready", "stored")])
    with ctx:
        scaled = ctx.enter_context(nc.sbuf_tensor(f"deg{l}_scaled", [P, NB, F], fp32))
        flat = rowsum[:, :, 0]
        with nc.Block() as block:
            @block.vector
            def _(dve):
                o = Order(dve, order)
                nc.vector.tensor_scalar(inv_root[:], flat, 1e-6, None, ALU.add).then_inc(ready, 1)
                dve.wait_ge(rooted, 1)
                o.then(nc.vector.reciprocal(inv_root[:], inv_root[:]))
                o.then(nc.vector.tensor_scalar(inv_root[:], inv_root[:], 0.0, 10.0, ALU.max, ALU.min))
                nc.vector.tensor_tensor(scaled[:], m.H[:], b3(inv_root[:], F), ALU.mult).then_inc(ready, 1)

            @block.scalar
            def _(act):
                act.wait_ge(ready, 1)
                nc.scalar.activation(inv_root[:], inv_root[:], ACT.Sqrt).then_inc(rooted, 1)

            @block.sync
            def _(sp):
                sp.wait_ge(ready, 2)
                sp.dma_start(table.rearrange("(b p) f -> p b f", p=P), scaled[:]).then_inc(stored, 16)
                sp.wait_ge(stored, 16)


def stage_last_norm(nc, m, inverse, out):
    ctx, (order, var_sem, std_sem, ready, stored) = stage(nc, ["ln_" + s for s in ("order", "var", "std", "ready", "stored")])
    with ctx:
        stat = ctx.enter_context(nc.sbuf_tensor("ln_stat", [P, 2, NB], fp32))
        square = ctx.enter_context(nc.sbuf_tensor("ln_sq", [P, NB, F], fp32))
        with nc.Block() as block:
            @block.vector
            def _(dve):
                o = Order(dve, order)
                o.then(nc.vector.tensor_tensor(m.out[:], m.out[:], b3(inverse[:], F), ALU.mult))
                o.then(nc.vector.tensor_tensor(m.out[:], m.out[:], m.H[:], ALU.add))
                normalize(nc, dve, o, m.out[:], (m.H[:], square[:]), stat, std_sem, var_sem)
                o.then(nc.vector.tensor_tensor(m.H[:], m.H[:], b2(m.gamma3[:], NB), ALU.mult))
                o.then(nc.vector.tensor_tensor(m.H[:], m.H[:], b2(m.beta3[:], NB), ALU.add))
                nc.vector.tensor_tensor(m.H[:], m.H[:], m.X[:], ALU.add).then_inc(ready, 1)

            @block.scalar
            def _(act):
                root(nc, act, stat, var_sem, std_sem)

            @block.sync
            def _(sp):
                sp.wait_ge(ready, 1)
                full = NB - 1
                sp.dma_start(out[0:full * P, :].rearrange("(b p) f -> p b f", p=P), m.H[:, 0:full, :]).then_inc(stored, 16)
                sp.dma_start(out[full * P:N, :], m.H[0:N - full * P, full, :]).then_inc(stored, 16)
                sp.wait_ge(stored, 32)


NAMES = {"x": "x", "L0_gnn_W_int": "W_int", "L0_gnn_b_int": "b_int", "L0_gnn_g_int": "g_int", "L0_gnn_be_int": "be_int",
         "L0_gnn_W_upd": "W_upd", "L0_gnn_b_upd": "b_upd", "L0_gnn_g_upd": "g_upd", "L0_gnn_be_upd": "be_upd",
         "L0_gnn_g_bn": "g_bn", "L0_gnn_be_bn": "be_bn", "L1_gnn_w_l": "w_l", "L1_gnn_w_r": "w_r", "L1_gnn_b": "b_l1",
         "L2_gnn_nb_W": "nb_W", "L2_gnn_nb_b": "nb_b", "L2_gnn_self_W": "self_W", "L2_gnn_self_b": "self_b",
         "L2_gnn_att1_W": "att1_W", "L2_gnn_att1_b": "att1_b", "L2_gnn_att2_W": "att2_W", "L2_gnn_att2_b": "att2_b",
         "L3_gnn_W1": "W1", "L3_gnn_b1": "b1", "L3_gnn_W2": "W2", "L3_gnn_b2": "b2", "L3_gnn_gamma": "gamma",
         "L3_gnn_beta": "beta"}


def kernel(**inputs):
    from concourse import bacc
    from concourse.bass_utils import run_bass_kernel_spmd

    nc = bacc.Bacc("TRN2", target_bir_lowering=False, num_devices=1)
    arrays = {short: np.ascontiguousarray(inputs[name]) for name, short in NAMES.items()}
    for name in ("src", "dst"):
        arrays[name] = np.pad(np.asarray(inputs[name]), (0, P * EC - E), constant_values=SENTINEL).reshape(P, EC)
    arrays["e"] = np.pad(np.asarray(inputs["edge_attr_32"]), ((0, P * EC - E), (0, 0)))
    args = {n: nc.dram_tensor(f"in_{n}", v.shape, mybir.dt.from_np(v.dtype), kind="ExternalInput").ap()
            for n, v in arrays.items()}
    out = nc.dram_tensor("out_dram", [N, F], fp32, kind="ExternalOutput").ap()
    build(nc, args, out)
    r = run_bass_kernel_spmd(nc, [{f"in_{n}": v for n, v in arrays.items()}], core_ids=[0])
    return r.results[0]["out_dram"]
```

```python
import concourse.bass as bass
from concourse import mybir
from contextlib import ExitStack
import numpy as np

fp32 = mybir.dt.float32
i32 = mybir.dt.int32
bf16 = mybir.dt.bfloat16
ALU = mybir.AluOpType
ACT = mybir.ActivationFunctionType
AX = mybir.AxisListType

P = 128
N = 6250
F = 64
EF = 32
E = 200000
NB = -(-N // P)
NPAD = NB * P
EC = 1568
SENTINEL = NPAD
PAIR = 2 * P
BATCH = 8
PPB = BATCH // 2
PAIRS_MAX = (E + NB * (PAIR - 1)) // PAIR
ITERS = -(-PAIRS_MAX // (2 * PPB))
T = ITERS * 2 * BATCH
TP = T + 16
TK = T + BATCH
QR = 7
EPS = 1e-5
ROW = EF + 2
GROUP = 3
GROUPS = [range(g, min(g + GROUP, BATCH)) for g in range(0, BATCH, GROUP)]
GAMMA, ZETA = -0.45, 1.05
LAYERS = 3


class Order:

    def __init__(self, eng, sem, per_step=0, k=None, before=0):
        self.eng, self.sem, self.n = eng, sem, before
        self.base = 0 if k is None else k * per_step
        self.last = before + per_step

    def mark(self, ins):
        ins.then_inc(self.sem, 1)
        self.n += 1
        return self

    def wait(self):
        self.eng.wait_ge(self.sem, self.base + self.n)

    def then(self, ins):
        self.mark(ins).wait()


class Net:
    pass


def b3(ap, n):
    return ap.unsqueeze(2).to_broadcast([ap.shape[0], ap.shape[1], n])


def b2(ap, n):
    return ap.unsqueeze(1).to_broadcast([ap.shape[0], n, ap.shape[1]])


class Stage(ExitStack):

    def __init__(self, nc):
        super().__init__()
        self.nc, self.sems = nc, []
        self.callback(self.clear)

    def sem(self, name):
        self.sems.append(self.nc.alloc_semaphore(name=name))
        return self.sems[-1]

    def clear(self):
        if self.sems:
            self.nc.clear_and_free_semaphores(self.sems)
            self.nc.all_engine_barrier()


def stage(nc, names):
    ctx = Stage(nc)
    return ctx, [ctx.sem(n) for n in names]


def load_pair_blocks(nc, eng, m, b):
    _, values = nc.values_load_multi_w_load_instructions(
        m.table[0:1, bass.ds(b * PPB, PPB)], engines=[eng.engine], min_val=0, max_val=NB - 1)
    return values


def fetch_rows(nc, pool, index_now, rows, table, indexed, gate, arrived):
    with pool.Fori(0, ITERS) as k:
        for j in range(2):
            pool.wait_ge(indexed[j], k + 1)
            pool.sem_inc(gate, 1)
            for t in range(BATCH):
                nc.gpsimd.indirect_dma_start(rows[:, j, t, :], None, table,
                                             bass.IndirectOffsetOnAxis(index_now[:, j, t:t + 1], 0)).then_inc(arrived[j], 16)


class IndexStager:

    def __init__(self, nc, act, index, index_now, slot_free, indexed, gate):
        self.nc, self.act, self.index, self.index_now = nc, act, index, index_now
        self.slot_free, self.indexed, self.gate = slot_free, indexed, gate

    def first(self):
        for j in range(2):
            self.nc.scalar.copy(self.index_now[:, j, :], self.index[:, j * BATCH:(j + 1) * BATCH]).then_inc(self.indexed[j], 1)

    def after(self, k, j):
        self.act.wait_ge(self.slot_free[j], k + 1)
        self.act.sem_inc(self.gate, 1)
        self.nc.scalar.copy(self.index_now[:, j, :],
                            self.index[:, bass.ds((k + 1) * 2 * BATCH + j * BATCH, BATCH)]).then_inc(self.indexed[j], 1)


def one_hots(nc, m, onehot, keys, b, j, scale=None, iota=None):
    for t in range(BATCH):
        at = bass.ds(b * BATCH + t, 1)
        if scale is None:
            last = nc.vector.tensor_scalar(onehot[:, j, t, :], (iota or m.iota_p)[:], keys[:, at], None, ALU.is_equal)
        else:
            last = nc.vector.tensor_scalar(onehot[:, j, t, :], (iota or m.iota_p)[:], keys[:, at], scale[:, at],
                                           ALU.is_equal, ALU.mult)
    return last


def add_to_nodes(nc, dve, o, m, acc, sums, blocks):
    w = acc.shape[2]
    for q in range(PPB):
        o.wait()
        at = acc[:, bass.ds(blocks[q], 1), :].rearrange("p a f -> p (a f)")
        ins = nc.vector.tensor_tensor(at, at, sums[:, q, 0:w], ALU.add)
        if q < PPB - 1:
            o.mark(ins)
    return ins



def stage_constants(nc, m, a):
    ctx, (made, loaded, ordered) = stage(nc, ["const_made", "x_loaded", "const_order"])
    with ctx, nc.Block() as block:
        @block.sync
        def _(sp):
            sp.wait_ge(ordered, 1)
            full = NB - 1
            sp.dma_start(m.X[:, 0:full, :], a["x"][0:full * P, :].rearrange("(b p) f -> p b f", p=P)).then_inc(loaded, 16)
            sp.dma_start(m.X[0:N - full * P, full, :], a["x"][full * P:N, :]).then_inc(loaded, 16)
            sp.dma_start(m.src[:], a["src"]).then_inc(loaded, 16)
            sp.dma_start(m.dst[:], a["dst"]).then_inc(loaded, 16)
            sp.wait_ge(loaded, 64)

        @block.gpsimd
        def _(pool):
            nc.gpsimd.iota(m.iota_p[:], pattern=[[1, P]], base=0, channel_multiplier=0,
                           allow_small_or_imprecise_dtypes=True).then_inc(made, 1)
            nc.gpsimd.iota(m.iota_b[:], pattern=[[1, P]], base=0, channel_multiplier=0,
                           allow_small_or_imprecise_dtypes=True).then_inc(made, 1)
            nc.gpsimd.memset(m.ident[:], 0.0).then_inc(made, 1)
            nc.gpsimd.memset(m.ones[:], 1.0).then_inc(made, 1)
            nc.gpsimd.memset(m.before[:], 1.0).then_inc(made, 1)
            nc.gpsimd.memset(m.valid[:], 1.0).then_inc(made, 1)
            nc.gpsimd.iota(m.numbers[:], pattern=[[1, NB + 1]], base=0, channel_multiplier=0,
                           allow_small_or_imprecise_dtypes=True).then_inc(made, 1)
            nc.gpsimd.iota(m.pair_no[:], pattern=[[1, QR]], base=0, channel_multiplier=QR,
                           allow_small_or_imprecise_dtypes=True).then_inc(made, 1)
            nc.gpsimd.iota(m.sentinel_slot[:], pattern=[[1, EC]], base=T * P + 1, channel_multiplier=0,
                           allow_small_or_imprecise_dtypes=True).then_inc(made, 1)
            pool.wait_ge(made, 9)
            nc.gpsimd.affine_select(out=m.ident[:], in_=m.ident[:], compare_op=ALU.not_equal, fill=1.0, base=0,
                                    pattern=[[-1, P]], channel_multiplier=1).then_inc(made, 1)
            nc.gpsimd.affine_select(out=m.before[:], in_=m.before[:], compare_op=ALU.is_gt, fill=0.0, base=0,
                                    pattern=[[1, P]], channel_multiplier=-1).then_inc(made, 1)
            nc.gpsimd.affine_select(out=m.valid[:], in_=m.valid[:], compare_op=ALU.is_gt, fill=0.0,
                                    base=N - (NB - 1) * P, pattern=[[0, P]], channel_multiplier=-1).then_inc(made, 1)

        @block.vector
        def _(dve):
            nc.vector.memset(m.X[:], 0.0).then_inc(ordered, 1)
            dve.wait_ge(made, 12)
            nc.vector.tensor_copy(m.ident_b[:], m.ident[:])


def place(nc, m, ctx, block, name, key, other, packed, block_table):
    order, counted, summed, tabled, flat, gate = (ctx.sem(f"{name}_{x}") for x in (
        "order", "counted", "summed", "tabled", "flat", "gate"))

    def sb(n, s, d):
        return ctx.enter_context(nc.sbuf_tensor(f"{name}_{n}", s, d))
    blk = sb("blk", [P, EC], fp32)
    tmp = sb("tmp", [P, EC], i32)
    hit = sb("hit", [P, EC], fp32)
    rank = sb("rank", [P, EC], fp32)
    slot = sb("slot", [P, EC], fp32)
    cnt = sb("cnt", [P, NB], fp32)
    tot = sb("tot", [P, NB], fp32)
    pairs_i = sb("pairs_i", [P, NB], i32)
    pairs = sb("pairs", [P, NB], fp32)
    upto = sb("upto", [P, NB], fp32)
    off = sb("off", [P, NB], fp32)
    past = sb("past", [P, QR, NB], fp32)
    pair_blk = sb("pair_blk", [P, QR], fp32)
    pair_blk_i = sb("pair_blk_i", [P, QR], i32)
    psum = ctx.enter_context(nc.psum_tensor(f"{name}_ps", [P, 2, NB], fp32))
    flat_dram = nc.dram_tensor(f"{name}_flat", [P * QR], i32).ap()

    @block.scalar
    def _(act):
        act.wait_ge(tabled, 1)
        act.dma_start(flat_dram.rearrange("(p q) -> p q", q=QR), pair_blk_i[:]).then_inc(flat, 16)
        act.wait_ge(flat, 16)
        act.dma_start(block_table[:], flat_dram.rearrange("(a n) -> a n", a=1)).then_inc(flat, 16)
        act.wait_ge(flat, 32)

    @block.tensor
    def _(pe):
        pe.wait_ge(counted, 1)
        nc.tensor.matmul(psum[:, 0, :], m.before[:], cnt[:], start=True, stop=True)
        nc.tensor.matmul(psum[:, 1, :], m.ones[:], cnt[:], start=True, stop=True).then_inc(summed, 1)

    @block.vector
    def _(dve):
        o = Order(dve, order)
        o.mark(nc.vector.tensor_copy(slot[:], m.sentinel_slot[:]))
        o.mark(nc.vector.tensor_copy(packed[:, :, 0].bitcast(i32), other[:]))
        o.then(nc.vector.tensor_single_scalar(tmp[:], key[:], 7, ALU.logical_shift_right))
        o.then(nc.vector.tensor_copy(blk[:], tmp[:]))
        o.then(nc.vector.tensor_single_scalar(tmp[:], key[:], P - 1, ALU.bitwise_and))
        o.then(nc.vector.tensor_copy(packed[:, :, 1], tmp[:]))
        start = o.n
        with dve.Fori(0, NB) as b:
            s = Order(dve, order, 1, b, start)
            s.then(nc.vector.tensor_scalar(hit[:], blk[:], m.numbers[:, bass.ds(b, 1)], 0.0, ALU.is_equal,
                                           ALU.add, accum_out=cnt[:, bass.ds(b, 1)]))
        o.n = start + NB
        dve.wait_ge(order, o.n)
        dve.sem_inc(counted, 1)
        dve.wait_ge(summed, 1)
        o.then(nc.vector.tensor_scalar(tot[:], psum[:, 1, :], float(PAIR - 1), None, ALU.add))
        o.then(nc.vector.tensor_copy(pairs_i[:], tot[:]))
        o.then(nc.vector.tensor_single_scalar(pairs_i[:], pairs_i[:], 8, ALU.logical_shift_right))
        o.then(nc.vector.tensor_copy(pairs[:], pairs_i[:]))
        o.then(nc.vector.tensor_tensor_scan(upto[:], pairs[:], pairs[:], 0.0, ALU.add, ALU.bypass))
        o.then(nc.vector.tensor_tensor(off[:], upto[:], pairs[:], ALU.subtract))
        o.then(nc.vector.scalar_tensor_tensor(out=off[:], in0=off[:], scalar=float(PAIR), in1=psum[:, 0, :],
                                              op0=ALU.mult, op1=ALU.add))
        o.then(nc.vector.tensor_tensor(past[:], b3(m.pair_no[:], NB), b2(upto[:], QR), ALU.is_ge))
        o.then(nc.vector.tensor_reduce(pair_blk[:], past[:], AX.X, ALU.add))
        o.then(nc.vector.tensor_scalar(pair_blk[:], pair_blk[:], float(NB - 1), None, ALU.min))
        nc.vector.tensor_copy(pair_blk_i[:], pair_blk[:]).then_inc(tabled, 1)
        start = o.n
        with dve.Fori(0, NB) as b:
            s = Order(dve, order, 3, b, start)
            s.then(nc.vector.tensor_scalar(hit[:], blk[:], m.numbers[:, bass.ds(b, 1)], None, ALU.is_equal))
            s.then(nc.vector.tensor_tensor_scan(rank[:], hit[:], hit[:], off[:, bass.ds(b, 1)], ALU.add, ALU.bypass))
            dve.sem_inc(gate, 1)
            s.then(nc.vector.copy_predicated(slot[:], hit[:].bitcast(i32), rank[:]))
        o.n = start + 3 * NB
        o.wait()
        o.then(nc.vector.tensor_scalar(tmp[:], slot[:], -1.0, None, ALU.add))
        o.then(nc.vector.tensor_single_scalar(hit[:].bitcast(i32), tmp[:], 7, ALU.logical_shift_right))
        o.then(nc.vector.tensor_copy(rank[:], hit[:].bitcast(i32)))
        o.then(nc.vector.tensor_single_scalar(hit[:].bitcast(i32), tmp[:], P - 1, ALU.bitwise_and))
        o.then(nc.vector.tensor_copy(slot[:], hit[:].bitcast(i32)))
        o.then(nc.vector.scalar_tensor_tensor(out=packed[:, :, 2].bitcast(i32), in0=slot[:], scalar=float(TP), in1=rank[:],
                                              op0=ALU.mult, op1=ALU.add))


def reorder(nc, ctx, block, name, packed, rows, features=None):
    w = rows.shape[2]
    now = ctx.enter_context(nc.sbuf_tensor(f"{name}_now", [P, 2, BATCH, w + 1], fp32))
    filled = [ctx.sem(f"{name}_filled{j}") for j in range(2)]
    written = [ctx.sem(f"{name}_written{j}") for j in range(2)]
    gate = ctx.sem(f"{name}_gate")
    steps = EC // (2 * BATCH)
    parts = 1 if features is None else 2

    @block.sync
    def _(sp):
        def fill(j, k):
            at = bass.ds(k * 2 * BATCH + j * BATCH, BATCH)
            sp.dma_start(now[:, j, :, w - 2:w + 1], packed[:, at, :]).then_inc(filled[j], 16)
            if features is not None:
                sp.dma_start(now[:, j, :, 0:EF], features[:, at, :]).then_inc(filled[j], 16)
        for j in range(2):
            fill(j, 0)
        with sp.Fori(1, steps) as k:
            for j in range(2):
                sp.wait_ge(written[j], k * (16 * BATCH))
                fill(j, k)

    @block.gpsimd
    def _(pool):
        with pool.Fori(0, steps) as k:
            for j in range(2):
                pool.wait_ge(filled[j], k * (16 * parts) + 16 * parts)
                pool.sem_inc(gate, 1)
                for c in range(BATCH):
                    nc.gpsimd.indirect_dma_start(
                        rows.rearrange("p t w -> (p t) w"),
                        bass.IndirectOffsetOnAxis(now[:, j, c, w:w + 1].bitcast(i32), 0),
                        now[:, j, c, 0:w], None).then_inc(written[j], 16)
        for j in range(2):
            pool.wait_ge(written[j], steps * 16 * BATCH)


def stage_place(nc, m):
    with Stage(nc) as ctx, nc.Block() as block:
        place(nc, m, ctx, block, "dst", m.dst, m.src, m.packed_dst, m.table_dst)


def stage_empty(nc, m):
    FILL = TP // 16
    ctx, (emptied, cleared, order) = stage(nc, ["emptied", "cleared", "fill_order"])
    with ctx:
        empty = ctx.enter_context(nc.sbuf_tensor("empty", [P, FILL, ROW], fp32))
        empty2 = ctx.enter_context(nc.sbuf_tensor("empty2", [P, T, 2], fp32))
        with nc.Block() as block:
            @block.sync
            def _(sp):
                sp.wait_ge(emptied, 1)
                for c in range(TP // FILL):
                    sp.dma_start(m.rows_dst[:, c * FILL:(c + 1) * FILL, :], empty[:]).then_inc(cleared, 16)
                sp.dma_start(m.rows_src[:, 0:T, :], empty2[:]).then_inc(cleared, 16)
                sp.wait_ge(cleared, 16 * (TP // FILL) + 16)

            @block.vector
            def _(dve):
                o = Order(dve, order)
                o.mark(nc.vector.memset(empty[:], 0.0))
                o.then(nc.vector.memset(empty2[:].bitcast(i32), 0))
                o.mark(nc.vector.memset(empty[:, :, EF:EF + 1].bitcast(i32), N))
                o.mark(nc.vector.memset(empty[:, :, EF + 1:ROW], -1.0))
                o.then(nc.vector.memset(empty2[:, :, 1:2], -1.0))
                dve.sem_inc(emptied, 1)


def stage_reorder_dst(nc, m, a):
    with Stage(nc) as ctx, nc.Block() as block:
        reorder(nc, ctx, block, "to_dst", m.packed_dst, m.rows_dst, a["e"].rearrange("(p c) f -> p c f", c=EC))
        place(nc, m, ctx, block, "src", m.src, m.dst, m.packed_src, m.table_src)


def stage_keys_dst(nc, m):
    CH = T // 16
    ctx, (came0, came1, taken) = stage(nc, ["chunk_came0", "chunk_came1", "chunk_taken"])
    came = (came0, came1)
    with ctx:
        chunk = ctx.enter_context(nc.sbuf_tensor("key_chunk", [P, 2, CH, ROW], fp32))
        with nc.Block() as block:
            @block.sync
            def _(sp):
                for c in range(T // CH):
                    if c >= 2:
                        sp.wait_ge(taken, 2 * (c - 1))
                    sp.dma_start(chunk[:, c % 2], m.rows_dst[:, c * CH:(c + 1) * CH, :]).then_inc(came[c % 2], 16)

            @block.vector
            def _(dve):
                for c in range(T // CH):
                    dve.wait_ge(came[c % 2], 16 * (c // 2 + 1))
                    nc.vector.tensor_copy(m.index_src[:, c * CH:(c + 1) * CH], chunk[:, c % 2, :, EF].bitcast(i32)).then_inc(taken, 1)
                    nc.vector.tensor_copy(m.key_dst[:, c * CH:(c + 1) * CH], chunk[:, c % 2, :, EF + 1]).then_inc(taken, 1)
                nc.vector.memset(m.key_dst[:, T:TK], -1.0)
                nc.vector.memset(m.index_src[:, T:T + 2 * BATCH], 0)


def stage_keys_src(nc, m):
    ctx, (came,) = stage(nc, ["pairs_came"])
    with ctx:
        pairs = ctx.enter_context(nc.sbuf_tensor("key_pairs", [P, T, 2], fp32))
        with nc.Block() as block:
            @block.sync
            def _(sp):
                sp.dma_start(pairs[:], m.rows_src[:, 0:T, :]).then_inc(came, 16)

            @block.vector
            def _(dve):
                dve.wait_ge(came, 16)
                nc.vector.tensor_copy(m.index_dst[:, 0:T], pairs[:, :, 0].bitcast(i32))
                nc.vector.tensor_copy(m.key_src[:, 0:T], pairs[:, :, 1])
                nc.vector.memset(m.key_src[:, T:TK], -1.0)
                nc.vector.memset(m.index_dst[:, T:T + 2 * BATCH], 0)



STEP = 7
assert NB % STEP == 0


def stage_weights(nc, m, a):
    ctx, (zeroed, loaded) = stage(nc, ["weights_zeroed", "weights_loaded"])
    with ctx, nc.Block() as block:
        loads = []
        for i, n in enumerate(("int", "upd")):
            W, cols = a[f"W_{n}"], slice(i * F, (i + 1) * F)
            loads.append((m.w_src[:, cols], W[0:F, :]))
            loads.append((m.w_dst[0:F, cols], W[F:2 * F, :]))
            loads.append((m.w_dst[F:F + 1, cols], a[f"b_{n}"].unsqueeze(0)))
            loads += [(m.w_edge[q * ROW:q * ROW + EF, q, cols], W[2 * F:, :]) for q in range(GROUP)]
            loads.append((m.gain[:, cols], a[f"g_{n}"].partition_broadcast(P)))
            loads.append((m.shift[:, cols], a[f"be_{n}"].partition_broadcast(P)))
        loads += [(m.w_edge3[q * ROW:q * ROW + EF, q, :], a["W1"][F:, :]) for q in range(GROUP)]
        for t, W, b in ((m.w_h3, a["W1"][0:F, :], a["b1"]), (m.w_out3, a["W2"], a["b2"])):
            loads += [(t[0:F, :], W), (t[F:F + 1, :], b.unsqueeze(0))]
        for l in range(LAYERS):
            for t, W, b in ((m.w_nb, a["nb_W"][l], a["nb_b"][l]), (m.w_self, a["self_W"][l], a["self_b"][l]),
                            (m.w_att_row, a["att1_W"][l, 0:F, :], a["att1_b"][l])):
                loads += [(t[0:F, l, :], W), (t[F:F + 1, l, :], b.unsqueeze(0))]
            loads.append((m.w_att_col[:, l, :], a["att1_W"][l, F:2 * F, :]))
            loads.append((m.att2[:, l, :], a["att2_W"][l, :, 0].partition_broadcast(P)))
            loads.append((m.att2_b[:, l:l + 1], a["att2_b"][l].partition_broadcast(P)))
        loads += [(t[:], a[n].partition_broadcast(P)) for t, n in
                  ((m.g_bn, "g_bn"), (m.be_bn, "be_bn"), (m.gamma3, "gamma"), (m.beta3, "beta"))]
        loads.append((m.w_r[F:F + 1, :], a["b_l1"].unsqueeze(0)))
        turned = [(m.w_l[:], a["w_l"].rearrange("o i -> i o")), (m.w_r[0:F, :], a["w_r"].rearrange("o i -> i o"))]

        @block.vector
        def _(dve):
            nc.vector.memset(m.w_edge[:], 0.0).then_inc(zeroed, 1)
            nc.vector.memset(m.w_edge3[:], 0.0).then_inc(zeroed, 1)

        @block.sync
        def _(sp):
            sp.wait_ge(zeroed, 2)
            for to, of in loads:
                sp.dma_start(to, of, allow_slow_non_contiguous=True).then_inc(loaded, 16)

        @block.scalar
        def _(act):
            for to, of in turned:
                act.dma_start(to, of, allow_slow_non_contiguous=True).then_inc(loaded, 16)
            act.wait_ge(loaded, 16 * (len(loads) + len(turned)))


def normalize(nc, dve, o, x, out, stat, std_sem, var_sem):
    mean, var = stat[:, 0, :], stat[:, 1, :]
    o.wait()
    o.then(nc.vector.tensor_reduce(mean, x, AX.X, ALU.add))
    o.then(nc.vector.tensor_scalar(mean, mean, 1.0 / F, None, ALU.mult))
    o.then(nc.vector.tensor_tensor(out[0], x, b3(mean, F), ALU.subtract))
    o.then(nc.vector.tensor_tensor(out[1], out[0], out[0], ALU.mult))
    o.then(nc.vector.tensor_reduce(var, out[1], AX.X, ALU.add))
    nc.vector.tensor_scalar(var, var, 1.0 / F, EPS, ALU.mult, ALU.add).then_inc(var_sem, 1)
    dve.wait_ge(std_sem, 1)
    o.then(nc.vector.reciprocal(mean, var))
    o.then(nc.vector.tensor_tensor(out[0], out[0], b3(mean, F), ALU.mult))


def root(nc, act, stat, var_sem, std_sem):
    act.wait_ge(var_sem, 1)
    nc.scalar.activation(stat[:, 1, :], stat[:, 1, :], ACT.Sqrt).then_inc(std_sem, 1)


def stage_norm(nc, m, name, x, h, table=None):
    ctx, (order, var_sem, std_sem, ready, stored) = stage(nc, [f"{name}_{s}" for s in (
        "order", "var", "std", "ready", "stored")])
    with ctx:
        stat = ctx.enter_context(nc.sbuf_tensor(f"{name}_stat", [P, 2, NB], fp32))
        square = ctx.enter_context(nc.sbuf_tensor(f"{name}_sq", [P, NB, F], fp32))
        with nc.Block() as block:
            @block.vector
            def _(dve):
                o = Order(dve, order)
                o.mark(nc.vector.memset(stat[:], 0.0))
                normalize(nc, dve, o, x, (h, square[:]), stat, std_sem, var_sem)
                nc.vector.tensor_scalar(h, h, 0.0, None, ALU.max).then_inc(ready, 1)

            @block.scalar
            def _(act):
                root(nc, act, stat, var_sem, std_sem)

            @block.sync
            def _(sp):
                if table is not None:
                    sp.wait_ge(ready, 1)
                    sp.dma_start(table.rearrange("(b p) f -> p b f", p=P), h).then_inc(stored, 16)
                    sp.wait_ge(stored, 16)


def stage_turn(nc, m, name, x, turned, w=F):
    ctx, (done, taken) = stage(nc, [f"{name}_{s}" for s in ("done", "taken")])
    with ctx:
        ps = ctx.enter_context(nc.psum_tensor(f"{name}_ps", [P, 8 * P], fp32))
        with nc.Block() as block:
            @block.tensor
            def _(pe):
                for k in range(NB // STEP):
                    pe.wait_ge(taken, k + 1)
                    for i in range(STEP):
                        src = x[:, k * STEP + i, :]
                        last = nc.tensor.transpose(ps[0:w, i * P:(i + 1) * P], src, m.ident[:])
                    last.then_inc(done, 1)

            @block.vector
            def _(dve):
                if w == F:
                    nc.vector.memset(turned[F:F + 1, :], 1.0).then_inc(taken, 1)
                else:
                    dve.sem_inc(taken, 1)
                for k in range(NB // STEP):
                    dve.wait_ge(done, k + 1)
                    nc.vector.tensor_copy(turned[0:w, bass.ds(k * STEP * P, STEP * P)],
                                          ps[0:w, 0:STEP * P]).then_inc(taken, 1)


def stage_product(nc, m, name, terms, out, width, plus=None, table=None):
    ctx, (done, taken, stored) = stage(nc, [f"{name}_{s}" for s in ("done", "taken", "stored")])
    with ctx:
        ps = ctx.enter_context(nc.psum_tensor(f"{name}_ps", [P, 8, P], fp32))
        with nc.Block() as block:
            @block.tensor
            def _(pe):
                pe.sem_inc(taken, 1)
                for k in range(NB // STEP):
                    pe.wait_ge(taken, k + 1)
                    for i in range(STEP):
                        for n, (turned, w) in enumerate(terms):
                            last = nc.tensor.matmul(ps[:, i, 0:width], turned[0:w.shape[0], bass.ds((k * STEP + i) * P, P)], w,
                                                    start=n == 0, stop=n == len(terms) - 1)
                    last.then_inc(done, 1)

            @block.vector
            def _(dve):
                for k in range(NB // STEP):
                    dve.wait_ge(done, k + 1)
                    at = bass.ds(k * STEP, STEP)
                    if plus is None:
                        nc.vector.tensor_copy(out[:, at, :], ps[:, 0:STEP, 0:width]).then_inc(taken, 1)
                    else:
                        nc.vector.tensor_tensor(out[:, at, :], ps[:, 0:STEP, 0:width], plus[:, at, :], ALU.add).then_inc(taken, 1)

            @block.sync
            def _(sp):
                if table is not None:
                    sp.wait_ge(taken, NB // STEP + 1)
                    sp.dma_start(table.rearrange("(b p) f -> p b f", p=P), out).then_inc(stored, 16)
                    sp.wait_ge(stored, 16)


def stage_attention(nc, m, l, turned, row_part, col_part, table):
    ctx, (inner, relued, outer, taken, stored) = stage(nc, [f"att{l}_{s}" for s in (
        "inner", "relued", "outer", "taken", "stored")])
    HALF = STEP * P // 2
    with ctx:
        hidden_ps = ctx.enter_context(nc.psum_tensor(f"att{l}_hid", [P, 4, 512], fp32))
        out_ps = ctx.enter_context(nc.psum_tensor(f"att{l}_out", [P, 2, 512], fp32))
        hidden = ctx.enter_context(nc.sbuf_tensor(f"att{l}_hidden", [F + 1, 2, STEP * P], fp32))
        with nc.Block() as block:
            @block.tensor
            def _(pe):
                for k in range(NB // STEP):
                    pe.wait_ge(taken, k + 1)
                    for s, w in enumerate((m.w_nb, m.w_self)):
                        for h in range(2):
                            last = nc.tensor.matmul(hidden_ps[0:F, 2 * s + h, 0:HALF], w[:, l, :],
                                                    turned[:, bass.ds(k * STEP * P + h * HALF, HALF)], start=True, stop=True)
                    last.then_inc(inner, 1)
                    pe.wait_ge(relued, k + 1)
                    for s, (w, n) in enumerate(((m.w_att_row, F + 1), (m.w_att_col, F))):
                        for i in range(STEP):
                            last = nc.tensor.matmul(out_ps[:, s, i * F:(i + 1) * F], hidden[0:n, s, i * P:(i + 1) * P],
                                                    w[:, l, :], start=True, stop=True)
                    last.then_inc(outer, 1)

            @block.vector
            def _(dve):
                nc.vector.memset(hidden[F:F + 1, :, :], 1.0).then_inc(taken, 1)
                for k in range(NB // STEP):
                    dve.wait_ge(inner, k + 1)
                    for s in range(2):
                        last = nc.vector.tensor_scalar(hidden[0:F, s, :].rearrange("p (h c) -> p h c", h=2),
                                                       hidden_ps[0:F, 2 * s:2 * s + 2, 0:HALF], 0.0, None, ALU.max)
                    last.then_inc(relued, 1)
                    dve.wait_ge(outer, k + 1)
                    for s, part in enumerate((row_part, col_part)):
                        last = nc.vector.tensor_copy(part[:, bass.ds(k * STEP, STEP), :],
                                                     out_ps[:, s, 0:STEP * F].rearrange("p (b f) -> p b f", f=F))
                    last.then_inc(taken, 1)

            @block.sync
            def _(sp):
                sp.wait_ge(taken, NB // STEP + 1)
                sp.dma_start(table.rearrange("(b p) f -> p b f", p=P), col_part[:]).then_inc(stored, 16)
                sp.wait_ge(stored, 16)


def stage_gate_norm(nc, m, sum_acc, square_acc, scale, shift):
    ctx, (order, summed, var_sem, std_sem) = stage(nc, ["gn_order", "gn_summed", "gn_var", "gn_std"])
    with ctx:
        ps = ctx.enter_context(nc.psum_tensor("gn_ps", [P, 2, 512], fp32))
        mu = ctx.enter_context(nc.sbuf_tensor("gn_mu", [P, 2 * F], fp32))
        var = ctx.enter_context(nc.sbuf_tensor("gn_var", [P, 2 * F], fp32))
        with nc.Block() as block:
            @block.tensor
            def _(pe):
                for i, acc in enumerate((sum_acc, square_acc)):
                    for c in range(BATCH):
                        last = nc.tensor.matmul(ps[:, i, 0:2 * F], m.ones[:], acc[:, c, :], start=c == 0, stop=c == BATCH - 1)
                last.then_inc(summed, 1)

            @block.vector
            def _(dve):
                o = Order(dve, order)
                dve.wait_ge(summed, 1)
                o.then(nc.vector.tensor_scalar(mu[:], ps[:, 0, 0:2 * F], 1.0 / E, None, ALU.mult))
                o.then(nc.vector.tensor_tensor(shift[:], mu[:], mu[:], ALU.mult))
                o.then(nc.vector.scalar_tensor_tensor(out=var[:], in0=ps[:, 1, 0:2 * F], scalar=1.0 / E, in1=shift[:],
                                                      op0=ALU.mult, op1=ALU.subtract))
                nc.vector.tensor_scalar(var[:], var[:], 0.0, EPS, ALU.max, ALU.add).then_inc(var_sem, 1)
                dve.wait_ge(std_sem, 1)
                o.then(nc.vector.reciprocal(scale[:], var[:]))
                o.then(nc.vector.tensor_tensor(scale[:], scale[:], m.gain[:], ALU.mult))
                o.then(nc.vector.tensor_tensor(mu[:], mu[:], scale[:], ALU.mult))
                o.then(nc.vector.tensor_tensor(shift[:], m.shift[:], mu[:], ALU.subtract))

            @block.scalar
            def _(act):
                act.wait_ge(var_sem, 1)
                nc.scalar.activation(var[:], var[:], ACT.Sqrt).then_inc(std_sem, 1)


def stage_conv_out(nc, m):
    ctx, (order, d_sem, mean_sem, var_sem, std_sem, neg_sem, log_sem, a_order) = stage(nc, ["co_" + s for s in (
        "order", "diff", "mean", "var", "std", "neg", "log", "act_order")])
    with ctx:
        ps = ctx.enter_context(nc.psum_tensor("co_ps", [P, 2, 512], fp32))
        d = ctx.enter_context(nc.sbuf_tensor("co_d", [P, NB, F], fp32))
        q = ctx.enter_context(nc.sbuf_tensor("co_q", [P, NB, F], fp32))
        mu = ctx.enter_context(nc.sbuf_tensor("co_mu", [P, F], fp32))
        std = ctx.enter_context(nc.sbuf_tensor("co_std", [P, F], fp32))
        with nc.Block() as block:
            @block.tensor
            def _(pe):
                for b in range(NB):
                    last = nc.tensor.matmul(ps[:, 0, 0:F], m.ones[:], m.acc[:, b, 0:F], start=b == 0, stop=b == NB - 1)
                last.then_inc(mean_sem, 1)
                pe.wait_ge(d_sem, 1)
                for b in range(NB):
                    last = nc.tensor.matmul(ps[:, 1, 0:F], (m.valid if b == NB - 1 else m.ones)[:], q[:, b, :],
                                            start=b == 0, stop=b == NB - 1)
                last.then_inc(var_sem, 1)

            @block.vector
            def _(dve):
                o = Order(dve, order)
                dve.wait_ge(mean_sem, 1)
                o.then(nc.vector.tensor_scalar(mu[:], ps[:, 0, 0:F], 1.0 / N, None, ALU.mult))
                o.then(nc.vector.tensor_tensor(d[:], m.acc[:, :, 0:F], b2(mu[:], NB), ALU.subtract))
                nc.vector.tensor_tensor(q[:], d[:], d[:], ALU.mult).then_inc(d_sem, 1)
                dve.wait_ge(var_sem, 1)
                nc.vector.tensor_scalar(std[:], ps[:, 1, 0:F], 1.0 / N, EPS, ALU.mult, ALU.add).then_inc(d_sem, 1)
                dve.wait_ge(std_sem, 1)
                o.then(nc.vector.reciprocal(mu[:], std[:]))
                o.then(nc.vector.tensor_tensor(mu[:], mu[:], m.g_bn[:], ALU.mult))
                o.then(nc.vector.tensor_tensor(d[:], d[:], b2(mu[:], NB), ALU.mult))
                o.then(nc.vector.tensor_tensor(d[:], d[:], b2(m.be_bn[:], NB), ALU.add))
                o.then(nc.vector.tensor_tensor(d[:], d[:], m.H[:], ALU.add))
                o.then(nc.vector.tensor_scalar(q[:], d[:], -1.0, None, ALU.mult))
                nc.vector.tensor_tensor(q[:], q[:], d[:], ALU.min).then_inc(neg_sem, 1)
                o.then(nc.vector.scalar_tensor_tensor(out=m.X[:], in0=d[:], scalar=0.0, in1=m.X[:], op0=ALU.max, op1=ALU.add))
                dve.wait_ge(log_sem, 1)
                o.then(nc.vector.tensor_tensor(m.X[:], m.X[:], q[:], ALU.add))

            @block.scalar
            def _(act):
                act.wait_ge(d_sem, 2)
                nc.scalar.activation(std[:], std[:], ACT.Sqrt).then_inc(std_sem, 1)
                act.wait_ge(neg_sem, 1)
                nc.scalar.activation(q[:], q[:], ACT.Exp).then_inc(a_order, 1)
                act.wait_ge(a_order, 1)
                nc.scalar.activation(q[:], q[:], ACT.Ln, bias=1.0).then_inc(log_sem, 1)


def stage_vector(nc, name, steps):
    ctx, (order,) = stage(nc, [f"{name}_order"])
    with ctx, nc.Block() as block:
        @block.vector
        def _(dve):
            steps(Order(dve, order))



def stage_conv_sums(nc, m, part_dst, table, kept, sum_acc, square_acc):
    W = 2 * F
    ctx = Stage(nc)
    with ctx:
        def sb(n, s, d=fp32):
            return ctx.enter_context(nc.sbuf_tensor(f"cs_{n}", s, d))

        def sem(n):
            return ctx.sem(f"cs_{n}")

        def sem2(n):
            return [sem(f"{n}{j}") for j in range(2)]
        e = sb("e", [P, 2, BATCH, ROW])
        rows = sb("rows", [P, 2, BATCH, W])
        index_now = sb("index", [P, 2, BATCH], i32)
        onehot = sb("onehot", [P, 2, BATCH, P])
        turned = sb("turned", [P, 2, BATCH, P])
        e_turned = sb("e_turned", [GROUP * ROW, 2, len(GROUPS), P])
        v = sb("v", [P, 2, BATCH, W])
        square = sb("square", [P, BATCH, W])
        turn_ps = ctx.enter_context(nc.psum_tensor("cs_turn_ps", [P, BATCH, P], fp32))
        e_ps = ctx.enter_context(nc.psum_tensor("cs_e_ps", [P, 4, P], fp32))
        v_ps = [ctx.enter_context(nc.psum_tensor(f"cs_v_ps{j}", [P, BATCH, W], fp32)) for j in range(2)]
        slot_free, indexed, arrived = sem2("free"), sem2("indexed"), sem2("arrived")
        gate, order = sem("gate"), sem("order")
        e_came, stored = sem2("e_came"), sem2("stored")
        hot, turn, turned_s, v_done, v_ready, squared = (sem(n) for n in ("hot", "turn_s", "turned_s", "v_done", "ready", "squared"))
        steps = ITERS

        with nc.Block() as block:
            @block.gpsimd
            def _(pool):
                fetch_rows(nc, pool, index_now, rows, table, indexed, gate, arrived)

            @block.sync
            def _(sp):
                def load(j, b):
                    sp.dma_start(e[:, j, :, :], m.rows_dst[:, bass.ds(b * BATCH, BATCH), :]).then_inc(e_came[j], 16)

                def store(j, b):
                    sp.wait_ge(v_ready, b + 1)
                    sp.dma_start(kept[:, bass.ds(b * BATCH, BATCH), :], v[:, j, :, :]).then_inc(stored[j], 16)
                for j in range(2):
                    load(j, j)
                with sp.Fori(0, steps - 1) as k:
                    for j in range(2):
                        sp.wait_ge(turn, k * 2 + j + 1)
                        load(j, k * 2 + 2 + j)
                        store(j, k * 2 + j)
                sp.wait_ge(turn, steps * 2 - 1)
                load(0, steps * 2)
                for j in range(2):
                    store(j, steps * 2 - 2 + j)
                for j in range(2):
                    sp.wait_ge(stored[j], 16 * steps)

            @block.tensor
            def _(pe):
                def values(b, j, n):
                    blocks = load_pair_blocks(nc, pe, m, b)
                    pe.wait_ge(hot, b + 1)
                    pe.wait_ge(e_came[j], n)
                    pe.sem_inc(gate, 1)
                    for t in range(BATCH):
                        nc.tensor.transpose(turn_ps[:, t, :], onehot[:, j, t, :], m.ident[:])
                    for g, tiles in enumerate(GROUPS):
                        last = nc.tensor.transpose(e_ps[0:len(tiles) * ROW, g, :],
                                                   e[:, j, tiles[0]:tiles[-1] + 1, :].rearrange("p t w -> p (t w)"), m.ident[:])
                    last.then_inc(turn, 1)
                    pe.wait_ge(turned_s, b + 1)
                    pe.sem_inc(gate, 1)
                    for t in range(BATCH):
                        at = part_dst[:, bass.ds(blocks[t // 2], 1), :].rearrange("p a f -> p (a f)")
                        nc.tensor.matmul(v_ps[j][:, t, :], turned[:, j, t, :], at, start=True, stop=False)
                        r = len(GROUPS[t // GROUP]) * ROW
                        last = nc.tensor.matmul(v_ps[j][:, t, :], e_turned[0:r, j, t // GROUP, :],
                                                m.w_edge[0:r, t % GROUP, :], start=False, stop=True)
                    last.then_inc(v_done, 1)
                values(0, 0, 16)
                with pe.Fori(0, steps) as k:
                    for j in range(2):
                        values(k * 2 + j + 1, 1 - j, k * 16 + 16 * (j + 1))

            @block.scalar
            def _(act):
                def turn_out(b, j):
                    act.wait_ge(turn, b + 1)
                    act.sem_inc(gate, 1)
                    for h in range(2):
                        nc.scalar.copy(turned[:, j, 4 * h:4 * h + 4, :], turn_ps[:, 4 * h:4 * h + 4, :])
                    whole, rest = len(GROUPS) - 1, len(GROUPS[-1]) * ROW
                    nc.scalar.copy(e_turned[:, j, 0:whole, :], e_ps[0:GROUP * ROW, 0:whole, :])
                    nc.scalar.copy(e_turned[0:rest, j, whole, :], e_ps[0:rest, whole, :]).then_inc(turned_s, 1)
                indices = IndexStager(nc, act, m.index_src, index_now, slot_free, indexed, gate)
                indices.first()
                turn_out(0, 0)
                with act.Fori(0, steps) as k:
                    for j in range(2):
                        b = k * 2 + j
                        turn_out(b + 1, 1 - j)
                        indices.after(k, j)
                        act.wait_ge(v_ready, b + 1)
                        act.wait_ge(order, b + 1)
                        act.sem_inc(gate, 1)
                        nc.scalar.square(square[:], v[:, j, :, :]).then_inc(squared, 1)

            @block.vector
            def _(dve):
                nc.vector.memset(sum_acc[:], 0.0)
                nc.vector.memset(square_acc[:], 0.0).then_inc(order, 1)
                dve.wait_ge(order, 1)
                one_hots(nc, m, onehot, m.key_dst, 0, 0).then_inc(hot, 1)

                def step(k, first):
                    for j in range(2):
                        b = k * 2 + j
                        one_hots(nc, m, onehot, m.key_dst, b + 1, 1 - j).then_inc(hot, 1)
                        dve.wait_ge(v_done, b + 1)
                        dve.wait_ge(arrived[j], k * (16 * BATCH) + 16 * BATCH)
                        if not first:
                            dve.wait_ge(stored[j], k * 16)
                        dve.sem_inc(gate, 1)
                        nc.vector.tensor_tensor(v[:, j, :, :], v_ps[j][:], rows[:, j, :, :], ALU.add).then_inc(v_ready, 1)
                        dve.wait_ge(v_ready, b + 1)
                        dve.sem_inc(slot_free[j], 1)
                        nc.vector.tensor_tensor(sum_acc[:], sum_acc[:], v[:, j, :, :], ALU.add)
                        dve.wait_ge(squared, b + 1)
                        dve.sem_inc(gate, 1)
                        nc.vector.tensor_tensor(square_acc[:], square_acc[:], square[:], ALU.add).then_inc(order, 1)
                        dve.wait_ge(order, b + 2)
                step(0, True)
                with dve.Fori(1, steps) as k:
                    step(k, False)


def stage_conv_messages(nc, m, kept, scale, shift):
    W = 2 * F
    LOADS = 4
    batches = T // BATCH
    assert batches % LOADS == 0
    ctx = Stage(nc)
    with ctx:
        def sb(n, s, d=fp32):
            return ctx.enter_context(nc.sbuf_tensor(f"cm_{n}", s, d))

        def sem(n):
            return ctx.sem(f"cm_{n}")
        v = sb("v", [P, LOADS, BATCH, W])
        log = sb("log", [P, 2, BATCH, W])
        gate_v = sb("gate", [P, 2, BATCH, F])
        message = sb("message", [P, 2, BATCH, F + 1])
        onehot = sb("onehot", [P, 2, BATCH, P])
        sums = [ctx.enter_context(nc.psum_tensor(f"cm_sums_ps{j}", [P, PPB, P], fp32)) for j in range(2)]
        came = [sem(f"came{j}") for j in range(LOADS)]
        normed, logged, opened, gated, ready, summed = (sem(n) for n in ("normed", "logged", "opened", "gated", "ready", "summed"))
        gate, order, act_order = sem("gate_s"), sem("order"), sem("act_order")
        with nc.Block() as block:
            reorder(nc, ctx, block, "to_src", m.packed_src, m.rows_src)

            @block.scalar
            def _(act):
                def load(b, j):
                    act.dma_start(v[:, j, :, :], kept[:, bass.ds(b * BATCH, BATCH), :]).then_inc(came[j], 16)

                def soften(b, j):
                    h = j % 2
                    act.wait_ge(normed, b + 1)
                    act.sem_inc(gate, 1)
                    nc.scalar.activation(log[:, h, :, :], v[:, j, :, :], ACT.Abs).then_inc(act_order, 1)
                    act.wait_ge(act_order, b * 2 + 1)
                    act.sem_inc(gate, 1)
                    nc.scalar.activation(log[:, h, :, :], log[:, h, :, :], ACT.Exp, scale=-1.0).then_inc(act_order, 1)
                    act.wait_ge(act_order, b * 2 + 2)
                    act.sem_inc(gate, 1)
                    nc.scalar.activation(log[:, h, :, :], log[:, h, :, :], ACT.Ln, bias=1.0).then_inc(logged, 1)

                def open_gate(b, j):
                    act.wait_ge(opened, b + 1)
                    act.sem_inc(gate, 1)
                    nc.scalar.activation(gate_v[:, j % 2, :, :], gate_v[:, j % 2, :, :], ACT.Exp).then_inc(gated, 1)
                nc.scalar.preload_act_table_set("natural_log_exp_and_others")
                for j in range(LOADS):
                    load(j, j)
                soften(0, 0)
                open_gate(0, 0)
                soften(1, 1)
                with act.Fori(0, batches // LOADS - 1) as k:
                    for i in range(1, 1 + LOADS):
                        b, j = k * LOADS + i, i % LOADS
                        open_gate(b, j)
                        soften(b + 1, (j + 1) % LOADS)
                        act.wait_ge(ready, b)
                        load(b + LOADS - 1, (j - 1) % LOADS)
                for b in range(batches - LOADS + 1, batches):
                    open_gate(b, b % LOADS)
                    if b + 1 < batches:
                        soften(b + 1, (b + 1) % LOADS)

            @block.vector
            def _(dve):
                o = Order(dve, order)
                o.mark(nc.vector.memset(m.acc[:], 0.0))
                o.then(nc.vector.memset(message[:, :, :, F:F + 1], 1.0))

                def norm(b, j, n, s):
                    dve.wait_ge(came[j], n)
                    dve.sem_inc(gate, 1)
                    s.then(nc.vector.tensor_tensor(v[:, j, :, :], v[:, j, :, :], b2(scale[:], BATCH), ALU.mult))
                    nc.vector.tensor_tensor(v[:, j, :, :], v[:, j, :, :], b2(shift[:], BATCH), ALU.add).then_inc(normed, 1)

                def multiply(b, j, s, behind=None):
                    h = j % 2
                    dve.wait_ge(logged, b + 1)
                    dve.sem_inc(gate, 1)
                    nc.vector.scalar_tensor_tensor(out=gate_v[:, h, :, :], in0=v[:, j, :, 0:F], scalar=0.0,
                                                   in1=log[:, h, :, 0:F], op0=ALU.min, op1=ALU.subtract).then_inc(opened, 1)
                    s.mark(nc.vector.scalar_tensor_tensor(out=log[:, h, :, F:W], in0=v[:, j, :, F:W], scalar=0.0,
                                                          in1=log[:, h, :, F:W], op0=ALU.max, op1=ALU.add))
                    one_hots(nc, m, onehot, m.key_dst, b, h)
                    blocks = None if behind is None else load_pair_blocks(nc, dve, m, behind)
                    dve.wait_ge(gated, b + 1)
                    s.wait()
                    dve.sem_inc(gate, 1)
                    nc.vector.tensor_tensor(message[:, h, :, 0:F], gate_v[:, h, :, :], log[:, h, :, F:W],
                                            ALU.mult).then_inc(ready, 1)
                    return blocks

                def collect(b, j, s, blocks):
                    dve.wait_ge(summed, b + 1)
                    s.mark(add_to_nodes(nc, dve, s, m, m.acc[:], sums[j % 2], blocks))
                norm(0, 0, 16, o)
                norm(1, 1, 16, o)
                multiply(0, 0, o)
                start = o.n
                with dve.Fori(0, batches // LOADS - 1) as k:
                    s = Order(dve, order, LOADS * (2 + PPB), k, start)
                    for j in range(LOADS):
                        b = k * LOADS + j
                        norm(b + 2, (j + 2) % LOADS, k * 16 + 16 * ((j + 2) // LOADS + 1), s)
                        blocks = multiply(b + 1, (j + 1) % LOADS, s, behind=b)
                        collect(b, j, s, blocks)
                    assert s.n == s.last
                o.n = start + (batches // LOADS - 1) * LOADS * (2 + PPB)
                for b in range(batches - LOADS, batches):
                    if b + 2 < batches:
                        norm(b + 2, (b + 2) % LOADS, 16 * ((b + 2) // LOADS + 1), o)
                    if b + 1 < batches:
                        blocks = multiply(b + 1, (b + 1) % LOADS, o, behind=b)
                    else:
                        blocks = load_pair_blocks(nc, dve, m, b)
                    collect(b, b % LOADS, o, blocks)

            @block.tensor
            def _(pe):
                with pe.Fori(0, ITERS) as k:
                    for j in range(2):
                        b = k * 2 + j
                        pe.wait_ge(ready, b + 1)
                        pe.sem_inc(gate, 1)
                        for t in range(BATCH):
                            last = nc.tensor.matmul(sums[j][:, t // 2, 0:F + 1], onehot[:, j, t, :], message[:, j, t, :],
                                                    start=t % 2 == 0, stop=t % 2 == 1)
                        last.then_inc(summed, 1)


def stage_gather_sum(nc, m, name, index, keys, table, acc, weight=None):
    ctx = Stage(nc)
    with ctx:
        def sem(n):
            return ctx.sem(f"{name}_{n}")

        def sem2(n):
            return [sem(f"{n}{j}") for j in range(2)]
        rows = ctx.enter_context(nc.sbuf_tensor(f"{name}_rows", [P, 2, BATCH, F], fp32))
        index_now = ctx.enter_context(nc.sbuf_tensor(f"{name}_index", [P, 2, BATCH], i32))
        onehot = ctx.enter_context(nc.sbuf_tensor(f"{name}_onehot", [P, 2, BATCH, P], fp32))
        sums = [ctx.enter_context(nc.psum_tensor(f"{name}_sums_ps{j}", [P, PPB, P], fp32)) for j in range(2)]
        slot_free, indexed, arrived, hot, summed = sem2("free"), sem2("indexed"), sem2("arrived"), sem2("hot"), sem2("summed")
        gate, order = sem("gate"), sem("order")
        with nc.Block() as block:
            @block.gpsimd
            def _(pool):
                fetch_rows(nc, pool, index_now, rows, table, indexed, gate, arrived)

            @block.scalar
            def _(act):
                indices = IndexStager(nc, act, index, index_now, slot_free, indexed, gate)
                indices.first()
                with act.Fori(0, ITERS) as k:
                    for j in range(2):
                        indices.after(k, j)

            @block.vector
            def _(dve):
                o = Order(dve, order)
                o.then(nc.vector.memset(acc, 0.0))
                with dve.Fori(0, ITERS) as k:
                    s = Order(dve, order, 2 * PPB, k, o.n)
                    for j in range(2):
                        one_hots(nc, m, onehot, keys, k * 2 + j, j, weight).then_inc(hot[j], 1)
                        blocks = load_pair_blocks(nc, dve, m, k * 2 + j)
                        dve.wait_ge(summed[j], k + 1)
                        dve.sem_inc(slot_free[j], 1)
                        s.mark(add_to_nodes(nc, dve, s, m, acc, sums[j], blocks))
                    assert s.n == s.last

            @block.tensor
            def _(pe):
                with pe.Fori(0, ITERS) as k:
                    for j in range(2):
                        pe.wait_ge(order, k * (2 * PPB) + j * PPB + 1)
                        pe.wait_ge(hot[j], k + 1)
                        pe.wait_ge(arrived[j], k * (16 * BATCH) + 16 * BATCH)
                        pe.sem_inc(gate, 1)
                        for t in range(BATCH):
                            last = nc.tensor.matmul(sums[j][:, t // 2, 0:F], onehot[:, j, t, :], rows[:, j, t, :],
                                                    start=t % 2 == 0, stop=t % 2 == 1)
                        last.then_inc(summed[j], 1)


def split3(nc, o, x, parts):
    hi, mid, lo = parts
    o.then(nc.vector.tensor_copy(hi, x))
    o.then(nc.vector.tensor_tensor(x, x, hi, ALU.subtract))
    o.then(nc.vector.tensor_copy(mid, x))
    return nc.vector.tensor_tensor(lo, x, mid, ALU.subtract)


def stage_masks(nc, m, l, row_part3, table, mask, rowsum):
    name = f"mask{l}"
    ctx = Stage(nc)
    with ctx:
        def sb(n, s, d=fp32):
            return ctx.enter_context(nc.sbuf_tensor(f"{name}_{n}", s, d))

        def sem(n):
            return ctx.sem(f"{name}_{n}")

        def sem2(n):
            return [sem(f"{n}{j}") for j in range(2)]
        rows = sb("rows", [P, 2, BATCH, F])
        index_now = sb("index", [P, 2, BATCH], i32)
        onehot = sb("onehot", [P, 2, BATCH, P], bf16)
        turned = sb("turned", [P, 2, BATCH, P], bf16)
        hidden = sb("hidden", [P, 2, BATCH, F])
        logit = sb("logit", [P, 2, BATCH])
        mask_now = sb("mask", [P, 2, BATCH])
        mask3 = sb("mask3", [P, 2, BATCH, 3], bf16)
        first = sb("first", [P, 1])
        turn_ps = ctx.enter_context(nc.psum_tensor(f"{name}_turn_ps", [P, BATCH, P], bf16))
        part_ps = [ctx.enter_context(nc.psum_tensor(f"{name}_part_ps{j}", [P, BATCH, F], fp32)) for j in range(2)]
        sums = [ctx.enter_context(nc.psum_tensor(f"{name}_sums_ps{j}", [P, PPB, P], fp32)) for j in range(2)]
        slot_free, indexed, arrived = sem2("free"), sem2("indexed"), sem2("arrived")
        hot, turn, turned_s, part, logits, opened, masked, summed = (
            sem(n) for n in ("hot", "turn", "turned", "part", "logits", "opened", "masked", "summed"))
        gate, order = sem("gate"), sem("order")
        with nc.Block() as block:
            @block.gpsimd
            def _(pool):
                fetch_rows(nc, pool, index_now, rows, table, indexed, gate, arrived)

            @block.vector
            def _(dve):
                o = Order(dve, order)
                o.then(nc.vector.memset(rowsum, 0.0))
                one_hots(nc, m, onehot, m.key_src, 0, 0, iota=m.iota_b).then_inc(hot, 1)
                with dve.Fori(0, ITERS) as k:
                    s = Order(dve, order, 2 * (7 + PPB), k, o.n)
                    for j in range(2):
                        b = k * 2 + j
                        one_hots(nc, m, onehot, m.key_src, b + 1, 1 - j, iota=m.iota_b).then_inc(hot, 1)
                        dve.wait_ge(part, b + 1)
                        dve.wait_ge(arrived[j], k * (16 * BATCH) + 16 * BATCH)
                        dve.sem_inc(gate, 1)
                        s.then(nc.vector.tensor_tensor(hidden[:, j, :, :], part_ps[j][:], rows[:, j, :, :], ALU.add))
                        dve.sem_inc(slot_free[j], 1)
                        s.then(nc.vector.scalar_tensor_tensor(out=hidden[:, j, :, :], in0=hidden[:, j, :, :], scalar=0.0,
                                                              in1=b2(m.att2[:, l, :], BATCH), op0=ALU.max, op1=ALU.mult))
                        nc.vector.tensor_reduce(logit[:, j, :], hidden[:, j, :, :], AX.X, ALU.add).then_inc(logits, 1)
                        blocks = load_pair_blocks(nc, dve, m, b)
                        dve.wait_ge(opened, b + 1)
                        dve.sem_inc(gate, 1)
                        s.then(nc.vector.tensor_scalar(mask_now[:, j, :], logit[:, j, :], ZETA - GAMMA, GAMMA, ALU.mult, ALU.add))
                        s.then(nc.vector.tensor_scalar(mask_now[:, j, :], mask_now[:, j, :], 0.0, 1.0, ALU.max, ALU.min))
                        nc.vector.tensor_copy(mask[:, bass.ds(b * BATCH, BATCH)], mask_now[:, j, :])
                        split3(nc, s, mask_now[:, j, :], [mask3[:, j, :, i] for i in range(3)]).then_inc(masked, 1)
                        dve.wait_ge(summed, b + 1)
                        s.mark(add_to_nodes(nc, dve, s, m, rowsum, sums[j], blocks))
                    assert s.n == s.last

            @block.scalar
            def _(act):
                def turn_out(b, j):
                    act.wait_ge(turn, b + 1)
                    act.sem_inc(gate, 1)
                    nc.scalar.copy(turned[:, j, :, :], turn_ps[:]).then_inc(turned_s, 1)
                nc.scalar.activation(first[:], m.att2_b[:, l:l + 1], ACT.Sigmoid)
                indices = IndexStager(nc, act, m.index_dst, index_now, slot_free, indexed, gate)
                indices.first()
                turn_out(0, 0)
                with act.Fori(0, ITERS) as k:
                    for j in range(2):
                        b = k * 2 + j
                        turn_out(b + 1, 1 - j)
                        indices.after(k, j)
                        act.wait_ge(logits, b + 1)
                        act.sem_inc(gate, 1)
                        nc.scalar.activation(logit[:, j, :], logit[:, j, :], ACT.Sigmoid, bias=m.att2_b[:, l:l + 1]).then_inc(opened, 1)

            @block.tensor
            def _(pe):
                def spread(b, j):
                    blocks = load_pair_blocks(nc, pe, m, b)
                    pe.wait_ge(hot, b + 1)
                    pe.sem_inc(gate, 1)
                    for t in range(BATCH):
                        last = nc.tensor.transpose(turn_ps[:, t, :], onehot[:, j, t, :], m.ident_b[:])
                    last.then_inc(turn, 1)
                    pe.wait_ge(turned_s, b + 1)
                    pe.sem_inc(gate, 1)
                    for t in range(BATCH):
                        for i in range(3):
                            at = row_part3[:, bass.ds(blocks[t // 2], 1), i, :].rearrange("p a f -> p (a f)")
                            last = nc.tensor.matmul(part_ps[j][:, t, :], turned[:, j, t, :], at, start=i == 0, stop=i == 2)
                    last.then_inc(part, 1)
                spread(0, 0)
                with pe.Fori(0, ITERS) as k:
                    for j in range(2):
                        b = k * 2 + j
                        spread(b + 1, 1 - j)
                        pe.wait_ge(masked, b + 1)
                        pe.sem_inc(gate, 1)
                        for t in range(BATCH):
                            last = nc.tensor.matmul(sums[j][:, t // 2, 0:3], onehot[:, j, t, :], mask3[:, j, t, :],
                                                    start=t % 2 == 0, stop=t % 2 == 1)
                        last.then_inc(summed, 1)


def stage_edge_mlp(nc, m, table, acc):
    ctx = Stage(nc)
    with ctx:
        def sb(n, s, d=fp32):
            return ctx.enter_context(nc.sbuf_tensor(f"mlp_{n}", s, d))

        def sem(n):
            return ctx.sem(f"mlp_{n}")

        def sem2(n):
            return [sem(f"{n}{j}") for j in range(2)]
        e = sb("e", [P, 2, BATCH, ROW])
        rows = sb("rows", [P, 2, BATCH, F])
        index_now = sb("index", [P, 2, BATCH], i32)
        onehot = sb("onehot", [P, 2, BATCH, P])
        e_turned = sb("e_turned", [GROUP * ROW, 2, len(GROUPS), P])
        hidden = sb("hidden", [P, 2, BATCH, F])
        e_ps = [ctx.enter_context(nc.psum_tensor(f"mlp_e_ps{j}", [P, 4, P], fp32)) for j in range(2)]
        part_ps = [ctx.enter_context(nc.psum_tensor(f"mlp_part_ps{j}", [P, BATCH, F], fp32)) for j in range(2)]
        sums = [ctx.enter_context(nc.psum_tensor(f"mlp_sums_ps{j}", [P, PPB, P], fp32)) for j in range(2)]
        slot_free, indexed, arrived, e_came, turn, turned_s, part, ready, summed = (
            sem2(n) for n in ("free", "indexed", "arrived", "e_came", "turn", "turned", "part", "ready", "summed"))
        gate, order = sem("gate"), sem("order")
        with nc.Block() as block:
            @block.gpsimd
            def _(pool):
                fetch_rows(nc, pool, index_now, rows, table, indexed, gate, arrived)

            @block.sync
            def _(sp):
                for j in range(2):
                    sp.sem_inc(turn[j], 1)
                with sp.Fori(0, ITERS) as k:
                    for j in range(2):
                        sp.wait_ge(turn[j], k + 1)
                        sp.dma_start(e[:, j, :, :], m.rows_dst[:, bass.ds(k * 2 * BATCH + j * BATCH, BATCH), :]).then_inc(e_came[j], 16)

            @block.tensor
            def _(pe):
                def edge_part(k, j):
                    pe.wait_ge(e_came[j], k * 16 + 16)
                    pe.sem_inc(gate, 1)
                    for g, tiles in enumerate(GROUPS):
                        last = nc.tensor.transpose(e_ps[j][0:len(tiles) * ROW, g, :],
                                                   e[:, j, tiles[0]:tiles[-1] + 1, :].rearrange("p t w -> p (t w)"), m.ident[:])
                    last.then_inc(turn[j], 1)
                    pe.wait_ge(turned_s[j], k + 1)
                    pe.sem_inc(gate, 1)
                    for t in range(BATCH):
                        n = len(GROUPS[t // GROUP]) * ROW
                        last = nc.tensor.matmul(part_ps[j][:, t, :], e_turned[0:n, j, t // GROUP, :],
                                                m.w_edge3[0:n, t % GROUP, :], start=True, stop=True)
                    last.then_inc(part[j], 1)

                def collect(k, j):
                    pe.wait_ge(ready[j], k + 1)
                    pe.sem_inc(gate, 1)
                    for t in range(BATCH):
                        last = nc.tensor.matmul(sums[j][:, t // 2, 0:F], onehot[:, j, t, :], hidden[:, j, t, :],
                                                start=t % 2 == 0, stop=t % 2 == 1)
                    last.then_inc(summed[j], 1)
                edge_part(0, 0)
                with pe.Fori(0, ITERS - 1) as k:
                    for j in range(2):
                        edge_part(k + j, 1 - j)
                        collect(k, j)
                edge_part(ITERS - 1, 1)
                collect(ITERS - 1, 0)
                collect(ITERS - 1, 1)

            @block.scalar
            def _(act):
                indices = IndexStager(nc, act, m.index_src, index_now, slot_free, indexed, gate)
                indices.first()

                def turn_out(k, j):
                    act.wait_ge(turn[j], k + 2)
                    act.sem_inc(gate, 1)
                    whole, rest = len(GROUPS) - 1, len(GROUPS[-1]) * ROW
                    nc.scalar.copy(e_turned[:, j, 0:whole, :], e_ps[j][0:GROUP * ROW, 0:whole, :])
                    nc.scalar.copy(e_turned[0:rest, j, whole, :], e_ps[j][0:rest, whole, :]).then_inc(turned_s[j], 1)
                turn_out(0, 0)
                with act.Fori(0, ITERS - 1) as k:
                    for j in range(2):
                        turn_out(k + j, 1 - j)
                        indices.after(k, j)
                turn_out(ITERS - 1, 1)

            @block.vector
            def _(dve):
                o = Order(dve, order)
                o.then(nc.vector.memset(acc, 0.0))
                with dve.Fori(0, ITERS) as k:
                    s = Order(dve, order, 2 * (1 + PPB), k, o.n)
                    for j in range(2):
                        one_hots(nc, m, onehot, m.key_dst, k * 2 + j, j)
                        dve.wait_ge(part[j], k + 1)
                        dve.wait_ge(arrived[j], k * (16 * BATCH) + 16 * BATCH)
                        dve.sem_inc(gate, 1)
                        s.then(nc.vector.tensor_tensor(hidden[:, j, :, :], part_ps[j][:], rows[:, j, :, :], ALU.add))
                        dve.sem_inc(slot_free[j], 1)
                        nc.vector.tensor_scalar(hidden[:, j, :, :], hidden[:, j, :, :], 0.0, None, ALU.max).then_inc(ready[j], 1)
                        blocks = load_pair_blocks(nc, dve, m, k * 2 + j)
                        dve.wait_ge(summed[j], k + 1)
                        s.mark(add_to_nodes(nc, dve, s, m, acc, sums[j], blocks))
                    assert s.n == s.last



def build(nc, a, out):
    m = Net()
    top = ExitStack()
    with top:
        def sb(n, s, d=fp32, ctx=top):
            return ctx.enter_context(nc.sbuf_tensor(n, s, d))

        def dram(n, s, d=fp32):
            return nc.dram_tensor(n, s, d).ap()
        m.X, m.H = sb("X", [P, NB, F]), sb("H", [P, NB, F])
        m.acc = sb("acc", [P, NB, F + 1])
        m.out = sb("out", [P, NB, F])
        m.iota_p, m.ident, m.ones = sb("iota_p", [P, P]), sb("ident", [P, P]), sb("ones", [P, P])
        m.iota_b, m.ident_b = sb("iota_b", [P, P], bf16), sb("ident_b", [P, P], bf16)
        m.before, m.valid = sb("before", [P, P]), sb("valid", [P, P])
        m.w_src, m.w_dst, m.w_edge = sb("w_src", [F, 2 * F]), sb("w_dst", [F + 1, 2 * F]), sb("w_edge", [P, GROUP, 2 * F])
        m.w_edge3, m.w_h3, m.w_out3 = sb("w_edge3", [P, GROUP, F]), sb("w_h3", [F + 1, F]), sb("w_out3", [F + 1, F])
        m.w_l, m.w_r = sb("w_l", [F, F]), sb("w_r", [F + 1, F])
        m.w_nb, m.w_self, m.w_att_row = (sb(n, [F + 1, LAYERS, F]) for n in ("w_nb", "w_self", "w_att_row"))
        m.w_att_col, m.att2, m.att2_b = sb("w_att_col", [F, LAYERS, F]), sb("att2", [P, LAYERS, F]), sb("att2_b", [P, LAYERS])
        m.gain, m.shift = sb("gain", [P, 2 * F]), sb("shift", [P, 2 * F])
        m.g_bn, m.be_bn, m.gamma3, m.beta3 = (sb(n, [P, F]) for n in ("g_bn", "be_bn", "gamma3", "beta3"))
        m.index_src, m.index_dst = sb("index_src", [P, T + 2 * BATCH], i32), sb("index_dst", [P, T + 2 * BATCH], i32)
        m.key_dst, m.key_src = sb("key_dst", [P, TK]), sb("key_src", [P, TK])
        m.table_dst, m.table_src = sb("table_dst", [1, P * QR], i32), sb("table_src", [1, P * QR], i32)
        m.rows_dst, m.rows_src = dram("rows_dst", [P, TP, ROW]), dram("rows_src", [P, TP, 2])
        layer0 = ExitStack()
        kept = dram("kept", [P, T, 2 * F])
        fetched128 = dram("fetched128", [NPAD, 2 * F])

        m.packed_src = sb("packed_src", [P, EC, 3], fp32, layer0)
        with ExitStack() as sort:
            m.src, m.dst = sb("src", [P, EC], i32, sort), sb("dst", [P, EC], i32, sort)
            m.packed_dst = sb("packed_dst", [P, EC, 3], fp32, sort)
            m.sentinel_slot = sb("sentinel_slot", [P, EC], fp32, sort)
            m.numbers, m.pair_no = sb("numbers", [P, NB + 1], fp32, sort), sb("pair_no", [P, QR], fp32, sort)
            stage_constants(nc, m, a)
            stage_weights(nc, m, a)
            stage_empty(nc, m)
            stage_place(nc, m)
            stage_reorder_dst(nc, m, a)
        stage_keys_dst(nc, m)

        m.table = m.table_dst
        stage_norm(nc, m, "n0", m.X[:], m.H[:])
        with ExitStack() as conv:
            part_dst = sb("part_dst", [P, NB, 2 * F], ctx=conv)
            with ExitStack() as pre:
                turned, part_src = sb("turned0", [F + 1, NPAD], ctx=pre), sb("part_src", [P, NB, 2 * F], ctx=pre)
                stage_turn(nc, m, "t0", m.H[:], turned)
                stage_product(nc, m, "p0", [(turned, m.w_dst[:])], part_dst[:], 2 * F)
                stage_product(nc, m, "p1", [(turned, m.w_src[:])], part_src[:], 2 * F, table=fetched128)
            sum_acc, square_acc = sb("sum_acc", [P, BATCH, 2 * F], ctx=conv), sb("square_acc", [P, BATCH, 2 * F], ctx=conv)
            scale, shift = sb("bn_scale", [P, 2 * F], ctx=conv), sb("bn_shift", [P, 2 * F], ctx=conv)
            stage_conv_sums(nc, m, part_dst, fetched128, kept, sum_acc, square_acc)
            stage_gate_norm(nc, m, sum_acc, square_acc, scale, shift)
            stage_conv_messages(nc, m, kept, scale, shift)
        layer0.close()
        stage_keys_src(nc, m)
        stage_conv_out(nc, m)

        inverse = sb("inverse", [P, NB])
        count = sb("count", [P, NB])
        table1 = dram("table1", [NPAD, F])
        stage_norm(nc, m, "n1", m.X[:], m.H[:], table=table1)

        def counts(o):
            o.then(nc.vector.tensor_copy(count[:], m.acc[:, :, F]))
            o.then(nc.vector.tensor_scalar(inverse[:], count[:], 1.0, None, ALU.max))
            o.then(nc.vector.reciprocal(inverse[:], inverse[:]))
        stage_vector(nc, "counts", counts)
        stage_gather_sum(nc, m, "sage", m.index_src, m.key_dst, table1, m.out[:])

        def mean(o):
            o.then(nc.vector.tensor_tensor(m.out[:], m.out[:], b3(inverse[:], F), ALU.mult))
        stage_vector(nc, "mean", mean)
        with ExitStack() as sage:
            turned_h, turned_m = sb("turned_h", [F + 1, NPAD], ctx=sage), sb("turned_m", [F + 1, NPAD], ctx=sage)
            stage_turn(nc, m, "t1", m.H[:], turned_h)
            stage_turn(nc, m, "t2", m.out[:], turned_m)
            stage_product(nc, m, "p2", [(turned_m, m.w_l[:]), (turned_h, m.w_r[:])], m.X[:], F, plus=m.X[:])

        m.table = m.table_src
        stage_norm(nc, m, "n2", m.X[:], m.H[:])
        with ExitStack() as hops:
            mask, rowsum = sb("mask", [P, T], ctx=hops), sb("rowsum", [P, NB, 3], ctx=hops)
            inv_root = sb("inv_root", [P, NB], ctx=hops)
            row_part3 = sb("row_part3", [P, NB, 3, F], bf16, hops)

            def start(o):
                o.then(nc.vector.tensor_copy(m.out[:], m.H[:]))
            stage_vector(nc, "hops", start)
            for l in range(LAYERS):
                cols, feats = dram(f"cols{l}", [NPAD, F]), dram(f"feats{l}", [NPAD, F])
                with ExitStack() as pre:
                    turned, col_part = sb(f"turned_l{l}", [F + 1, NPAD], ctx=pre), sb(f"col_part{l}", [P, NB, F], ctx=pre)
                    row_part = sb(f"row_part{l}", [P, NB, F], ctx=pre)
                    stage_turn(nc, m, f"tl{l}", m.H[:], turned)
                    stage_attention(nc, m, l, turned, row_part, col_part, cols)

                    def split(o):
                        o.mark(split3(nc, o, row_part[:], [row_part3[:, :, i, :] for i in range(3)]))
                    stage_vector(nc, f"split{l}", split)
                stage_masks(nc, m, l, row_part3, cols, mask, rowsum[:])
                stage_degree(nc, m, l, rowsum, inv_root, feats)
                stage_gather_sum(nc, m, f"hop{l}", m.index_dst, m.key_src, feats, m.H[:], weight=mask)

                def after(o):
                    o.then(nc.vector.tensor_tensor(m.H[:], m.H[:], b3(inv_root[:], F), ALU.mult))
                    o.then(nc.vector.tensor_tensor(m.out[:], m.out[:], m.H[:], ALU.add))
                stage_vector(nc, f"after{l}", after)

        def hops_out(o):
            o.then(nc.vector.tensor_tensor(m.X[:], m.X[:], m.out[:], ALU.add))
        stage_vector(nc, "hops_out", hops_out)

        m.table = m.table_dst
        stage_norm(nc, m, "n3", m.X[:], m.H[:])
        table3 = dram("table3", [NPAD, F])
        with ExitStack() as mlp:
            turned = sb("turned3", [F + 1, NPAD], ctx=mlp)
            stage_turn(nc, m, "t3", m.H[:], turned)
            stage_product(nc, m, "p3", [(turned, m.w_h3[:])], m.out[:], F, table=table3)
        stage_edge_mlp(nc, m, table3, m.acc[:, :, 0:F])

        with ExitStack() as mlp:
            turned = sb("turned4", [F + 1, NPAD], ctx=mlp)
            stage_turn(nc, m, "t4", m.acc[:], turned, F + 1)
            stage_product(nc, m, "p4", [(turned, m.w_out3[:])], m.out[:], F)
        stage_last_norm(nc, m, inverse, out)


def stage_degree(nc, m, l, rowsum, inv_root, table):
    ctx, (order, rooted, ready, stored) = stage(nc, [f"deg{l}_{s}" for s in ("order", "rooted", "ready", "stored")])
    with ctx:
        scaled = ctx.enter_context(nc.sbuf_tensor(f"deg{l}_scaled", [P, NB, F], fp32))
        with nc.Block() as block:
            @block.vector
            def _(dve):
                o = Order(dve, order)
                o.then(nc.vector.tensor_reduce(inv_root[:], rowsum[:], AX.X, ALU.add))
                nc.vector.tensor_scalar(inv_root[:], inv_root[:], 1e-6, None, ALU.add).then_inc(ready, 1)
                dve.wait_ge(rooted, 1)
                o.then(nc.vector.reciprocal(inv_root[:], inv_root[:]))
                o.then(nc.vector.tensor_scalar(inv_root[:], inv_root[:], 0.0, 10.0, ALU.max, ALU.min))
                nc.vector.tensor_tensor(scaled[:], m.H[:], b3(inv_root[:], F), ALU.mult).then_inc(ready, 1)

            @block.scalar
            def _(act):
                act.wait_ge(ready, 1)
                nc.scalar.activation(inv_root[:], inv_root[:], ACT.Sqrt).then_inc(rooted, 1)

            @block.sync
            def _(sp):
                sp.wait_ge(ready, 2)
                sp.dma_start(table.rearrange("(b p) f -> p b f", p=P), scaled[:]).then_inc(stored, 16)
                sp.wait_ge(stored, 16)


def stage_last_norm(nc, m, inverse, out):
    ctx, (order, var_sem, std_sem, ready, stored) = stage(nc, ["ln_" + s for s in ("order", "var", "std", "ready", "stored")])
    with ctx:
        stat = ctx.enter_context(nc.sbuf_tensor("ln_stat", [P, 2, NB], fp32))
        square = ctx.enter_context(nc.sbuf_tensor("ln_sq", [P, NB, F], fp32))
        with nc.Block() as block:
            @block.vector
            def _(dve):
                o = Order(dve, order)
                o.then(nc.vector.tensor_tensor(m.out[:], m.out[:], b3(inverse[:], F), ALU.mult))
                o.then(nc.vector.tensor_tensor(m.out[:], m.out[:], m.H[:], ALU.add))
                normalize(nc, dve, o, m.out[:], (m.H[:], square[:]), stat, std_sem, var_sem)
                o.then(nc.vector.tensor_tensor(m.H[:], m.H[:], b2(m.gamma3[:], NB), ALU.mult))
                o.then(nc.vector.tensor_tensor(m.H[:], m.H[:], b2(m.beta3[:], NB), ALU.add))
                nc.vector.tensor_tensor(m.H[:], m.H[:], m.X[:], ALU.add).then_inc(ready, 1)

            @block.scalar
            def _(act):
                root(nc, act, stat, var_sem, std_sem)

            @block.sync
            def _(sp):
                sp.wait_ge(ready, 1)
                full = NB - 1
                sp.dma_start(out[0:full * P, :].rearrange("(b p) f -> p b f", p=P), m.H[:, 0:full, :]).then_inc(stored, 16)
                sp.dma_start(out[full * P:N, :], m.H[0:N - full * P, full, :]).then_inc(stored, 16)
                sp.wait_ge(stored, 32)


NAMES = {"x": "x", "L0_gnn_W_int": "W_int", "L0_gnn_b_int": "b_int", "L0_gnn_g_int": "g_int", "L0_gnn_be_int": "be_int",
         "L0_gnn_W_upd": "W_upd", "L0_gnn_b_upd": "b_upd", "L0_gnn_g_upd": "g_upd", "L0_gnn_be_upd": "be_upd",
         "L0_gnn_g_bn": "g_bn", "L0_gnn_be_bn": "be_bn", "L1_gnn_w_l": "w_l", "L1_gnn_w_r": "w_r", "L1_gnn_b": "b_l1",
         "L2_gnn_nb_W": "nb_W", "L2_gnn_nb_b": "nb_b", "L2_gnn_self_W": "self_W", "L2_gnn_self_b": "self_b",
         "L2_gnn_att1_W": "att1_W", "L2_gnn_att1_b": "att1_b", "L2_gnn_att2_W": "att2_W", "L2_gnn_att2_b": "att2_b",
         "L3_gnn_W1": "W1", "L3_gnn_b1": "b1", "L3_gnn_W2": "W2", "L3_gnn_b2": "b2", "L3_gnn_gamma": "gamma",
         "L3_gnn_beta": "beta"}


def kernel(**inputs):
    from concourse import bacc
    from concourse.bass_utils import run_bass_kernel_spmd

    nc = bacc.Bacc("TRN2", target_bir_lowering=False, num_devices=1)
    arrays = {short: np.ascontiguousarray(inputs[name]) for name, short in NAMES.items()}
    for name in ("src", "dst"):
        arrays[name] = np.pad(np.asarray(inputs[name]), (0, P * EC - E), constant_values=SENTINEL).reshape(P, EC)
    arrays["e"] = np.pad(np.asarray(inputs["edge_attr_32"]), ((0, P * EC - E), (0, 0)))
    args = {n: nc.dram_tensor(f"in_{n}", v.shape, mybir.dt.from_np(v.dtype), kind="ExternalInput").ap()
            for n, v in arrays.items()}
    out = nc.dram_tensor("out_dram", [N, F], fp32, kind="ExternalOutput").ap()
    build(nc, args, out)
    r = run_bass_kernel_spmd(nc, [{f"in_{n}": v for n, v in arrays.items()}], core_ids=[0])
    return r.results[0]["out_dram"]
```

```python
import concourse.bass as bass
from concourse import mybir
from contextlib import ExitStack
import numpy as np

fp32 = mybir.dt.float32
i32 = mybir.dt.int32
bf16 = mybir.dt.bfloat16
ALU = mybir.AluOpType
ACT = mybir.ActivationFunctionType
AX = mybir.AxisListType

P = 128
N = 6250
F = 64
EF = 32
E = 200000
NB = -(-N // P)
NPAD = NB * P
EC = 1568
SENTINEL = NPAD
PAIR = 2 * P
BATCH = 8
PPB = BATCH // 2
PAIRS_MAX = (E + NB * (PAIR - 1)) // PAIR
ITERS = -(-PAIRS_MAX // (2 * PPB))
T = ITERS * 2 * BATCH
TP = T + 16
TK = T + BATCH
QR = 7
STEP = 7
assert NB % STEP == 0
EPS = 1e-5
ROW = EF + 2
GROUP = 3
GROUPS = [range(g, min(g + GROUP, BATCH)) for g in range(0, BATCH, GROUP)]
GAMMA, ZETA = -0.45, 1.05
LAYERS = 3


class Order:

    def __init__(self, eng, sem, per_step=0, k=None, before=0):
        self.eng, self.sem, self.n = eng, sem, before
        self.base = 0 if k is None else k * per_step
        self.last = before + per_step

    def mark(self, ins):
        ins.then_inc(self.sem, 1)
        self.n += 1
        return self

    def wait(self):
        self.eng.wait_ge(self.sem, self.base + self.n)

    def then(self, ins):
        self.mark(ins).wait()


class Net:
    pass


def b3(ap, n):
    return ap.unsqueeze(2).to_broadcast([ap.shape[0], ap.shape[1], n])


def b2(ap, n):
    return ap.unsqueeze(1).to_broadcast([ap.shape[0], n, ap.shape[1]])


class Stage(ExitStack):

    def __init__(self, nc):
        super().__init__()
        self.nc, self.sems = nc, []
        self.callback(self.clear)

    def sem(self, name):
        self.sems.append(self.nc.alloc_semaphore(name=name))
        return self.sems[-1]

    def clear(self):
        if self.sems:
            self.nc.clear_and_free_semaphores(self.sems)
            self.nc.all_engine_barrier()


def stage(nc, names):
    ctx = Stage(nc)
    return ctx, [ctx.sem(n) for n in names]


def load_pair_blocks(nc, eng, m, b):
    _, values = nc.values_load_multi_w_load_instructions(
        m.table[0:1, bass.ds(b * PPB, PPB)], engines=[eng.engine], min_val=0, max_val=NB - 1)
    return values


def fetch_rows(nc, pool, index_now, rows, table, indexed, gate, arrived):
    with pool.Fori(0, ITERS) as k:
        for j in range(2):
            pool.wait_ge(indexed[j], k + 1)
            pool.sem_inc(gate, 1)
            for t in range(BATCH):
                nc.gpsimd.indirect_dma_start(rows[:, j, t, :], None, table,
                                             bass.IndirectOffsetOnAxis(index_now[:, j, t:t + 1], 0)).then_inc(arrived[j], 16)


class IndexStager:

    def __init__(self, nc, act, index, index_now, slot_free, indexed, gate, stored=None):
        self.nc, self.act, self.index, self.index_now = nc, act, index, index_now
        self.slot_free, self.indexed, self.gate, self.stored = slot_free, indexed, gate, stored

    def first(self):
        for j in range(2):
            self.nc.scalar.copy(self.index_now[:, j, :], self.index[:, j * BATCH:(j + 1) * BATCH]).then_inc(self.indexed[j], 1)

    def after(self, k, j):
        self.act.wait_ge(self.slot_free[j], k + 1)
        if self.stored is not None:
            self.act.wait_ge(self.stored[j], k * 16 + 16)
        self.act.sem_inc(self.gate, 1)
        self.nc.scalar.copy(self.index_now[:, j, :],
                            self.index[:, bass.ds((k + 1) * 2 * BATCH + j * BATCH, BATCH)]).then_inc(self.indexed[j], 1)


def one_hots(nc, m, onehot, keys, b, j, iota=None):
    for t in range(BATCH):
        last = nc.vector.tensor_scalar(onehot[:, j, t, :], (iota or m.iota_p)[:], keys[:, bass.ds(b * BATCH + t, 1)],
                                       None, ALU.is_equal)
    return last


def add_to_nodes(nc, dve, o, m, acc, sums, blocks):
    w = acc.shape[2]
    for q in range(PPB):
        o.wait()
        at = acc[:, bass.ds(blocks[q], 1), :].rearrange("p a f -> p (a f)")
        ins = nc.vector.tensor_tensor(at, at, sums[:, q, 0:w], ALU.add)
        if q < PPB - 1:
            o.mark(ins)
    return ins



def stage_constants(nc, m, a):
    ctx, (made, loaded, ordered) = stage(nc, ["const_made", "x_loaded", "const_order"])
    with ctx, nc.Block() as block:
        @block.sync
        def _(sp):
            sp.wait_ge(ordered, 1)
            full = NB - 1
            sp.dma_start(m.X[:, 0:full, :], a["x"][0:full * P, :].rearrange("(b p) f -> p b f", p=P)).then_inc(loaded, 16)
            sp.dma_start(m.X[0:N - full * P, full, :], a["x"][full * P:N, :]).then_inc(loaded, 16)
            sp.dma_start(m.src[:], a["src"]).then_inc(loaded, 16)
            sp.dma_start(m.dst[:], a["dst"]).then_inc(loaded, 16)
            sp.wait_ge(loaded, 64)

        @block.gpsimd
        def _(pool):
            nc.gpsimd.iota(m.iota_p[:], pattern=[[1, P]], base=0, channel_multiplier=0,
                           allow_small_or_imprecise_dtypes=True).then_inc(made, 1)
            nc.gpsimd.iota(m.iota_b[:], pattern=[[1, P]], base=0, channel_multiplier=0,
                           allow_small_or_imprecise_dtypes=True).then_inc(made, 1)
            nc.gpsimd.iota(m.iota_col[:], pattern=[[0, 1]], base=0, channel_multiplier=1,
                           allow_small_or_imprecise_dtypes=True).then_inc(made, 1)
            nc.gpsimd.memset(m.ident[:], 0.0).then_inc(made, 1)
            nc.gpsimd.memset(m.ones[:], 1.0).then_inc(made, 1)
            nc.gpsimd.memset(m.before[:], 1.0).then_inc(made, 1)
            nc.gpsimd.memset(m.valid[:], 1.0).then_inc(made, 1)
            nc.gpsimd.iota(m.numbers[:], pattern=[[1, NB + 1]], base=0, channel_multiplier=0,
                           allow_small_or_imprecise_dtypes=True).then_inc(made, 1)
            nc.gpsimd.iota(m.pair_no[:], pattern=[[1, QR]], base=0, channel_multiplier=QR,
                           allow_small_or_imprecise_dtypes=True).then_inc(made, 1)
            nc.gpsimd.iota(m.sentinel_slot[:], pattern=[[1, EC]], base=T * P + 1, channel_multiplier=0,
                           allow_small_or_imprecise_dtypes=True).then_inc(made, 1)
            pool.wait_ge(made, 10)
            nc.gpsimd.affine_select(out=m.ident[:], in_=m.ident[:], compare_op=ALU.not_equal, fill=1.0, base=0,
                                    pattern=[[-1, P]], channel_multiplier=1).then_inc(made, 1)
            nc.gpsimd.affine_select(out=m.before[:], in_=m.before[:], compare_op=ALU.is_gt, fill=0.0, base=0,
                                    pattern=[[1, P]], channel_multiplier=-1).then_inc(made, 1)
            nc.gpsimd.affine_select(out=m.valid[:], in_=m.valid[:], compare_op=ALU.is_gt, fill=0.0,
                                    base=N - (NB - 1) * P, pattern=[[0, P]], channel_multiplier=-1).then_inc(made, 1)

        @block.vector
        def _(dve):
            nc.vector.memset(m.X[:], 0.0).then_inc(ordered, 1)
            dve.wait_ge(made, 13)
            nc.vector.tensor_copy(m.ident_b[:], m.ident[:])


def place(nc, m, ctx, block, name, key, other, packed, block_table):
    order, counted, summed, tabled, flat, gate = (ctx.sem(f"{name}_{x}") for x in (
        "order", "counted", "summed", "tabled", "flat", "gate"))

    def sb(n, s, d):
        return ctx.enter_context(nc.sbuf_tensor(f"{name}_{n}", s, d))
    blk = sb("blk", [P, EC], bf16)
    tmp = sb("tmp", [P, EC], i32)
    hit = sb("hit", [P, EC], bf16)
    high, low = sb("high", [P, EC], i32), sb("low", [P, EC], i32)
    rank = sb("rank", [P, EC], fp32)
    slot = sb("slot", [P, EC], fp32)
    cnt = sb("cnt", [P, NB], fp32)
    tot = sb("tot", [P, NB], fp32)
    pairs_i = sb("pairs_i", [P, NB], i32)
    pairs = sb("pairs", [P, NB], fp32)
    upto = sb("upto", [P, NB], fp32)
    off = sb("off", [P, NB], fp32)
    past = sb("past", [P, QR, NB], fp32)
    pair_blk = sb("pair_blk", [P, QR], fp32)
    pair_blk_i = sb("pair_blk_i", [P, QR], i32)
    psum = ctx.enter_context(nc.psum_tensor(f"{name}_ps", [P, 2, NB], fp32))
    flat_dram = nc.dram_tensor(f"{name}_flat", [P * QR], i32).ap()

    @block.scalar
    def _(act):
        act.wait_ge(tabled, 1)
        act.dma_start(flat_dram.rearrange("(p q) -> p q", q=QR), pair_blk_i[:]).then_inc(flat, 16)
        act.wait_ge(flat, 16)
        act.dma_start(block_table[:], flat_dram.rearrange("(a n) -> a n", a=1)).then_inc(flat, 16)
        act.wait_ge(flat, 32)

    @block.tensor
    def _(pe):
        pe.wait_ge(counted, 1)
        nc.tensor.matmul(psum[:, 0, :], m.before[:], cnt[:], start=True, stop=True)
        nc.tensor.matmul(psum[:, 1, :], m.ones[:], cnt[:], start=True, stop=True).then_inc(summed, 1)

    @block.vector
    def _(dve):
        o = Order(dve, order)
        o.mark(nc.vector.tensor_copy(slot[:], m.sentinel_slot[:]))
        o.mark(nc.vector.tensor_copy(packed[:, :, 0].bitcast(i32), other[:]))
        o.then(nc.vector.tensor_single_scalar(tmp[:], key[:], 7, ALU.logical_shift_right))
        o.then(nc.vector.tensor_copy(blk[:], tmp[:]))
        o.then(nc.vector.tensor_single_scalar(tmp[:], key[:], P - 1, ALU.bitwise_and))
        o.then(nc.vector.tensor_copy(packed[:, :, 1], tmp[:]))
        start = o.n
        with dve.Fori(0, NB // STEP) as k:
            s = Order(dve, order, STEP, k, start)
            for i in range(STEP):
                b = k * STEP + i
                s.then(nc.vector.tensor_scalar(hit[:], blk[:], m.numbers[:, bass.ds(b, 1)], 0.0, ALU.is_equal,
                                               ALU.add, accum_out=cnt[:, bass.ds(b, 1)]))
        o.n = start + NB
        dve.wait_ge(order, o.n)
        dve.sem_inc(counted, 1)
        dve.wait_ge(summed, 1)
        o.then(nc.vector.tensor_scalar(tot[:], psum[:, 1, :], float(PAIR - 1), None, ALU.add))
        o.then(nc.vector.tensor_copy(pairs_i[:], tot[:]))
        o.then(nc.vector.tensor_single_scalar(pairs_i[:], pairs_i[:], 8, ALU.logical_shift_right))
        o.then(nc.vector.tensor_copy(pairs[:], pairs_i[:]))
        o.then(nc.vector.tensor_tensor_scan(upto[:], pairs[:], pairs[:], 0.0, ALU.add, ALU.bypass))
        o.then(nc.vector.tensor_tensor(off[:], upto[:], pairs[:], ALU.subtract))
        o.then(nc.vector.scalar_tensor_tensor(out=off[:], in0=off[:], scalar=float(PAIR), in1=psum[:, 0, :],
                                              op0=ALU.mult, op1=ALU.add))
        o.then(nc.vector.tensor_tensor(past[:], b3(m.pair_no[:], NB), b2(upto[:], QR), ALU.is_ge))
        o.then(nc.vector.tensor_reduce(pair_blk[:], past[:], AX.X, ALU.add))
        o.then(nc.vector.tensor_scalar(pair_blk[:], pair_blk[:], float(NB - 1), None, ALU.min))
        nc.vector.tensor_copy(pair_blk_i[:], pair_blk[:]).then_inc(tabled, 1)
        start = o.n
        with dve.Fori(0, NB // STEP) as k:
            s = Order(dve, order, 3 * STEP, k, start)
            for i in range(STEP):
                b = k * STEP + i
                s.then(nc.vector.tensor_scalar(hit[:], blk[:], m.numbers[:, bass.ds(b, 1)], None, ALU.is_equal))
                s.then(nc.vector.tensor_tensor_scan(rank[:], hit[:], hit[:], off[:, bass.ds(b, 1)], ALU.add, ALU.bypass))
                dve.sem_inc(gate, 1)
                s.then(nc.vector.copy_predicated(slot[:], hit[:].bitcast(mybir.dt.int16), rank[:]))
        o.n = start + 3 * NB
        o.wait()
        o.then(nc.vector.tensor_scalar(tmp[:], slot[:], -1.0, None, ALU.add))
        o.then(nc.vector.tensor_single_scalar(high[:], tmp[:], 7, ALU.logical_shift_right))
        o.then(nc.vector.tensor_copy(rank[:], high[:]))
        o.then(nc.vector.tensor_single_scalar(low[:], tmp[:], P - 1, ALU.bitwise_and))
        o.then(nc.vector.tensor_copy(slot[:], low[:]))
        o.then(nc.vector.scalar_tensor_tensor(out=packed[:, :, 2].bitcast(i32), in0=slot[:], scalar=float(TP), in1=rank[:],
                                              op0=ALU.mult, op1=ALU.add))


def reorder(nc, ctx, block, name, packed, rows, features=None):
    w = rows.shape[2]
    now = ctx.enter_context(nc.sbuf_tensor(f"{name}_now", [P, 2, BATCH, w + 1], fp32))
    filled = [ctx.sem(f"{name}_filled{j}") for j in range(2)]
    written = [ctx.sem(f"{name}_written{j}") for j in range(2)]
    gate = ctx.sem(f"{name}_gate")
    steps = EC // (2 * BATCH)
    parts = 1 if features is None else 2

    @block.sync
    def _(sp):
        def fill(j, k):
            at = bass.ds(k * 2 * BATCH + j * BATCH, BATCH)
            sp.dma_start(now[:, j, :, w - 2:w + 1], packed[:, at, :]).then_inc(filled[j], 16)
            if features is not None:
                sp.dma_start(now[:, j, :, 0:EF], features[:, at, :]).then_inc(filled[j], 16)
        for j in range(2):
            fill(j, 0)
        with sp.Fori(1, steps) as k:
            for j in range(2):
                sp.wait_ge(written[j], k * (16 * BATCH))
                fill(j, k)

    @block.gpsimd
    def _(pool):
        with pool.Fori(0, steps) as k:
            for j in range(2):
                pool.wait_ge(filled[j], k * (16 * parts) + 16 * parts)
                pool.sem_inc(gate, 1)
                for c in range(BATCH):
                    nc.gpsimd.indirect_dma_start(
                        rows.rearrange("p t w -> (p t) w"),
                        bass.IndirectOffsetOnAxis(now[:, j, c, w:w + 1].bitcast(i32), 0),
                        now[:, j, c, 0:w], None).then_inc(written[j], 16)
        for j in range(2):
            pool.wait_ge(written[j], steps * 16 * BATCH)


def weight_loads(m, a):
    loads = []
    for i, n in enumerate(("int", "upd")):
        W, cols = a[f"W_{n}"], slice(i * F, (i + 1) * F)
        loads.append((m.w_src[:, cols], W[0:F, :]))
        loads.append((m.w_dst[0:F, cols], W[F:2 * F, :]))
        loads.append((m.w_dst[F:F + 1, cols], a[f"b_{n}"].unsqueeze(0)))
        loads += [(m.w_edge[q * ROW:q * ROW + EF, q, cols], W[2 * F:, :]) for q in range(GROUP)]
        loads.append((m.gain[:, cols], a[f"g_{n}"].partition_broadcast(P)))
        loads.append((m.shift[:, cols], a[f"be_{n}"].partition_broadcast(P)))
    loads += [(m.w_edge3[q * ROW:q * ROW + EF, q, :], a["W1"][F:, :]) for q in range(GROUP)]
    for t, W, b in ((m.w_h3, a["W1"][0:F, :], a["b1"]), (m.w_out3, a["W2"], a["b2"])):
        loads += [(t[0:F, :], W), (t[F:F + 1, :], b.unsqueeze(0))]
    for l in range(LAYERS):
        for cols, n in ((slice(0, F), "nb"), (slice(F, 2 * F), "self")):
            loads += [(m.w_att1[0:F, l, cols], a[f"{n}_W"][l]), (m.w_att1[F:F + 1, l, cols], a[f"{n}_b"][l].unsqueeze(0))]
            loads.append((m.w_att2[cols, l, cols], a["att1_W"][l, cols, :]))
        loads.append((m.b_att[:, l, :], a["att1_b"][l].partition_broadcast(P)))
        loads.append((m.att2[:, l, :], a["att2_W"][l, :, 0].partition_broadcast(P)))
        loads.append((m.att2_b[:, l:l + 1], a["att2_b"][l].partition_broadcast(P)))
    loads += [(t[:], a[n].partition_broadcast(P)) for t, n in
              ((m.g_bn, "g_bn"), (m.be_bn, "be_bn"), (m.gamma3, "gamma"), (m.beta3, "beta"))]
    loads.append((m.w_r[F:F + 1, :], a["b_l1"].unsqueeze(0)))
    return loads + [(m.w_l[:], a["w_l"].rearrange("o i -> i o")), (m.w_r[0:F, :], a["w_r"].rearrange("o i -> i o"))]


def fill(nc, m, a, ctx, block):
    COLS = TP // 16
    made, order, cleared, loaded = (ctx.sem(n) for n in ("fill_made", "fill_order", "fill_cleared", "weights_loaded"))
    empty = ctx.enter_context(nc.sbuf_tensor("empty", [P, COLS, ROW], fp32))
    empty2 = ctx.enter_context(nc.sbuf_tensor("empty2", [P, COLS, 2], fp32))

    @block.gpsimd
    def _(pool):
        nc.gpsimd.memset(m.w_edge[:], 0.0).then_inc(made, 1)
        nc.gpsimd.memset(m.w_edge3[:], 0.0).then_inc(made, 1)
        nc.gpsimd.memset(m.w_att2[:], 0.0).then_inc(made, 1)
        nc.gpsimd.memset(empty[:], 0.0).then_inc(order, 1)
        pool.wait_ge(order, 1)
        nc.gpsimd.memset(empty[:, :, EF:EF + 1].bitcast(i32), N).then_inc(made, 1)
        nc.gpsimd.memset(empty[:, :, EF + 1:ROW], -1.0).then_inc(made, 1)
        nc.gpsimd.memset(empty2[:, :, 0:1].bitcast(i32), N).then_inc(made, 1)
        nc.gpsimd.memset(empty2[:, :, 1:2], -1.0).then_inc(made, 1)

    @block.sync
    def _(sp):
        loads = weight_loads(m, a)
        sp.wait_ge(made, 3)
        for to, of in loads:
            sp.dma_start(to, of, allow_slow_non_contiguous=True).then_inc(loaded, 16)
        sp.wait_ge(made, 7)
        for c in range(TP // COLS):
            sp.dma_start(m.rows_dst[:, c * COLS:(c + 1) * COLS, :], empty[:]).then_inc(cleared, 16)
            sp.dma_start(m.rows_src[:, c * COLS:(c + 1) * COLS, :], empty2[:]).then_inc(cleared, 16)
        sp.wait_ge(loaded, 16 * len(loads))
        sp.wait_ge(cleared, 32 * (TP // COLS))


def stage_place(nc, m, a):
    with Stage(nc) as ctx, nc.Block() as block:
        fill(nc, m, a, ctx, block)
        place(nc, m, ctx, block, "dst", m.dst, m.src, m.packed_dst, m.table_dst)


def stage_reorder_dst(nc, m, a):
    with Stage(nc) as ctx, nc.Block() as block:
        reorder(nc, ctx, block, "to_dst", m.packed_dst, m.rows_dst, a["e"].rearrange("(p c) f -> p c f", c=EC))
        place(nc, m, ctx, block, "src", m.src, m.dst, m.packed_src, m.table_src)


class Keys:

    def __init__(self, nc, name, rows, index, keys):
        self.nc, self.index, self.keys = nc, index, keys
        self.ctx = Stage(nc)
        self.came = self.ctx.sem(f"{name}_came")
        self.pairs = self.ctx.enter_context(nc.sbuf_tensor(f"{name}_pairs", [P, T, 2], fp32))
        self.rows = rows

    def start(self):
        with self.nc.Block() as block:
            @block.sync
            def _(sp):
                w = self.rows.shape[2]
                sp.dma_start(self.pairs[:], self.rows[:, 0:T, w - 2:w]).then_inc(self.came, 16)

    def finish(self):
        nc = self.nc
        with self.ctx, nc.Block() as block:
            @block.vector
            def _(dve):
                nc.vector.memset(self.keys[:, T:TK], -1.0)
                nc.vector.memset(self.index[:, T:T + 2 * BATCH], 0)
                dve.wait_ge(self.came, 16)
                nc.vector.tensor_copy(self.index[:, 0:T], self.pairs[:, :, 0].bitcast(i32))
                nc.vector.tensor_copy(self.keys[:, 0:T], self.pairs[:, :, 1])





def normalize(nc, dve, o, x, out, stat, std_sem, var_sem):
    mean, var = stat[:, 0, :], stat[:, 1, :]
    o.wait()
    o.then(nc.vector.tensor_reduce(mean, x, AX.X, ALU.add))
    o.then(nc.vector.tensor_scalar(mean, mean, 1.0 / F, None, ALU.mult))
    o.then(nc.vector.tensor_tensor(out[0], x, b3(mean, F), ALU.subtract))
    o.then(nc.vector.tensor_tensor(out[1], out[0], out[0], ALU.mult))
    o.then(nc.vector.tensor_reduce(var, out[1], AX.X, ALU.add))
    nc.vector.tensor_scalar(var, var, 1.0 / F, EPS, ALU.mult, ALU.add).then_inc(var_sem, 1)
    dve.wait_ge(std_sem, 1)
    o.then(nc.vector.reciprocal(mean, var))
    o.then(nc.vector.tensor_tensor(out[0], out[0], b3(mean, F), ALU.mult))


def root(nc, act, stat, var_sem, std_sem):
    act.wait_ge(var_sem, 1)
    nc.scalar.activation(stat[:, 1, :], stat[:, 1, :], ACT.Sqrt).then_inc(std_sem, 1)


def stage_norm(nc, m, name, x, h, table=None):
    ctx, (order, var_sem, std_sem, ready, stored) = stage(nc, [f"{name}_{s}" for s in (
        "order", "var", "std", "ready", "stored")])
    with ctx:
        stat = ctx.enter_context(nc.sbuf_tensor(f"{name}_stat", [P, 2, NB], fp32))
        square = ctx.enter_context(nc.sbuf_tensor(f"{name}_sq", [P, NB, F], fp32))
        with nc.Block() as block:
            @block.vector
            def _(dve):
                o = Order(dve, order)
                o.mark(nc.vector.memset(stat[:], 0.0))
                normalize(nc, dve, o, x, (h, square[:]), stat, std_sem, var_sem)
                nc.vector.tensor_scalar(h, h, 0.0, None, ALU.max).then_inc(ready, 1)

            @block.scalar
            def _(act):
                root(nc, act, stat, var_sem, std_sem)

            @block.sync
            def _(sp):
                if table is not None:
                    sp.wait_ge(ready, 1)
                    sp.dma_start(table.rearrange("(b p) f -> p b f", p=P), h).then_inc(stored, 16)
                    sp.wait_ge(stored, 16)


def stage_turn(nc, m, name, x, turned, w=F):
    ctx, (done, taken) = stage(nc, [f"{name}_{s}" for s in ("done", "taken")])
    with ctx:
        ps = [ctx.enter_context(nc.psum_tensor(f"{name}_ps{j}", [P, 8 * P], fp32)) for j in range(2)]
        with nc.Block() as block:
            @block.tensor
            def _(pe):
                for k in range(NB // STEP):
                    if k >= 2:
                        pe.wait_ge(taken, k)
                    for i in range(STEP):
                        src = x[:, k * STEP + i, :]
                        last = nc.tensor.transpose(ps[k % 2][0:w, i * P:(i + 1) * P], src, m.ident[:])
                    last.then_inc(done, 1)

            @block.vector
            def _(dve):
                if w == F:
                    nc.vector.memset(turned[F:F + 1, :], 1.0).then_inc(taken, 1)
                else:
                    dve.sem_inc(taken, 1)
                for k in range(NB // STEP):
                    dve.wait_ge(done, k + 1)
                    nc.vector.tensor_copy(turned[0:w, bass.ds(k * STEP * P, STEP * P)],
                                          ps[k % 2][0:w, 0:STEP * P]).then_inc(taken, 1)


def stage_product(nc, m, name, terms, out, width, plus=None, table=None):
    ctx, (done, taken, stored) = stage(nc, [f"{name}_{s}" for s in ("done", "taken", "stored")])
    with ctx:
        ps = [ctx.enter_context(nc.psum_tensor(f"{name}_ps{j}", [P, 8, P], fp32)) for j in range(2)]
        with nc.Block() as block:
            @block.tensor
            def _(pe):
                for k in range(NB // STEP):
                    if k >= 2:
                        pe.wait_ge(taken, k - 1)
                    for i in range(STEP):
                        for n, (turned, w) in enumerate(terms):
                            last = nc.tensor.matmul(ps[k % 2][:, i, 0:width], turned[0:w.shape[0], bass.ds((k * STEP + i) * P, P)], w,
                                                    start=n == 0, stop=n == len(terms) - 1)
                    last.then_inc(done, 1)

            @block.vector
            def _(dve):
                for k in range(NB // STEP):
                    dve.wait_ge(done, k + 1)
                    at = bass.ds(k * STEP, STEP)
                    if plus is None:
                        nc.vector.tensor_copy(out[:, at, :], ps[k % 2][:, 0:STEP, 0:width]).then_inc(taken, 1)
                    else:
                        nc.vector.tensor_tensor(out[:, at, :], ps[k % 2][:, 0:STEP, 0:width], plus[:, at, :], ALU.add).then_inc(taken, 1)

            @block.sync
            def _(sp):
                if table is not None:
                    sp.wait_ge(taken, NB // STEP)
                    sp.dma_start(table.rearrange("(b p) f -> p b f", p=P), out).then_inc(stored, 16)
                    sp.wait_ge(stored, 16)


def stage_attention(nc, m, l, turned, row_part3, col_part, table):
    ctx, (inner, relued, outer, taken, stored, order) = stage(nc, [f"att{l}_{s}" for s in (
        "inner", "relued", "outer", "taken", "stored", "order")])
    HALF = STEP * P // 2
    ROUNDS = NB // STEP
    with ctx:
        hidden_ps = [ctx.enter_context(nc.psum_tensor(f"att{l}_hid{j}", [P, 2, 512], fp32)) for j in range(2)]
        out_ps = [ctx.enter_context(nc.psum_tensor(f"att{l}_out{j}", [P, 8, 2 * F], fp32)) for j in range(2)]
        hidden = ctx.enter_context(nc.sbuf_tensor(f"att{l}_hidden", [P, 2, STEP * P], fp32))
        row_part = ctx.enter_context(nc.sbuf_tensor(f"att{l}_row", [P, STEP, F], fp32))
        with nc.Block() as block:
            @block.tensor
            def _(pe):
                def first(k):
                    if k >= 2:
                        pe.wait_ge(relued, k - 1)
                    for h in range(2):
                        last = nc.tensor.matmul(hidden_ps[k % 2][:, h, 0:HALF], m.w_att1[:, l, :],
                                                turned[:, bass.ds(k * STEP * P + h * HALF, HALF)], start=True, stop=True)
                    last.then_inc(inner, 1)
                first(0)
                for k in range(ROUNDS):
                    if k < ROUNDS - 1:
                        first(k + 1)
                    pe.wait_ge(relued, k + 1)
                    if k >= 2:
                        pe.wait_ge(taken, k - 1)
                    for i in range(STEP):
                        last = nc.tensor.matmul(out_ps[k % 2][:, i, :], hidden[:, k % 2, i * P:(i + 1) * P], m.w_att2[:, l, :],
                                                start=True, stop=True)
                    last.then_inc(outer, 1)

            @block.vector
            def _(dve):
                o = Order(dve, order)

                def relu(k):
                    dve.wait_ge(inner, k + 1)
                    nc.vector.tensor_scalar(hidden[:, k % 2, :].rearrange("p (h c) -> p h c", h=2),
                                            hidden_ps[k % 2][:, :, 0:HALF], 0.0, None, ALU.max).then_inc(relued, 1)
                relu(0)
                for k in range(ROUNDS):
                    if k < ROUNDS - 1:
                        relu(k + 1)
                    at = slice(k * STEP, (k + 1) * STEP)
                    dve.wait_ge(outer, k + 1)
                    o.mark(nc.vector.tensor_tensor(row_part[:], out_ps[k % 2][:, 0:STEP, 0:F], b2(m.b_att[:, l, :], STEP), ALU.add))
                    nc.vector.tensor_copy(col_part[:, at, :], out_ps[k % 2][:, 0:STEP, F:2 * F]).then_inc(taken, 1)
                    o.wait()
                    o.then(split3(nc, o, row_part[:], [row_part3[:, at, i, :] for i in range(3)]))

            @block.sync
            def _(sp):
                rows = table.rearrange("(b p) f -> p b f", p=P)
                sp.dma_start(rows[:, :, F:2 * F], m.H[:]).then_inc(stored, 16)
                for k in range(ROUNDS):
                    at = slice(k * STEP, (k + 1) * STEP)
                    sp.wait_ge(taken, k + 1)
                    sp.dma_start(rows[:, at, 0:F], col_part[:, at, :]).then_inc(stored, 16)
                sp.wait_ge(stored, 16 * (ROUNDS + 1))


def stage_gate_norm(nc, m, sum_acc, square_acc, scale, shift):
    ctx, (order, summed, var_sem, std_sem) = stage(nc, ["gn_order", "gn_summed", "gn_var", "gn_std"])
    with ctx:
        ps = ctx.enter_context(nc.psum_tensor("gn_ps", [P, 2, 512], fp32))
        mu = ctx.enter_context(nc.sbuf_tensor("gn_mu", [P, 2 * F], fp32))
        var = ctx.enter_context(nc.sbuf_tensor("gn_var", [P, 2 * F], fp32))
        with nc.Block() as block:
            @block.tensor
            def _(pe):
                for i, acc in enumerate((sum_acc, square_acc)):
                    for c in range(BATCH):
                        last = nc.tensor.matmul(ps[:, i, 0:2 * F], m.ones[:], acc[:, c, :], start=c == 0, stop=c == BATCH - 1)
                last.then_inc(summed, 1)

            @block.vector
            def _(dve):
                o = Order(dve, order)
                dve.wait_ge(summed, 1)
                o.then(nc.vector.tensor_scalar(mu[:], ps[:, 0, 0:2 * F], 1.0 / E, None, ALU.mult))
                o.then(nc.vector.tensor_tensor(shift[:], mu[:], mu[:], ALU.mult))
                o.then(nc.vector.scalar_tensor_tensor(out=var[:], in0=ps[:, 1, 0:2 * F], scalar=1.0 / E, in1=shift[:],
                                                      op0=ALU.mult, op1=ALU.subtract))
                nc.vector.tensor_scalar(var[:], var[:], 0.0, EPS, ALU.max, ALU.add).then_inc(var_sem, 1)
                dve.wait_ge(std_sem, 1)
                o.then(nc.vector.reciprocal(scale[:], var[:]))
                o.then(nc.vector.tensor_tensor(scale[:], scale[:], m.gain[:], ALU.mult))
                o.then(nc.vector.tensor_tensor(mu[:], mu[:], scale[:], ALU.mult))
                o.then(nc.vector.tensor_tensor(shift[:], m.shift[:], mu[:], ALU.subtract))

            @block.scalar
            def _(act):
                act.wait_ge(var_sem, 1)
                nc.scalar.activation(var[:], var[:], ACT.Sqrt).then_inc(std_sem, 1)


def stage_conv_out(nc, m):
    ctx, (order, d_sem, mean_sem, var_sem, std_sem, neg_sem, log_sem, a_order) = stage(nc, ["co_" + s for s in (
        "order", "diff", "mean", "var", "std", "neg", "log", "act_order")])
    with ctx:
        ps = ctx.enter_context(nc.psum_tensor("co_ps", [P, 2, 512], fp32))
        d = ctx.enter_context(nc.sbuf_tensor("co_d", [P, NB, F], fp32))
        q = ctx.enter_context(nc.sbuf_tensor("co_q", [P, NB, F], fp32))
        mu = ctx.enter_context(nc.sbuf_tensor("co_mu", [P, F], fp32))
        std = ctx.enter_context(nc.sbuf_tensor("co_std", [P, F], fp32))
        with nc.Block() as block:
            @block.tensor
            def _(pe):
                for b in range(NB):
                    last = nc.tensor.matmul(ps[:, 0, 0:F], m.ones[:], m.acc[:, b, 0:F], start=b == 0, stop=b == NB - 1)
                last.then_inc(mean_sem, 1)
                pe.wait_ge(d_sem, 1)
                for b in range(NB):
                    last = nc.tensor.matmul(ps[:, 1, 0:F], (m.valid if b == NB - 1 else m.ones)[:], q[:, b, :],
                                            start=b == 0, stop=b == NB - 1)
                last.then_inc(var_sem, 1)

            @block.vector
            def _(dve):
                o = Order(dve, order)
                dve.wait_ge(mean_sem, 1)
                o.then(nc.vector.tensor_scalar(mu[:], ps[:, 0, 0:F], 1.0 / N, None, ALU.mult))
                o.then(nc.vector.tensor_tensor(d[:], m.acc[:, :, 0:F], b2(mu[:], NB), ALU.subtract))
                nc.vector.tensor_tensor(q[:], d[:], d[:], ALU.mult).then_inc(d_sem, 1)
                dve.wait_ge(var_sem, 1)
                nc.vector.tensor_scalar(std[:], ps[:, 1, 0:F], 1.0 / N, EPS, ALU.mult, ALU.add).then_inc(d_sem, 1)
                dve.wait_ge(std_sem, 1)
                o.then(nc.vector.reciprocal(mu[:], std[:]))
                o.then(nc.vector.tensor_tensor(mu[:], mu[:], m.g_bn[:], ALU.mult))
                o.then(nc.vector.tensor_tensor(d[:], d[:], b2(mu[:], NB), ALU.mult))
                o.then(nc.vector.tensor_tensor(d[:], d[:], b2(m.be_bn[:], NB), ALU.add))
                o.then(nc.vector.tensor_tensor(d[:], d[:], m.H[:], ALU.add))
                o.then(nc.vector.tensor_scalar(q[:], d[:], -1.0, None, ALU.mult))
                nc.vector.tensor_tensor(q[:], q[:], d[:], ALU.min).then_inc(neg_sem, 1)
                o.then(nc.vector.scalar_tensor_tensor(out=m.X[:], in0=d[:], scalar=0.0, in1=m.X[:], op0=ALU.max, op1=ALU.add))
                dve.wait_ge(log_sem, 1)
                o.then(nc.vector.tensor_tensor(m.X[:], m.X[:], q[:], ALU.add))

            @block.scalar
            def _(act):
                act.wait_ge(d_sem, 2)
                nc.scalar.activation(std[:], std[:], ACT.Sqrt).then_inc(std_sem, 1)
                act.wait_ge(neg_sem, 1)
                nc.scalar.activation(q[:], q[:], ACT.Exp).then_inc(a_order, 1)
                act.wait_ge(a_order, 1)
                nc.scalar.activation(q[:], q[:], ACT.Ln, bias=1.0).then_inc(log_sem, 1)


def stage_vector(nc, name, steps):
    ctx, (order,) = stage(nc, [f"{name}_order"])
    with ctx, nc.Block() as block:
        @block.vector
        def _(dve):
            steps(Order(dve, order))



def stage_conv_sums(nc, m, part_dst, table, kept, sum_acc, square_acc):
    W = 2 * F
    ctx = Stage(nc)
    with ctx:
        def sb(n, s, d=fp32):
            return ctx.enter_context(nc.sbuf_tensor(f"cs_{n}", s, d))

        def sem(n):
            return ctx.sem(f"cs_{n}")

        def sem2(n):
            return [sem(f"{n}{j}") for j in range(2)]
        e = sb("e", [P, 2, BATCH, ROW])
        rows = sb("rows", [P, 2, BATCH, W])
        index_now = sb("index", [P, 2, BATCH], i32)
        onehot = sb("onehot", [P, 2, BATCH, P])
        turned = sb("turned", [P, 2, BATCH, P])
        e_turned = sb("e_turned", [GROUP * ROW, 2, len(GROUPS), P])
        v = sb("v", [P, 2, BATCH, W])
        square = sb("square", [P, BATCH, W])
        turn_ps = ctx.enter_context(nc.psum_tensor("cs_turn_ps", [P, BATCH, P], fp32))
        e_ps = ctx.enter_context(nc.psum_tensor("cs_e_ps", [P, 4, P], fp32))
        v_ps = [ctx.enter_context(nc.psum_tensor(f"cs_v_ps{j}", [P, BATCH, W], fp32)) for j in range(2)]
        slot_free, indexed, arrived = sem2("free"), sem2("indexed"), sem2("arrived")
        gate, order = sem("gate"), sem("order")
        e_came, stored = sem2("e_came"), sem2("stored")
        hot, turn, turned_s, v_done, v_ready, squared = (sem(n) for n in ("hot", "turn_s", "turned_s", "v_done", "ready", "squared"))
        steps = ITERS

        with nc.Block() as block:
            @block.gpsimd
            def _(pool):
                fetch_rows(nc, pool, index_now, rows, table, indexed, gate, arrived)

            @block.sync
            def _(sp):
                def load(j, b):
                    sp.dma_start(e[:, j, :, :], m.rows_dst[:, bass.ds(b * BATCH, BATCH), :]).then_inc(e_came[j], 16)

                def store(j, b):
                    sp.wait_ge(v_ready, b + 1)
                    sp.dma_start(kept[:, bass.ds(b * BATCH, BATCH), :], v[:, j, :, :]).then_inc(stored[j], 16)
                for j in range(2):
                    load(j, j)
                with sp.Fori(0, steps - 1) as k:
                    for j in range(2):
                        sp.wait_ge(turn, k * 2 + j + 1)
                        load(j, k * 2 + 2 + j)
                        store(j, k * 2 + j)
                sp.wait_ge(turn, steps * 2 - 1)
                load(0, steps * 2)
                for j in range(2):
                    store(j, steps * 2 - 2 + j)
                for j in range(2):
                    sp.wait_ge(stored[j], 16 * steps)

            @block.tensor
            def _(pe):
                def values(b, j, n):
                    blocks = load_pair_blocks(nc, pe, m, b)
                    pe.wait_ge(hot, b + 1)
                    pe.wait_ge(e_came[j], n)
                    pe.sem_inc(gate, 1)
                    for t in range(BATCH):
                        nc.tensor.transpose(turn_ps[:, t, :], onehot[:, j, t, :], m.ident[:])
                    for g, tiles in enumerate(GROUPS):
                        last = nc.tensor.transpose(e_ps[0:len(tiles) * ROW, g, :],
                                                   e[:, j, tiles[0]:tiles[-1] + 1, :].rearrange("p t w -> p (t w)"), m.ident[:])
                    last.then_inc(turn, 1)
                    pe.wait_ge(turned_s, b + 1)
                    pe.sem_inc(gate, 1)
                    for t in range(BATCH):
                        at = part_dst[:, bass.ds(blocks[t // 2], 1), :].rearrange("p a f -> p (a f)")
                        nc.tensor.matmul(v_ps[j][:, t, :], turned[:, j, t, :], at, start=True, stop=False)
                        r = len(GROUPS[t // GROUP]) * ROW
                        last = nc.tensor.matmul(v_ps[j][:, t, :], e_turned[0:r, j, t // GROUP, :],
                                                m.w_edge[0:r, t % GROUP, :], start=False, stop=True)
                    last.then_inc(v_done, 1)
                values(0, 0, 16)
                with pe.Fori(0, steps) as k:
                    for j in range(2):
                        values(k * 2 + j + 1, 1 - j, k * 16 + 16 * (j + 1))

            @block.scalar
            def _(act):
                def turn_out(b, j):
                    act.wait_ge(turn, b + 1)
                    act.sem_inc(gate, 1)
                    for h in range(2):
                        nc.scalar.copy(turned[:, j, 4 * h:4 * h + 4, :], turn_ps[:, 4 * h:4 * h + 4, :])
                    whole, rest = len(GROUPS) - 1, len(GROUPS[-1]) * ROW
                    nc.scalar.copy(e_turned[:, j, 0:whole, :], e_ps[0:GROUP * ROW, 0:whole, :])
                    nc.scalar.copy(e_turned[0:rest, j, whole, :], e_ps[0:rest, whole, :]).then_inc(turned_s, 1)
                indices = IndexStager(nc, act, m.index_src, index_now, slot_free, indexed, gate)
                indices.first()
                turn_out(0, 0)
                with act.Fori(0, steps) as k:
                    for j in range(2):
                        b = k * 2 + j
                        turn_out(b + 1, 1 - j)
                        indices.after(k, j)
                        act.wait_ge(v_ready, b + 1)
                        act.wait_ge(order, b + 1)
                        act.sem_inc(gate, 1)
                        nc.scalar.square(square[:], v[:, j, :, :]).then_inc(squared, 1)

            @block.vector
            def _(dve):
                nc.vector.memset(sum_acc[:], 0.0)
                nc.vector.memset(square_acc[:], 0.0).then_inc(order, 1)
                dve.wait_ge(order, 1)
                one_hots(nc, m, onehot, m.key_dst, 0, 0).then_inc(hot, 1)

                def step(k, first):
                    for j in range(2):
                        b = k * 2 + j
                        one_hots(nc, m, onehot, m.key_dst, b + 1, 1 - j).then_inc(hot, 1)
                        dve.wait_ge(v_done, b + 1)
                        dve.wait_ge(arrived[j], k * (16 * BATCH) + 16 * BATCH)
                        if not first:
                            dve.wait_ge(stored[j], k * 16)
                        dve.sem_inc(gate, 1)
                        nc.vector.tensor_tensor(v[:, j, :, :], v_ps[j][:], rows[:, j, :, :], ALU.add).then_inc(v_ready, 1)
                        dve.wait_ge(v_ready, b + 1)
                        dve.sem_inc(slot_free[j], 1)
                        nc.vector.tensor_tensor(sum_acc[:], sum_acc[:], v[:, j, :, :], ALU.add)
                        dve.wait_ge(squared, b + 1)
                        dve.sem_inc(gate, 1)
                        nc.vector.tensor_tensor(square_acc[:], square_acc[:], square[:], ALU.add).then_inc(order, 1)
                        dve.wait_ge(order, b + 2)
                step(0, True)
                with dve.Fori(1, steps) as k:
                    step(k, False)


def stage_conv_messages(nc, m, kept, scale, shift):
    W = 2 * F
    LOADS = 4
    batches = T // BATCH
    assert batches % LOADS == 0
    ctx = Stage(nc)
    with ctx:
        def sb(n, s, d=fp32):
            return ctx.enter_context(nc.sbuf_tensor(f"cm_{n}", s, d))

        def sem(n):
            return ctx.sem(f"cm_{n}")
        v = sb("v", [P, LOADS, BATCH, W])
        log = sb("log", [P, 2, BATCH, W])
        gate_v = sb("gate", [P, 2, BATCH, F])
        message = sb("message", [P, 2, BATCH, F + 1])
        onehot = sb("onehot", [P, 2, BATCH, P])
        sums = [ctx.enter_context(nc.psum_tensor(f"cm_sums_ps{j}", [P, PPB, P], fp32)) for j in range(2)]
        came = [sem(f"came{j}") for j in range(LOADS)]
        normed, logged, opened, gated, ready, summed = (sem(n) for n in ("normed", "logged", "opened", "gated", "ready", "summed"))
        gate, order, act_order = sem("gate_s"), sem("order"), sem("act_order")
        with nc.Block() as block:
            reorder(nc, ctx, block, "to_src", m.packed_src, m.rows_src)

            @block.scalar
            def _(act):
                def load(b, j):
                    act.dma_start(v[:, j, :, :], kept[:, bass.ds(b * BATCH, BATCH), :]).then_inc(came[j], 16)

                def soften(b, j):
                    h = j % 2
                    act.wait_ge(normed, b + 1)
                    act.sem_inc(gate, 1)
                    nc.scalar.activation(log[:, h, :, :], v[:, j, :, :], ACT.Abs).then_inc(act_order, 1)
                    act.wait_ge(act_order, b * 2 + 1)
                    act.sem_inc(gate, 1)
                    nc.scalar.activation(log[:, h, :, :], log[:, h, :, :], ACT.Exp, scale=-1.0).then_inc(act_order, 1)
                    act.wait_ge(act_order, b * 2 + 2)
                    act.sem_inc(gate, 1)
                    nc.scalar.activation(log[:, h, :, :], log[:, h, :, :], ACT.Ln, bias=1.0).then_inc(logged, 1)

                def open_gate(b, j):
                    act.wait_ge(opened, b + 1)
                    act.sem_inc(gate, 1)
                    nc.scalar.activation(gate_v[:, j % 2, :, :], gate_v[:, j % 2, :, :], ACT.Exp).then_inc(gated, 1)
                nc.scalar.preload_act_table_set("natural_log_exp_and_others")
                for j in range(LOADS):
                    load(j, j)
                soften(0, 0)
                open_gate(0, 0)
                soften(1, 1)
                with act.Fori(0, batches // LOADS - 1) as k:
                    for i in range(1, 1 + LOADS):
                        b, j = k * LOADS + i, i % LOADS
                        open_gate(b, j)
                        soften(b + 1, (j + 1) % LOADS)
                        act.wait_ge(ready, b)
                        load(b + LOADS - 1, (j - 1) % LOADS)
                for b in range(batches - LOADS + 1, batches):
                    open_gate(b, b % LOADS)
                    if b + 1 < batches:
                        soften(b + 1, (b + 1) % LOADS)

            @block.vector
            def _(dve):
                o = Order(dve, order)
                o.mark(nc.vector.memset(m.acc[:], 0.0))
                o.then(nc.vector.memset(message[:, :, :, F:F + 1], 1.0))

                def norm(b, j, n, s):
                    dve.wait_ge(came[j], n)
                    dve.sem_inc(gate, 1)
                    s.then(nc.vector.tensor_tensor(v[:, j, :, :], v[:, j, :, :], b2(scale[:], BATCH), ALU.mult))
                    nc.vector.tensor_tensor(v[:, j, :, :], v[:, j, :, :], b2(shift[:], BATCH), ALU.add).then_inc(normed, 1)

                def multiply(b, j, s, behind=None):
                    h = j % 2
                    dve.wait_ge(logged, b + 1)
                    dve.sem_inc(gate, 1)
                    nc.vector.scalar_tensor_tensor(out=gate_v[:, h, :, :], in0=v[:, j, :, 0:F], scalar=0.0,
                                                   in1=log[:, h, :, 0:F], op0=ALU.min, op1=ALU.subtract).then_inc(opened, 1)
                    s.mark(nc.vector.scalar_tensor_tensor(out=log[:, h, :, F:W], in0=v[:, j, :, F:W], scalar=0.0,
                                                          in1=log[:, h, :, F:W], op0=ALU.max, op1=ALU.add))
                    one_hots(nc, m, onehot, m.key_dst, b, h)
                    blocks = None if behind is None else load_pair_blocks(nc, dve, m, behind)
                    dve.wait_ge(gated, b + 1)
                    s.wait()
                    dve.sem_inc(gate, 1)
                    nc.vector.tensor_tensor(message[:, h, :, 0:F], gate_v[:, h, :, :], log[:, h, :, F:W],
                                            ALU.mult).then_inc(ready, 1)
                    return blocks

                def collect(b, j, s, blocks):
                    dve.wait_ge(summed, b + 1)
                    s.mark(add_to_nodes(nc, dve, s, m, m.acc[:], sums[j % 2], blocks))
                norm(0, 0, 16, o)
                norm(1, 1, 16, o)
                multiply(0, 0, o)
                start = o.n
                with dve.Fori(0, batches // LOADS - 1) as k:
                    s = Order(dve, order, LOADS * (2 + PPB), k, start)
                    for j in range(LOADS):
                        b = k * LOADS + j
                        norm(b + 2, (j + 2) % LOADS, k * 16 + 16 * ((j + 2) // LOADS + 1), s)
                        blocks = multiply(b + 1, (j + 1) % LOADS, s, behind=b)
                        collect(b, j, s, blocks)
                    assert s.n == s.last
                o.n = start + (batches // LOADS - 1) * LOADS * (2 + PPB)
                for b in range(batches - LOADS, batches):
                    if b + 2 < batches:
                        norm(b + 2, (b + 2) % LOADS, 16 * ((b + 2) // LOADS + 1), o)
                    if b + 1 < batches:
                        blocks = multiply(b + 1, (b + 1) % LOADS, o, behind=b)
                    else:
                        blocks = load_pair_blocks(nc, dve, m, b)
                    collect(b, b % LOADS, o, blocks)

            @block.tensor
            def _(pe):
                with pe.Fori(0, ITERS) as k:
                    for j in range(2):
                        b = k * 2 + j
                        pe.wait_ge(ready, b + 1)
                        pe.sem_inc(gate, 1)
                        for t in range(BATCH):
                            last = nc.tensor.matmul(sums[j][:, t // 2, 0:F + 1], onehot[:, j, t, :], message[:, j, t, :],
                                                    start=t % 2 == 0, stop=t % 2 == 1)
                        last.then_inc(summed, 1)


def stage_gather_sum(nc, m, name, index, keys, table, acc):
    ctx = Stage(nc)
    with ctx:
        def sem(n):
            return ctx.sem(f"{name}_{n}")

        def sem2(n):
            return [sem(f"{n}{j}") for j in range(2)]
        rows = ctx.enter_context(nc.sbuf_tensor(f"{name}_rows", [P, 2, BATCH, F], fp32))
        index_now = ctx.enter_context(nc.sbuf_tensor(f"{name}_index", [P, 2, BATCH], i32))
        onehot = ctx.enter_context(nc.sbuf_tensor(f"{name}_onehot", [P, 2, BATCH, P], fp32))
        sums = [ctx.enter_context(nc.psum_tensor(f"{name}_sums_ps{j}", [P, PPB, P], fp32)) for j in range(2)]
        slot_free, indexed, arrived, hot, summed = sem2("free"), sem2("indexed"), sem2("arrived"), sem2("hot"), sem2("summed")
        gate, order = sem("gate"), sem("order")
        with nc.Block() as block:
            @block.gpsimd
            def _(pool):
                fetch_rows(nc, pool, index_now, rows, table, indexed, gate, arrived)

            @block.scalar
            def _(act):
                indices = IndexStager(nc, act, index, index_now, slot_free, indexed, gate)
                indices.first()
                with act.Fori(0, ITERS) as k:
                    for j in range(2):
                        indices.after(k, j)

            @block.vector
            def _(dve):
                o = Order(dve, order)
                o.then(nc.vector.memset(acc, 0.0))
                with dve.Fori(0, ITERS) as k:
                    s = Order(dve, order, 2 * PPB, k, o.n)
                    for j in range(2):
                        one_hots(nc, m, onehot, keys, k * 2 + j, j).then_inc(hot[j], 1)
                        blocks = load_pair_blocks(nc, dve, m, k * 2 + j)
                        dve.wait_ge(summed[j], k + 1)
                        dve.sem_inc(slot_free[j], 1)
                        s.mark(add_to_nodes(nc, dve, s, m, acc, sums[j], blocks))
                    assert s.n == s.last

            @block.tensor
            def _(pe):
                with pe.Fori(0, ITERS) as k:
                    for j in range(2):
                        pe.wait_ge(order, k * (2 * PPB) + j * PPB + 1)
                        pe.wait_ge(hot[j], k + 1)
                        pe.wait_ge(arrived[j], k * (16 * BATCH) + 16 * BATCH)
                        pe.sem_inc(gate, 1)
                        for t in range(BATCH):
                            last = nc.tensor.matmul(sums[j][:, t // 2, 0:F], onehot[:, j, t, :], rows[:, j, t, :],
                                                    start=t % 2 == 0, stop=t % 2 == 1)
                        last.then_inc(summed[j], 1)


def split3(nc, o, x, parts):
    hi, mid, lo = parts
    o.then(nc.vector.tensor_copy(hi, x))
    o.then(nc.vector.tensor_tensor(x, x, hi, ALU.subtract))
    o.then(nc.vector.tensor_copy(mid, x))
    return nc.vector.tensor_tensor(lo, x, mid, ALU.subtract)


def stage_masks(nc, m, l, row_part3, table, x_dst, mask, rowsum):
    name = f"mask{l}"
    ctx = Stage(nc)
    with ctx:
        def sb(n, s, d=fp32):
            return ctx.enter_context(nc.sbuf_tensor(f"{name}_{n}", s, d))

        def sem(n):
            return ctx.sem(f"{name}_{n}")

        def sem2(n):
            return [sem(f"{n}{j}") for j in range(2)]
        rows = sb("rows", [P, 2, BATCH, 2 * F])
        index_now = sb("index", [P, 2, BATCH], i32)
        onehot = sb("onehot", [P, 2, BATCH, P], bf16)
        turned = sb("turned", [P, 2, BATCH, P], bf16)
        hidden = sb("hidden", [P, 2, BATCH, F])
        logit = sb("logit", [P, 2, BATCH])
        mask_now = sb("mask", [P, 2, BATCH])
        mask3 = sb("mask3", [P, 2, BATCH, 3], bf16)
        first = sb("first", [P, 1])
        turn_ps = ctx.enter_context(nc.psum_tensor(f"{name}_turn_ps", [P, BATCH, P], bf16))
        part_ps = [ctx.enter_context(nc.psum_tensor(f"{name}_part_ps{j}", [P, BATCH, F], fp32)) for j in range(2)]
        sums = [ctx.enter_context(nc.psum_tensor(f"{name}_sums_ps{j}", [P, PPB, P], fp32)) for j in range(2)]
        slot_free, indexed, arrived, stored = sem2("free"), sem2("indexed"), sem2("arrived"), sem2("stored")
        hot, turn, turned_s, part, logits, opened, masked, summed = (
            sem(n) for n in ("hot", "turn", "turned", "part", "logits", "opened", "masked", "summed"))
        gate, order = sem("gate"), sem("order")
        with nc.Block() as block:
            @block.gpsimd
            def _(pool):
                fetch_rows(nc, pool, index_now, rows, table, indexed, gate, arrived)

            @block.sync
            def _(sp):
                with sp.Fori(0, ITERS) as k:
                    for j in range(2):
                        sp.wait_ge(arrived[j], k * (16 * BATCH) + 16 * BATCH)
                        sp.dma_start(x_dst[:, bass.ds(k * 2 * BATCH + j * BATCH, BATCH), :],
                                     rows[:, j, :, F:2 * F]).then_inc(stored[j], 16)
                for j in range(2):
                    sp.wait_ge(stored[j], 16 * ITERS)

            @block.vector
            def _(dve):
                o = Order(dve, order)
                o.then(nc.vector.memset(rowsum, 0.0))
                one_hots(nc, m, onehot, m.key_src, 0, 0, iota=m.iota_b).then_inc(hot, 1)
                with dve.Fori(0, ITERS) as k:
                    s = Order(dve, order, 2 * (7 + PPB), k, o.n)
                    for j in range(2):
                        b = k * 2 + j
                        one_hots(nc, m, onehot, m.key_src, b + 1, 1 - j, iota=m.iota_b).then_inc(hot, 1)
                        dve.wait_ge(part, b + 1)
                        dve.wait_ge(arrived[j], k * (16 * BATCH) + 16 * BATCH)
                        dve.sem_inc(gate, 1)
                        s.then(nc.vector.tensor_tensor(hidden[:, j, :, :], part_ps[j][:], rows[:, j, :, 0:F], ALU.add))
                        dve.sem_inc(slot_free[j], 1)
                        s.then(nc.vector.scalar_tensor_tensor(out=hidden[:, j, :, :], in0=hidden[:, j, :, :], scalar=0.0,
                                                              in1=b2(m.att2[:, l, :], BATCH), op0=ALU.max, op1=ALU.mult))
                        nc.vector.tensor_reduce(logit[:, j, :], hidden[:, j, :, :], AX.X, ALU.add).then_inc(logits, 1)
                        blocks = load_pair_blocks(nc, dve, m, b)
                        dve.wait_ge(opened, b + 1)
                        dve.sem_inc(gate, 1)
                        s.then(nc.vector.tensor_scalar(mask_now[:, j, :], logit[:, j, :], ZETA - GAMMA, GAMMA, ALU.mult, ALU.add))
                        s.then(nc.vector.tensor_scalar(mask_now[:, j, :], mask_now[:, j, :], 0.0, 1.0, ALU.max, ALU.min))
                        nc.vector.tensor_copy(mask[:, bass.ds(b * BATCH, BATCH)], mask_now[:, j, :])
                        split3(nc, s, mask_now[:, j, :], [mask3[:, j, :, i] for i in range(3)]).then_inc(masked, 1)
                        dve.wait_ge(summed, b + 1)
                        s.mark(add_to_nodes(nc, dve, s, m, rowsum, sums[j], blocks))
                    assert s.n == s.last

            @block.scalar
            def _(act):
                def turn_out(b, j):
                    act.wait_ge(turn, b + 1)
                    act.sem_inc(gate, 1)
                    nc.scalar.copy(turned[:, j, :, :], turn_ps[:]).then_inc(turned_s, 1)
                nc.scalar.activation(first[:], m.att2_b[:, l:l + 1], ACT.Sigmoid)
                indices = IndexStager(nc, act, m.index_dst, index_now, slot_free, indexed, gate, stored)
                indices.first()
                turn_out(0, 0)
                with act.Fori(0, ITERS) as k:
                    for j in range(2):
                        b = k * 2 + j
                        turn_out(b + 1, 1 - j)
                        indices.after(k, j)
                        act.wait_ge(logits, b + 1)
                        act.sem_inc(gate, 1)
                        nc.scalar.activation(logit[:, j, :], logit[:, j, :], ACT.Sigmoid, bias=m.att2_b[:, l:l + 1]).then_inc(opened, 1)

            @block.tensor
            def _(pe):
                def spread(b, j):
                    blocks = load_pair_blocks(nc, pe, m, b)
                    pe.wait_ge(hot, b + 1)
                    pe.sem_inc(gate, 1)
                    for t in range(BATCH):
                        last = nc.tensor.transpose(turn_ps[:, t, :], onehot[:, j, t, :], m.ident_b[:])
                    last.then_inc(turn, 1)
                    pe.wait_ge(turned_s, b + 1)
                    pe.sem_inc(gate, 1)
                    for t in range(BATCH):
                        for i in range(3):
                            at = row_part3[:, bass.ds(blocks[t // 2], 1), i, :].rearrange("p a f -> p (a f)")
                            last = nc.tensor.matmul(part_ps[j][:, t, :], turned[:, j, t, :], at, start=i == 0, stop=i == 2)
                    last.then_inc(part, 1)
                spread(0, 0)
                with pe.Fori(0, ITERS) as k:
                    for j in range(2):
                        b = k * 2 + j
                        spread(b + 1, 1 - j)
                        pe.wait_ge(masked, b + 1)
                        pe.sem_inc(gate, 1)
                        for t in range(BATCH):
                            last = nc.tensor.matmul(sums[j][:, t // 2, 0:3], onehot[:, j, t, :], mask3[:, j, t, :],
                                                    start=t % 2 == 0, stop=t % 2 == 1)
                        last.then_inc(summed, 1)


def stage_halves(nc, m, lo_rows, hi):
    CHUNKS = T // P
    assert T % P == 0
    ctx, (order, parted, turned, out, stored) = stage(nc, ["half_" + n for n in ("order", "parted", "turned", "out", "stored")])
    with ctx:
        half = ctx.enter_context(nc.sbuf_tensor("half_i", [P, T], i32))
        lo = ctx.enter_context(nc.sbuf_tensor("half_lo", [P, T], bf16))
        lo_turned = ctx.enter_context(nc.sbuf_tensor("half_turned", [P, CHUNKS, P], bf16))
        ps = ctx.enter_context(nc.psum_tensor("half_ps", [P, 16, P], bf16))
        with nc.Block() as block:
            @block.vector
            def _(dve):
                o = Order(dve, order)
                o.then(nc.vector.tensor_single_scalar(half[:], m.index_dst[:, 0:T], P - 1, ALU.bitwise_and))
                o.then(nc.vector.tensor_copy(lo[:], half[:]))
                dve.sem_inc(parted, 1)
                o.then(nc.vector.tensor_single_scalar(half[:], m.index_dst[:, 0:T], 7, ALU.logical_shift_right))
                nc.vector.tensor_copy(hi[:], half[:])
                dve.wait_ge(turned, 1)
                nc.vector.tensor_copy(lo_turned[:], ps[:, 0:CHUNKS, :]).then_inc(out, 1)

            @block.tensor
            def _(pe):
                pe.wait_ge(parted, 1)
                for c in range(CHUNKS):
                    last = nc.tensor.transpose(ps[:, c, :], lo[:, c * P:(c + 1) * P], m.ident_b[:])
                last.then_inc(turned, 1)

            @block.sync
            def _(sp):
                sp.wait_ge(out, 1)
                sp.dma_start(lo_rows.rearrange("a (c t e) -> (a t) c e", t=P, e=P), lo_turned[:]).then_inc(stored, 16)
                sp.wait_ge(stored, 16)


def stage_hop(nc, m, name, x_dst, lo_rows, hi, inv3, mask, acc):
    ctx = Stage(nc)
    BATCHES = 2 * ITERS
    with ctx:
        def sb(n, s, d=fp32):
            return ctx.enter_context(nc.sbuf_tensor(f"{name}_{n}", s, d))

        def sem(n):
            return ctx.sem(f"{name}_{n}")

        def sem2(n):
            return [sem(f"{n}{j}") for j in range(2)]
        x = sb("x", [P, 2, BATCH, F])
        lo = sb("lo", [P, 2, BATCH * P], bf16)
        lo_hot = sb("lo_hot", [P, 2, BATCH * P], bf16)
        hi_hot = sb("hi_hot", [P, BATCH, NB])
        picked = sb("picked", [P, BATCH, NB])
        inv = sb("inv", [P, BATCH])
        weight = sb("weight", [P, 2, BATCH])
        scaled_x = sb("scaled_x", [P, 2, BATCH, F])
        sums_now = sb("sums_now", [P, 2, PPB, F])
        onehot = sb("onehot", [P, 2, BATCH, P])
        inv_ps = [ctx.enter_context(nc.psum_tensor(f"{name}_inv_ps{j}", [P, BATCH, F], fp32)) for j in range(2)]
        sums = [ctx.enter_context(nc.psum_tensor(f"{name}_sums_ps{j}", [P, PPB, P], fp32)) for j in range(2)]
        x_came, lo_came = sem2("x_came"), sem2("lo_came")
        lo_made, spread, weighted, scaled, summed, taken, added = (
            sem(n) for n in ("lo_made", "spread", "weighted", "scaled", "summed", "taken", "added"))
        gate, order, pool_order = sem("gate"), sem("order"), sem("pool_order")
        with nc.Block() as block:
            @block.sync
            def _(sp):
                def load(k, j):
                    sp.dma_start(x[:, j, :, :], x_dst[:, bass.ds(k * 2 * BATCH + j * BATCH, BATCH), :]).then_inc(x_came[j], 16)
                for j in range(2):
                    load(0, j)
                with sp.Fori(1, ITERS) as k:
                    for j in range(2):
                        sp.wait_ge(scaled, k * 2 + j - 1)
                        load(k, j)

            @block.scalar
            def _(act):
                def load(k, j):
                    at = lo_rows[:, bass.ds(k * (2 * BATCH * P) + j * BATCH * P, BATCH * P)]
                    act.dma_start(lo[:, j, :], at.to_broadcast([P, BATCH * P])).then_inc(lo_came[j], 16)

                def scale(b, j, k):
                    act.wait_ge(x_came[j], k * 16 + 16)
                    act.wait_ge(weighted, b + 1)
                    act.wait_ge(summed, b + 1)
                    act.sem_inc(gate, 1)
                    for t in range(BATCH):
                        last = nc.scalar.activation(scaled_x[:, j, t, :], x[:, j, t, :], ACT.Copy, scale=weight[:, j, t:t + 1])
                    last.then_inc(scaled, 1)

                def take(b, j):
                    act.wait_ge(summed, b + 3)
                    act.wait_ge(added, b + 1)
                    nc.scalar.copy(sums_now[:, j, :, :], sums[j][:, :, 0:F]).then_inc(taken, 1)
                act.sem_inc(taken, 2)
                for j in range(2):
                    load(0, j)
                act.wait_ge(lo_made, 1)
                load(1, 0)

                def step(b, j, k):
                    act.wait_ge(lo_made, b + 1)
                    load(k + 1, j)
                    scale(b - 1, 1 - j, k - 1 + j)
                step(1, 1, 0)
                with act.Fori(1, ITERS - 1) as k:
                    for j in range(2):
                        step(k * 2 + j, j, k)
                        take(k * 2 + j - 2, j)
                for b in range(BATCHES - 3, BATCHES):
                    scale(b, b % 2, b // 2)
                    take(b - 1, (b - 1) % 2)
                take(BATCHES - 1, 1)

            @block.tensor
            def _(pe):
                def spread_inv(b, j):
                    pe.wait_ge(lo_made, b + 1)
                    for t in range(BATCH):
                        for i in range(3):
                            last = nc.tensor.matmul(inv_ps[j][:, t, 0:NB], lo_hot[:, j, t * P:(t + 1) * P], inv3[:, i, :],
                                                    start=i == 0, stop=i == 2)
                    last.then_inc(spread, 1)

                def collect(b, j):
                    pe.wait_ge(scaled, b + 1)
                    pe.wait_ge(taken, b + 1)
                    for t in range(BATCH):
                        last = nc.tensor.matmul(sums[j][:, t // 2, 0:F], onehot[:, j, t, :], scaled_x[:, j, t, :],
                                                start=t % 2 == 0, stop=t % 2 == 1)
                    last.then_inc(summed, 1)
                pe.sem_inc(summed, 2)
                spread_inv(0, 0)
                spread_inv(1, 1)
                with pe.Fori(0, ITERS - 1) as k:
                    for j in range(2):
                        spread_inv(k * 2 + j + 2, j)
                        collect(k * 2 + j, j)
                for j in range(2):
                    collect(BATCHES - 2 + j, j)

            @block.gpsimd
            def _(pool):
                o = Order(pool, pool_order)
                pool.sem_inc(added, 2)
                o.mark(nc.gpsimd.memset(acc, 0.0))
                with pool.Fori(0, ITERS) as k:
                    s = Order(pool, pool_order, 2 * PPB, k, o.n)
                    for j in range(2):
                        b = k * 2 + j
                        blocks = load_pair_blocks(nc, pool, m, b)
                        pool.wait_ge(taken, b + 3)
                        for q in range(PPB):
                            s.wait()
                            at = acc[:, bass.ds(blocks[q], 1), :].rearrange("p a f -> p (a f)")
                            s.mark(nc.gpsimd.tensor_tensor(at, at, sums_now[:, j, q, :], ALU.add))
                        s.wait()
                        pool.sem_inc(added, 1)
                    assert s.n == s.last

            @block.vector
            def _(dve):
                def node_hots(b, j, k):
                    dve.wait_ge(lo_came[j], k * 16 + 16)
                    nc.vector.tensor_scalar(lo_hot[:, j, :], lo[:, j, :], m.iota_col[:], None, ALU.is_equal).then_inc(lo_made, 1)

                def hots(b, j, tiles):
                    for t in tiles:
                        nc.vector.tensor_scalar(onehot[:, j, t, :], m.iota_p[:], m.key_src[:, bass.ds(b * BATCH + t, 1)],
                                                None, ALU.is_equal)

                def step(b, j, k, s, more=True):
                    if more:
                        node_hots(b + 1, 1 - j, k + j)
                    s.then(nc.vector.tensor_tensor(hi_hot[:], b2(m.iota_p[:, 0:NB], BATCH),
                                                   b3(hi[:, bass.ds(b * BATCH, BATCH)], NB), ALU.is_equal))
                    dve.wait_ge(spread, b + 1)
                    dve.sem_inc(gate, 1)
                    s.mark(nc.vector.tensor_tensor(picked[:], inv_ps[j][:, :, 0:NB], hi_hot[:], ALU.mult))
                    dve.wait_ge(summed, b + 1)
                    dve.sem_inc(gate, 1)
                    hots(b, j, range(BATCH // 2))
                    s.wait()
                    s.mark(nc.vector.tensor_reduce(inv[:], picked[:], AX.X, ALU.add))
                    hots(b, j, range(BATCH // 2, BATCH))
                    s.wait()
                    dve.sem_inc(gate, 1)
                    nc.vector.tensor_tensor(weight[:, j, :], inv[:], mask[:, bass.ds(b * BATCH, BATCH)], ALU.mult).then_inc(weighted, 1)
                o = Order(dve, order)
                node_hots(0, 0, 0)
                PER = 3
                with dve.Fori(0, ITERS - 1) as k:
                    s = Order(dve, order, 2 * PER, k)
                    for j in range(2):
                        step(k * 2 + j, j, k, s)
                    assert s.n == s.last
                o.n = (ITERS - 1) * 2 * PER
                step(BATCHES - 2, 0, ITERS - 1, o)
                step(BATCHES - 1, 1, ITERS - 1, o, more=False)


def stage_edge_mlp(nc, m, table, acc):
    ctx = Stage(nc)
    with ctx:
        def sb(n, s, d=fp32):
            return ctx.enter_context(nc.sbuf_tensor(f"mlp_{n}", s, d))

        def sem(n):
            return ctx.sem(f"mlp_{n}")

        def sem2(n):
            return [sem(f"{n}{j}") for j in range(2)]
        e = sb("e", [P, 2, BATCH, ROW])
        rows = sb("rows", [P, 2, BATCH, F])
        index_now = sb("index", [P, 2, BATCH], i32)
        onehot = sb("onehot", [P, 2, BATCH, P])
        e_turned = sb("e_turned", [GROUP * ROW, 2, len(GROUPS), P])
        hidden = sb("hidden", [P, 2, BATCH, F])
        e_ps = [ctx.enter_context(nc.psum_tensor(f"mlp_e_ps{j}", [P, 4, P], fp32)) for j in range(2)]
        part_ps = [ctx.enter_context(nc.psum_tensor(f"mlp_part_ps{j}", [P, BATCH, F], fp32)) for j in range(2)]
        sums = [ctx.enter_context(nc.psum_tensor(f"mlp_sums_ps{j}", [P, PPB, P], fp32)) for j in range(2)]
        slot_free, indexed, arrived, e_came, turn, turned_s, part, ready, summed = (
            sem2(n) for n in ("free", "indexed", "arrived", "e_came", "turn", "turned", "part", "ready", "summed"))
        gate, order = sem("gate"), sem("order")
        with nc.Block() as block:
            @block.gpsimd
            def _(pool):
                fetch_rows(nc, pool, index_now, rows, table, indexed, gate, arrived)

            @block.sync
            def _(sp):
                for j in range(2):
                    sp.sem_inc(turn[j], 1)
                with sp.Fori(0, ITERS) as k:
                    for j in range(2):
                        sp.wait_ge(turn[j], k + 1)
                        sp.dma_start(e[:, j, :, :], m.rows_dst[:, bass.ds(k * 2 * BATCH + j * BATCH, BATCH), :]).then_inc(e_came[j], 16)

            @block.tensor
            def _(pe):
                def edge_part(k, j):
                    pe.wait_ge(e_came[j], k * 16 + 16)
                    pe.sem_inc(gate, 1)
                    for g, tiles in enumerate(GROUPS):
                        last = nc.tensor.transpose(e_ps[j][0:len(tiles) * ROW, g, :],
                                                   e[:, j, tiles[0]:tiles[-1] + 1, :].rearrange("p t w -> p (t w)"), m.ident[:])
                    last.then_inc(turn[j], 1)
                    pe.wait_ge(turned_s[j], k + 1)
                    pe.sem_inc(gate, 1)
                    for t in range(BATCH):
                        n = len(GROUPS[t // GROUP]) * ROW
                        last = nc.tensor.matmul(part_ps[j][:, t, :], e_turned[0:n, j, t // GROUP, :],
                                                m.w_edge3[0:n, t % GROUP, :], start=True, stop=True)
                    last.then_inc(part[j], 1)

                def collect(k, j):
                    pe.wait_ge(ready[j], k + 1)
                    pe.sem_inc(gate, 1)
                    for t in range(BATCH):
                        last = nc.tensor.matmul(sums[j][:, t // 2, 0:F], onehot[:, j, t, :], hidden[:, j, t, :],
                                                start=t % 2 == 0, stop=t % 2 == 1)
                    last.then_inc(summed[j], 1)
                edge_part(0, 0)
                with pe.Fori(0, ITERS - 1) as k:
                    for j in range(2):
                        edge_part(k + j, 1 - j)
                        collect(k, j)
                edge_part(ITERS - 1, 1)
                collect(ITERS - 1, 0)
                collect(ITERS - 1, 1)

            @block.scalar
            def _(act):
                indices = IndexStager(nc, act, m.index_src, index_now, slot_free, indexed, gate)
                indices.first()

                def turn_out(k, j):
                    act.wait_ge(turn[j], k + 2)
                    act.sem_inc(gate, 1)
                    whole, rest = len(GROUPS) - 1, len(GROUPS[-1]) * ROW
                    nc.scalar.copy(e_turned[:, j, 0:whole, :], e_ps[j][0:GROUP * ROW, 0:whole, :])
                    nc.scalar.copy(e_turned[0:rest, j, whole, :], e_ps[j][0:rest, whole, :]).then_inc(turned_s[j], 1)
                turn_out(0, 0)
                with act.Fori(0, ITERS - 1) as k:
                    for j in range(2):
                        turn_out(k + j, 1 - j)
                        indices.after(k, j)
                turn_out(ITERS - 1, 1)

            @block.vector
            def _(dve):
                o = Order(dve, order)
                o.then(nc.vector.memset(acc, 0.0))
                with dve.Fori(0, ITERS) as k:
                    s = Order(dve, order, 2 * (1 + PPB), k, o.n)
                    for j in range(2):
                        one_hots(nc, m, onehot, m.key_dst, k * 2 + j, j)
                        dve.wait_ge(part[j], k + 1)
                        dve.wait_ge(arrived[j], k * (16 * BATCH) + 16 * BATCH)
                        dve.sem_inc(gate, 1)
                        s.then(nc.vector.tensor_tensor(hidden[:, j, :, :], part_ps[j][:], rows[:, j, :, :], ALU.add))
                        dve.sem_inc(slot_free[j], 1)
                        nc.vector.tensor_scalar(hidden[:, j, :, :], hidden[:, j, :, :], 0.0, None, ALU.max).then_inc(ready[j], 1)
                        blocks = load_pair_blocks(nc, dve, m, k * 2 + j)
                        dve.wait_ge(summed[j], k + 1)
                        s.mark(add_to_nodes(nc, dve, s, m, acc, sums[j], blocks))
                    assert s.n == s.last



def build(nc, a, out):
    m = Net()
    top = ExitStack()
    with top:
        def sb(n, s, d=fp32, ctx=top):
            return ctx.enter_context(nc.sbuf_tensor(n, s, d))

        def dram(n, s, d=fp32):
            return nc.dram_tensor(n, s, d).ap()
        m.X, m.H = sb("X", [P, NB, F]), sb("H", [P, NB, F])
        m.acc = sb("acc", [P, NB, F + 1])
        m.out = sb("out", [P, NB, F])
        m.iota_p, m.ident, m.ones = sb("iota_p", [P, P]), sb("ident", [P, P]), sb("ones", [P, P])
        m.iota_col = sb("iota_col", [P, 1])
        m.iota_b, m.ident_b = sb("iota_b", [P, P], bf16), sb("ident_b", [P, P], bf16)
        m.before, m.valid = sb("before", [P, P]), sb("valid", [P, P])
        m.w_src, m.w_dst, m.w_edge = sb("w_src", [F, 2 * F]), sb("w_dst", [F + 1, 2 * F]), sb("w_edge", [P, GROUP, 2 * F])
        m.w_edge3, m.w_h3, m.w_out3 = sb("w_edge3", [P, GROUP, F]), sb("w_h3", [F + 1, F]), sb("w_out3", [F + 1, F])
        m.w_l, m.w_r = sb("w_l", [F, F]), sb("w_r", [F + 1, F])
        m.w_att1, m.w_att2, m.b_att = sb("w_att1", [F + 1, LAYERS, 2 * F]), sb("w_att2", [P, LAYERS, 2 * F]), sb("b_att", [P, LAYERS, F])
        m.att2, m.att2_b = sb("att2", [P, LAYERS, F]), sb("att2_b", [P, LAYERS])
        m.gain, m.shift = sb("gain", [P, 2 * F]), sb("shift", [P, 2 * F])
        m.g_bn, m.be_bn, m.gamma3, m.beta3 = (sb(n, [P, F]) for n in ("g_bn", "be_bn", "gamma3", "beta3"))
        m.index_src, m.index_dst = sb("index_src", [P, T + 2 * BATCH], i32), sb("index_dst", [P, T + 2 * BATCH], i32)
        m.key_dst, m.key_src = sb("key_dst", [P, TK]), sb("key_src", [P, TK])
        m.table_dst, m.table_src = sb("table_dst", [1, P * QR], i32), sb("table_src", [1, P * QR], i32)
        m.rows_dst, m.rows_src = dram("rows_dst", [P, TP, ROW]), dram("rows_src", [P, TP, 2])
        layer0 = ExitStack()
        kept = dram("kept", [P, T, 2 * F])
        fetched128 = dram("fetched128", [NPAD, 2 * F])

        m.packed_src = sb("packed_src", [P, EC, 3], fp32, layer0)
        with ExitStack() as sort:
            m.src, m.dst = sb("src", [P, EC], i32, sort), sb("dst", [P, EC], i32, sort)
            m.packed_dst = sb("packed_dst", [P, EC, 3], fp32, sort)
            m.sentinel_slot = sb("sentinel_slot", [P, EC], fp32, sort)
            m.numbers, m.pair_no = sb("numbers", [P, NB + 1], fp32, sort), sb("pair_no", [P, QR], fp32, sort)
            stage_constants(nc, m, a)
            stage_place(nc, m, a)
            stage_reorder_dst(nc, m, a)

        m.table = m.table_dst
        with ExitStack() as conv:
            part_dst = sb("part_dst", [P, NB, 2 * F], ctx=conv)
            keys = Keys(nc, "keys_dst", m.rows_dst, m.index_src, m.key_dst)
            keys.start()
            stage_norm(nc, m, "n0", m.X[:], m.H[:])
            with ExitStack() as pre:
                turned, part_src = sb("turned0", [F + 1, NPAD], ctx=pre), sb("part_src", [P, NB, 2 * F], ctx=pre)
                stage_turn(nc, m, "t0", m.H[:], turned)
                stage_product(nc, m, "p0", [(turned, m.w_dst[:])], part_dst[:], 2 * F)
                stage_product(nc, m, "p1", [(turned, m.w_src[:])], part_src[:], 2 * F, table=fetched128)
            keys.finish()
            sum_acc, square_acc = sb("sum_acc", [P, BATCH, 2 * F], ctx=conv), sb("square_acc", [P, BATCH, 2 * F], ctx=conv)
            scale, shift = sb("bn_scale", [P, 2 * F], ctx=conv), sb("bn_shift", [P, 2 * F], ctx=conv)
            stage_conv_sums(nc, m, part_dst, fetched128, kept, sum_acc, square_acc)
            stage_gate_norm(nc, m, sum_acc, square_acc, scale, shift)
            stage_conv_messages(nc, m, kept, scale, shift)
        layer0.close()
        keys = Keys(nc, "keys_src", m.rows_src, m.index_dst, m.key_src)
        keys.start()
        stage_conv_out(nc, m)
        keys.finish()

        inverse = sb("inverse", [P, NB])
        count = sb("count", [P, NB])
        table1 = dram("table1", [NPAD, F])
        stage_norm(nc, m, "n1", m.X[:], m.H[:], table=table1)

        def counts(o):
            o.then(nc.vector.tensor_copy(count[:], m.acc[:, :, F]))
            o.then(nc.vector.tensor_scalar(inverse[:], count[:], 1.0, None, ALU.max))
            o.then(nc.vector.reciprocal(inverse[:], inverse[:]))
        stage_vector(nc, "counts", counts)
        stage_gather_sum(nc, m, "sage", m.index_src, m.key_dst, table1, m.out[:])

        def mean(o):
            o.then(nc.vector.tensor_tensor(m.out[:], m.out[:], b3(inverse[:], F), ALU.mult))
        stage_vector(nc, "mean", mean)
        with ExitStack() as sage:
            turned_h, turned_m = sb("turned_h", [F + 1, NPAD], ctx=sage), sb("turned_m", [F + 1, NPAD], ctx=sage)
            stage_turn(nc, m, "t1", m.H[:], turned_h)
            stage_turn(nc, m, "t2", m.out[:], turned_m)
            stage_product(nc, m, "p2", [(turned_m, m.w_l[:]), (turned_h, m.w_r[:])], m.X[:], F, plus=m.X[:])

        m.table = m.table_src
        stage_norm(nc, m, "n2", m.X[:], m.H[:])
        with ExitStack() as hops:
            mask, rowsum = sb("mask", [P, T], ctx=hops), sb("rowsum", [P, NB, 3], ctx=hops)
            inv_root, inv3 = sb("inv_root", [P, NB], ctx=hops), sb("inv3", [P, 3, NB], bf16, hops)
            hi = sb("dst_block", [P, T], ctx=hops)
            lo_rows, x_dst = dram("lo_rows", [1, T * P], bf16), dram("x_dst", [P, T, F])
            row_part3 = sb("row_part3", [P, NB, 3, F], bf16, hops)

            def start(o):
                o.then(nc.vector.tensor_copy(m.out[:], m.H[:]))
            stage_vector(nc, "hops", start)
            stage_halves(nc, m, lo_rows, hi)
            for l in range(LAYERS):
                cols = dram(f"cols{l}", [NPAD, 2 * F])
                with ExitStack() as pre:
                    turned, col_part = sb(f"turned_l{l}", [F + 1, NPAD], ctx=pre), sb(f"col_part{l}", [P, NB, F], ctx=pre)
                    stage_turn(nc, m, f"tl{l}", m.H[:], turned)
                    stage_attention(nc, m, l, turned, row_part3, col_part, cols)
                stage_masks(nc, m, l, row_part3, cols, x_dst, mask, rowsum[:])
                stage_degree(nc, m, l, rowsum, inv_root, inv3)
                stage_hop(nc, m, f"hop{l}", x_dst, lo_rows, hi, inv3, mask, m.H[:])

                def after(o):
                    o.then(nc.vector.tensor_tensor(m.H[:], m.H[:], b3(inv_root[:], F), ALU.mult))
                    o.then(nc.vector.tensor_tensor(m.out[:], m.out[:], m.H[:], ALU.add))
                stage_vector(nc, f"after{l}", after)

        def hops_out(o):
            o.then(nc.vector.tensor_tensor(m.X[:], m.X[:], m.out[:], ALU.add))
        stage_vector(nc, "hops_out", hops_out)

        m.table = m.table_dst
        stage_norm(nc, m, "n3", m.X[:], m.H[:])
        table3 = dram("table3", [NPAD, F])
        with ExitStack() as mlp:
            turned = sb("turned3", [F + 1, NPAD], ctx=mlp)
            stage_turn(nc, m, "t3", m.H[:], turned)
            stage_product(nc, m, "p3", [(turned, m.w_h3[:])], m.out[:], F, table=table3)
        stage_edge_mlp(nc, m, table3, m.acc[:, :, 0:F])

        with ExitStack() as mlp:
            turned = sb("turned4", [F + 1, NPAD], ctx=mlp)
            stage_turn(nc, m, "t4", m.acc[:], turned, F + 1)
            stage_product(nc, m, "p4", [(turned, m.w_out3[:])], m.out[:], F)
        stage_last_norm(nc, m, inverse, out)


def stage_degree(nc, m, l, rowsum, inv_root, inv3):
    ctx, (order, rooted, ready) = stage(nc, [f"deg{l}_{s}" for s in ("order", "rooted", "ready")])
    with ctx:
        rest = ctx.enter_context(nc.sbuf_tensor(f"deg{l}_rest", [P, NB], fp32))
        with nc.Block() as block:
            @block.vector
            def _(dve):
                o = Order(dve, order)
                o.then(nc.vector.tensor_reduce(inv_root[:], rowsum[:], AX.X, ALU.add))
                nc.vector.tensor_scalar(inv_root[:], inv_root[:], 1e-6, None, ALU.add).then_inc(ready, 1)
                dve.wait_ge(rooted, 1)
                o.then(nc.vector.reciprocal(inv_root[:], inv_root[:]))
                o.then(nc.vector.tensor_scalar(inv_root[:], inv_root[:], 0.0, 10.0, ALU.max, ALU.min))
                o.then(nc.vector.tensor_copy(rest[:], inv_root[:]))
                split3(nc, o, rest[:], [inv3[:, i, :] for i in range(3)])

            @block.scalar
            def _(act):
                act.wait_ge(ready, 1)
                nc.scalar.activation(inv_root[:], inv_root[:], ACT.Sqrt).then_inc(rooted, 1)


def stage_last_norm(nc, m, inverse, out):
    ctx, (order, var_sem, std_sem, ready, stored) = stage(nc, ["ln_" + s for s in ("order", "var", "std", "ready", "stored")])
    with ctx:
        stat = ctx.enter_context(nc.sbuf_tensor("ln_stat", [P, 2, NB], fp32))
        square = ctx.enter_context(nc.sbuf_tensor("ln_sq", [P, NB, F], fp32))
        with nc.Block() as block:
            @block.vector
            def _(dve):
                o = Order(dve, order)
                o.then(nc.vector.tensor_tensor(m.out[:], m.out[:], b3(inverse[:], F), ALU.mult))
                o.then(nc.vector.tensor_tensor(m.out[:], m.out[:], m.H[:], ALU.add))
                normalize(nc, dve, o, m.out[:], (m.H[:], square[:]), stat, std_sem, var_sem)
                o.then(nc.vector.tensor_tensor(m.H[:], m.H[:], b2(m.gamma3[:], NB), ALU.mult))
                o.then(nc.vector.tensor_tensor(m.H[:], m.H[:], b2(m.beta3[:], NB), ALU.add))
                nc.vector.tensor_tensor(m.H[:], m.H[:], m.X[:], ALU.add).then_inc(ready, 1)

            @block.scalar
            def _(act):
                root(nc, act, stat, var_sem, std_sem)

            @block.sync
            def _(sp):
                sp.wait_ge(ready, 1)
                full = NB - 1
                sp.dma_start(out[0:full * P, :].rearrange("(b p) f -> p b f", p=P), m.H[:, 0:full, :]).then_inc(stored, 16)
                sp.dma_start(out[full * P:N, :], m.H[0:N - full * P, full, :]).then_inc(stored, 16)
                sp.wait_ge(stored, 32)


NAMES = {"x": "x", "L0_gnn_W_int": "W_int", "L0_gnn_b_int": "b_int", "L0_gnn_g_int": "g_int", "L0_gnn_be_int": "be_int",
         "L0_gnn_W_upd": "W_upd", "L0_gnn_b_upd": "b_upd", "L0_gnn_g_upd": "g_upd", "L0_gnn_be_upd": "be_upd",
         "L0_gnn_g_bn": "g_bn", "L0_gnn_be_bn": "be_bn", "L1_gnn_w_l": "w_l", "L1_gnn_w_r": "w_r", "L1_gnn_b": "b_l1",
         "L2_gnn_nb_W": "nb_W", "L2_gnn_nb_b": "nb_b", "L2_gnn_self_W": "self_W", "L2_gnn_self_b": "self_b",
         "L2_gnn_att1_W": "att1_W", "L2_gnn_att1_b": "att1_b", "L2_gnn_att2_W": "att2_W", "L2_gnn_att2_b": "att2_b",
         "L3_gnn_W1": "W1", "L3_gnn_b1": "b1", "L3_gnn_W2": "W2", "L3_gnn_b2": "b2", "L3_gnn_gamma": "gamma",
         "L3_gnn_beta": "beta"}


def kernel(**inputs):
    from concourse import bacc
    from concourse.bass_utils import run_bass_kernel_spmd

    nc = bacc.Bacc("TRN2", target_bir_lowering=False, num_devices=1)
    arrays = {short: np.ascontiguousarray(inputs[name]) for name, short in NAMES.items()}
    for name in ("src", "dst"):
        arrays[name] = np.pad(np.asarray(inputs[name]), (0, P * EC - E), constant_values=SENTINEL).reshape(P, EC)
    arrays["e"] = np.pad(np.asarray(inputs["edge_attr_32"]), ((0, P * EC - E), (0, 0)))
    args = {n: nc.dram_tensor(f"in_{n}", v.shape, mybir.dt.from_np(v.dtype), kind="ExternalInput").ap()
            for n, v in arrays.items()}
    out = nc.dram_tensor("out_dram", [N, F], fp32, kind="ExternalOutput").ap()
    build(nc, args, out)
    r = run_bass_kernel_spmd(nc, [{f"in_{n}": v for n, v in arrays.items()}], core_ids=[0])
    return r.results[0]["out_dram"]
```
